# Optimizing a Trainium2 kernel written in Bass

```python
import numpy as np
import jax
import jax.numpy as jnp

def _softmax(x, axis=-1):
    return jax.nn.softmax(x, axis=axis)

def _gelu(x):
    return jax.nn.gelu(x, approximate=True)

def _silu(x):
    return jax.nn.silu(x)

def _sigmoid(x):
    return jax.nn.sigmoid(x)

def _layernorm(x, axis=-1, eps=1e-05):
    m = jnp.mean(x, axis=axis, keepdims=True)
    v = jnp.var(x, axis=axis, keepdims=True)
    return (x - m) / jnp.sqrt(v + eps)

def _scatter_add(tgt, idx, src, axis=0):
    return tgt.at[idx].add(src)

def _segment_sum(src, seg, n):
    return jax.ops.segment_sum(src, seg, n)
kernel_name = 'mk_macaron_d2_jaxref_r8_7968db'

def setup_inputs(seed: int=0):
    np.random.seed(seed)
    _w = jnp.asarray

    def _L0_attn_setup():
        import jax, jax.numpy as jnp
        import numpy as np
        HIDDEN_DIM = 128
        NUM_HEADS = 16
        HEAD_DIM = HIDDEN_DIM // NUM_HEADS
        SCALAR_NORM = float(np.sqrt(HIDDEN_DIM / NUM_HEADS))
        key = jax.random.key(seed)
        k1, k2 = jax.random.split(key)
        B, N, D = (2, 256, HIDDEN_DIM)
        x = jax.random.normal(k1, (B, N, D), dtype=jnp.float32)
        limit = float(np.sqrt(6.0 / (D + 3 * D)))
        W_qkv = jax.random.uniform(k2, (3 * D, D), dtype=jnp.float32, minval=-limit, maxval=limit)
        return {'x': x, 'W_qkv': W_qkv}
    _L0_attn_in = _L0_attn_setup()

    def _L0_ffn_setup():
        import jax, jax.numpy as jnp
        import numpy as np
        DIM = 128
        NUM_EXPERTS = 8
        HIDDEN = 512
        CAP_FACTOR = 2.0
        B, S = (4, 256)
        key = jax.random.key(seed)
        ks = jax.random.split(key, 6)
        scale_r = 1.0 / np.sqrt(DIM)
        scale_1 = 1.0 / np.sqrt(DIM)
        scale_2 = 1.0 / np.sqrt(HIDDEN)
        return {'x': jax.random.normal(ks[0], (B, S, DIM), dtype=jnp.float32), 'router_w': jax.random.uniform(ks[1], (NUM_EXPERTS, DIM), jnp.float32, -scale_r, scale_r), 'w1': jax.random.uniform(ks[2], (NUM_EXPERTS, DIM, HIDDEN), jnp.float32, -scale_1, scale_1), 'b1': jax.random.uniform(ks[3], (NUM_EXPERTS, HIDDEN), jnp.float32, -scale_1, scale_1), 'w2': jax.random.uniform(ks[4], (NUM_EXPERTS, HIDDEN, DIM), jnp.float32, -scale_2, scale_2), 'b2': jax.random.uniform(ks[5], (NUM_EXPERTS, DIM), jnp.float32, -scale_2, scale_2)}
    _L0_ffn_in = _L0_ffn_setup()

    def _L1_attn_setup():
        import jax, jax.numpy as jnp
        import numpy as np
        D_MODEL = 128
        H = 16
        LN_EPS = 1e-05

        def _layernorm(x, g, b):
            mu = jnp.mean(x, axis=-1, keepdims=True)
            var = jnp.mean(jnp.square(x - mu), axis=-1, keepdims=True)
            return (x - mu) * jax.lax.rsqrt(var + LN_EPS) * g + b

        def _attention(tokens, Wq, bq, Wk, bk, Wv, bv, Wo, bo, dist_scale):
            B, T, D = tokens.shape
            dh = D // H
            q = (tokens @ Wq + bq).reshape(B, T, H, dh)
            k = (tokens @ Wk + bk).reshape(B, T, H, dh)
            v = (tokens @ Wv + bv).reshape(B, T, H, dh)
            S = jnp.einsum('bthd,buhd->btuh', q, k)
            pos = jnp.arange(T)
            dist = jnp.abs(pos[None, :] - pos[:, None]).astype(S.dtype)
            S = S - dist_scale * dist[None, :, :, None]
            mask_uh = jnp.triu(jnp.ones((T, H), bool), k=1)
            S = jnp.where(mask_uh[None, None, :, :], -jnp.inf, S)
            S = S / jnp.sqrt(jnp.asarray(dh, S.dtype))
            P = jax.nn.softmax(S, axis=2)
            A = jnp.einsum('btuh,buhd->bthd', P, v).reshape(B, T, D)
            return A @ Wo + bo
        key = jax.random.key(seed)
        ks = jax.random.split(key, 16)
        B, T, D = (2, 256, D_MODEL)
        d_ff = 4 * D
        s = 1.0 / np.sqrt(D)
        sf = 1.0 / np.sqrt(d_ff)
        return {'tokens': jax.random.normal(ks[0], (B, T, D), jnp.float32), 'Wq': jax.random.normal(ks[1], (D, D), jnp.float32) * s, 'bq': jnp.zeros((D,), jnp.float32), 'Wk': jax.random.normal(ks[2], (D, D), jnp.float32) * s, 'bk': jnp.zeros((D,), jnp.float32), 'Wv': jax.random.normal(ks[3], (D, D), jnp.float32) * s, 'bv': jnp.zeros((D,), jnp.float32), 'Wo': jax.random.normal(ks[4], (D, D), jnp.float32) * s, 'bo': jnp.zeros((D,), jnp.float32), 'dist_scale': jnp.asarray(0.01, jnp.float32), 'W1': jax.random.normal(ks[5], (D, d_ff), jnp.float32) * s, 'b1': jnp.zeros((d_ff,), jnp.float32), 'W2': jax.random.normal(ks[6], (d_ff, D), jnp.float32) * sf, 'b2': jnp.zeros((D,), jnp.float32), 'ln1_g': jnp.ones((D,), jnp.float32), 'ln1_b': jnp.zeros((D,), jnp.float32), 'ln2_g': jnp.ones((D,), jnp.float32), 'ln2_b': jnp.zeros((D,), jnp.float32)}
    _L1_attn_in = _L1_attn_setup()

    def _L1_ffn_setup():
        import jax, jax.numpy as jnp
        import numpy as np
        H, F, E_SHARED, E_ROUTED, K = (128, 512, 1, 8, 2)

        def _expert(x, w_up, w_down):
            h = jax.nn.gelu(jnp.einsum('bsh,hf->bsf', x, w_up), approximate=False)
            return jnp.einsum('bsf,fh->bsh', h, w_down)
        key = jax.random.key(seed)
        ks = jax.random.split(key, 6)
        x = jax.random.normal(ks[0], (4, 256, H), dtype=jnp.float32)
        s = 0.02
        shared_up = jax.random.normal(ks[1], (E_SHARED, H, F), dtype=jnp.float32) * s
        shared_down = jax.random.normal(ks[2], (E_SHARED, F, H), dtype=jnp.float32) * s
        routed_up = jax.random.normal(ks[3], (E_ROUTED, H, F), dtype=jnp.float32) * s
        routed_down = jax.random.normal(ks[4], (E_ROUTED, F, H), dtype=jnp.float32) * s
        router_w = jax.random.normal(ks[5], (H, E_ROUTED), dtype=jnp.float32) * s
        return {'x': x, 'shared_up': shared_up, 'shared_down': shared_down, 'routed_up': routed_up, 'routed_down': routed_down, 'router_w': router_w}
    _L1_ffn_in = _L1_ffn_setup()
    _d = {'L0_attn_x': _L0_attn_in['x'], 'L0_attn_W_qkv': _L0_attn_in['W_qkv'], 'L0_ffn_router_w': _L0_ffn_in['router_w'], 'L0_ffn_w1': _L0_ffn_in['w1'], 'L0_ffn_b1': _L0_ffn_in['b1'], 'L0_ffn_w2': _L0_ffn_in['w2'], 'L0_ffn_b2': _L0_ffn_in['b2'], 'L1_attn_Wq': _L1_attn_in['Wq'], 'L1_attn_bq': _L1_attn_in['bq'], 'L1_attn_Wk': _L1_attn_in['Wk'], 'L1_attn_bk': _L1_attn_in['bk'], 'L1_attn_Wv': _L1_attn_in['Wv'], 'L1_attn_bv': _L1_attn_in['bv'], 'L1_attn_Wo': _L1_attn_in['Wo'], 'L1_attn_bo': _L1_attn_in['bo'], 'L1_attn_dist_scale': _L1_attn_in['dist_scale'], 'L1_attn_W1': _L1_attn_in['W1'], 'L1_attn_b1': _L1_attn_in['b1'], 'L1_attn_W2': _L1_attn_in['W2'], 'L1_attn_b2': _L1_attn_in['b2'], 'L1_attn_ln1_g': _L1_attn_in['ln1_g'], 'L1_attn_ln1_b': _L1_attn_in['ln1_b'], 'L1_attn_ln2_g': _L1_attn_in['ln2_g'], 'L1_attn_ln2_b': _L1_attn_in['ln2_b'], 'L1_ffn_shared_up': _L1_ffn_in['shared_up'], 'L1_ffn_shared_down': _L1_ffn_in['shared_down'], 'L1_ffn_routed_up': _L1_ffn_in['routed_up'], 'L1_ffn_routed_down': _L1_ffn_in['routed_down'], 'L1_ffn_router_w': _L1_ffn_in['router_w']}
    _x0 = _d['L0_attn_x']
    _d['L0_attn_x'] = jax.random.normal(jax.random.fold_in(jax.random.key(seed), 1), (32, 256, 128), dtype=_x0.dtype)
    del _x0
    return _d

def reference(L0_attn_x, L0_attn_W_qkv, L0_ffn_router_w, L0_ffn_w1, L0_ffn_b1, L0_ffn_w2, L0_ffn_b2, L1_attn_Wq, L1_attn_bq, L1_attn_Wk, L1_attn_bk, L1_attn_Wv, L1_attn_bv, L1_attn_Wo, L1_attn_bo, L1_attn_dist_scale, L1_attn_W1, L1_attn_b1, L1_attn_W2, L1_attn_b2, L1_attn_ln1_g, L1_attn_ln1_b, L1_attn_ln2_g, L1_attn_ln2_b, L1_ffn_shared_up, L1_ffn_shared_down, L1_ffn_routed_up, L1_ffn_routed_down, L1_ffn_router_w):

    def _L0_attn_ref(x, W_qkv):
        import jax, jax.numpy as jnp
        import numpy as np
        HIDDEN_DIM = 128
        NUM_HEADS = 16
        HEAD_DIM = HIDDEN_DIM // NUM_HEADS
        SCALAR_NORM = float(np.sqrt(HIDDEN_DIM / NUM_HEADS))
        b, n, d = x.shape
        h, hd = (NUM_HEADS, HEAD_DIM)
        qkv = x @ W_qkv.T
        q, k, v = jnp.split(qkv, 3, axis=-1)
        q = q.reshape(b, n, h, hd).transpose(0, 2, 1, 3)
        k = k.reshape(b, n, h, hd).transpose(0, 2, 1, 3)
        v = v.reshape(b, n, h, hd).transpose(0, 2, 1, 3)
        scores = jnp.einsum('bhik,bhjk->bhij', q, k) / SCALAR_NORM
        attn = jax.nn.softmax(scores, axis=-1)
        out = jnp.einsum('bhij,bhjk->bhik', attn, v)
        return out.transpose(0, 2, 1, 3).reshape(b, n, d)

    def _L0_ffn_ref(x, router_w, w1, b1, w2, b2):
        import jax, jax.numpy as jnp
        import numpy as np
        DIM = 128
        NUM_EXPERTS = 8
        HIDDEN = 512
        CAP_FACTOR = 2.0
        B, S = (4, 256)
        Bz, Sz, Dz = x.shape
        E = router_w.shape[0]
        capacity = max(1, int(Sz * CAP_FACTOR / E) + 1)
        scores = jax.nn.softmax(jnp.einsum('bsd,ed->bse', x, router_w), axis=-1)
        scores_t = jnp.swapaxes(scores, 1, 2)
        gate_vals, sel_idx = jax.lax.top_k(scores_t, capacity)
        b_idx = jnp.arange(Bz)[:, None, None]
        tokens = x[b_idx, sel_idx]
        h = jnp.einsum('becd,edh->bech', tokens, w1) + b1[None, :, None, :]
        h = jax.nn.gelu(h, approximate=False)
        y = jnp.einsum('bech,ehd->becd', h, w2) + b2[None, :, None, :]
        gated = y * gate_vals[..., None]
        out = jnp.zeros_like(x).at[b_idx, sel_idx].add(gated)
        return out

    def _L1_attn_ref(tokens, Wq, bq, Wk, bk, Wv, bv, Wo, bo, dist_scale, W1, b1, W2, b2, ln1_g, ln1_b, ln2_g, ln2_b):
        import jax, jax.numpy as jnp
        import numpy as np
        D_MODEL = 128
        H = 16
        LN_EPS = 1e-05

        def _layernorm(x, g, b):
            mu = jnp.mean(x, axis=-1, keepdims=True)
            var = jnp.mean(jnp.square(x - mu), axis=-1, keepdims=True)
            return (x - mu) * jax.lax.rsqrt(var + LN_EPS) * g + b

        def _attention(tokens, Wq, bq, Wk, bk, Wv, bv, Wo, bo, dist_scale):
            B, T, D = tokens.shape
            dh = D // H
            q = (tokens @ Wq + bq).reshape(B, T, H, dh)
            k = (tokens @ Wk + bk).reshape(B, T, H, dh)
            v = (tokens @ Wv + bv).reshape(B, T, H, dh)
            S = jnp.einsum('bthd,buhd->btuh', q, k)
            pos = jnp.arange(T)
            dist = jnp.abs(pos[None, :] - pos[:, None]).astype(S.dtype)
            S = S - dist_scale * dist[None, :, :, None]
            mask_uh = jnp.triu(jnp.ones((T, H), bool), k=1)
            S = jnp.where(mask_uh[None, None, :, :], -jnp.inf, S)
            S = S / jnp.sqrt(jnp.asarray(dh, S.dtype))
            P = jax.nn.softmax(S, axis=2)
            A = jnp.einsum('btuh,buhd->bthd', P, v).reshape(B, T, D)
            return A @ Wo + bo
        x_attn = _attention(tokens, Wq, bq, Wk, bk, Wv, bv, Wo, bo, dist_scale)
        x = _layernorm(tokens + x_attn, ln1_g, ln1_b)
        y = jax.nn.relu(x @ W1 + b1) @ W2 + b2
        z = _layernorm(y + x, ln2_g, ln2_b)
        return z

    def _L1_ffn_ref(x, shared_up, shared_down, routed_up, routed_down, router_w):
        import jax, jax.numpy as jnp
        import numpy as np
        H, F, E_SHARED, E_ROUTED, K = (128, 512, 1, 8, 2)

        def _expert(x, w_up, w_down):
            h = jax.nn.gelu(jnp.einsum('bsh,hf->bsf', x, w_up), approximate=False)
            return jnp.einsum('bsf,fh->bsh', h, w_down)
        shared_out = jnp.zeros_like(x)
        for i in range(E_SHARED):
            shared_out = shared_out + _expert(x, shared_up[i], shared_down[i])
        probs = jax.nn.softmax(jnp.einsum('bsh,he->bse', x, router_w), axis=-1)
        top_k_prob, top_k_idx = jax.lax.top_k(probs, K)
        onehot = jax.nn.one_hot(top_k_idx, E_ROUTED, dtype=x.dtype)
        gates = jnp.einsum('bsk,bske->bse', top_k_prob, onehot)
        routed_out = jnp.zeros_like(x)
        for e in range(E_ROUTED):
            y = _expert(x, routed_up[e], routed_down[e])
            routed_out = routed_out + gates[..., e:e + 1] * y
        return shared_out + routed_out + x
    x = L0_attn_x
    x = x + 0.5 * _L0_ffn_ref(_layernorm(x, axis=-1), L0_ffn_router_w, L0_ffn_w1, L0_ffn_b1, L0_ffn_w2, L0_ffn_b2)
    x = x + _L0_attn_ref(_layernorm(x, axis=-1), L0_attn_W_qkv)
    x = x + 0.5 * _L0_ffn_ref(_layernorm(x, axis=-1), L0_ffn_router_w, L0_ffn_w1, L0_ffn_b1, L0_ffn_w2, L0_ffn_b2)
    x = x + 0.5 * _L1_ffn_ref(_layernorm(x, axis=-1), L1_ffn_shared_up, L1_ffn_shared_down, L1_ffn_routed_up, L1_ffn_routed_down, L1_ffn_router_w)
    x = x + _L1_attn_ref(_layernorm(x, axis=-1), L1_attn_Wq, L1_attn_bq, L1_attn_Wk, L1_attn_bk, L1_attn_Wv, L1_attn_bv, L1_attn_Wo, L1_attn_bo, L1_attn_dist_scale, L1_attn_W1, L1_attn_b1, L1_attn_W2, L1_attn_b2, L1_attn_ln1_g, L1_attn_ln1_b, L1_attn_ln2_g, L1_attn_ln2_b)
    x = x + 0.5 * _L1_ffn_ref(_layernorm(x, axis=-1), L1_ffn_shared_up, L1_ffn_shared_down, L1_ffn_routed_up, L1_ffn_routed_down, L1_ffn_router_w)
    return x

_drawn_inputs = setup_inputs


def setup_inputs(seed=0):
    import zlib

    import numpy as np

    out = dict(_drawn_inputs(seed))
    spreads = {'L1_attn_bq': (0.0, 0.8),
     'L1_attn_bk': (0.0, 0.8),
     'L1_attn_bv': (0.0, 0.1),
     'L1_attn_bo': (0.0, 0.1),
     'L1_attn_b1': (0.0, 0.304),
     'L1_attn_b2': (0.0, 0.1),
     'L1_attn_ln1_g': (1.0, 0.2),
     'L1_attn_ln1_b': (0.0, 0.1),
     'L1_attn_ln2_g': (1.0, 0.2),
     'L1_attn_ln2_b': (0.0, 0.1)}
    factors = {'L0_ffn_b1': 8.0,
     'L0_ffn_b2': 6.568,
     'L1_ffn_routed_up': 8.0,
     'L1_ffn_routed_down': 8.0,
     'L1_ffn_router_w': 8.0}
    for name, (base, spread) in spreads.items():
        noise = np.random.default_rng([zlib.crc32(name.encode()), seed]).standard_normal(out[name].shape)
        drawn = base * np.exp(spread * noise) if base else spread * noise
        out[name] = jnp.asarray(drawn.astype(out[name].dtype))
    for name, factor in factors.items():
        out[name] = (out[name] * factor).astype(out[name].dtype)
    return out
```

```python
from contextlib import ExitStack

import numpy as np

import concourse.bass as bass
from concourse import mybir

F32 = mybir.dt.float32
F32R = mybir.dt.float32r
ALU = mybir.AluOpType
ACT = mybir.ActivationFunctionType
AX = mybir.AxisListType

P = 128
BATCH, SEQ, D = 32, 256, 128
CH = SEQ // P
TILES = BATCH * CH
UT = 4
UNITS = TILES // UT
UW = UT * P
E = 8
F = 512
FC = F // P
CAP = SEQ * 2 // E + 1
HEADS, HD = 16, D // 16
G, HG = 4, 4
HW = P // HG
ROW_M, ROW_MASK = 3 * HD, 3 * HD + 2
EPS = 1e-5
SM_SCALE = float(1.0 / np.sqrt(HD))
MASKED = -1e30


def shape_constants():
    ident = np.eye(P, dtype=np.float32)
    cols = np.zeros((P, 16), np.float32)
    r = np.arange(P) % HW
    term = r // HD
    cols[:, 0] = np.where(r >= ROW_M, 1, term == 2)
    cols[:, 1] = np.where(r >= ROW_M, 0, np.where(term == 2, -1, 1))
    cols[:, 2] = np.where(r >= ROW_M, 1, term == 1)
    cols[:, 3] = np.where(r >= ROW_M, 0, np.where(term == 1, -1, 1))
    prio = np.broadcast_to(np.arange(E, 0, -1, dtype=np.float32), (P, E))
    t = np.arange(SEQ)
    dist = np.abs(t[:, None] - t[None, :]).astype(np.float32)
    dist = dist.reshape(CH, P, SEQ).transpose(1, 0, 2).reshape(P, CH * SEQ)
    aug = np.zeros((2, 1 + HEADS, HEADS, HW), np.float32)
    aug[0, 0, :, ROW_MASK] = 1
    aug[1, 0, :, ROW_M:ROW_M + 2] = 1
    for h in range(HEADS):
        aug[1, 1 + h, h, ROW_MASK] = 1
    aug = aug.transpose(1, 0, 2, 3).reshape(1 + HEADS, 2 * HEADS * HW)
    rows = np.zeros((2, 1 + HEADS, SEQ), np.float32)
    rows[:, 0] = 1
    for h in range(HEADS):
        rows[1, 1 + h, :h] = MASKED
    rows = rows.transpose(1, 0, 2).reshape(1 + HEADS, 2 * SEQ)
    return {
        "c_ident": ident, "c_cols": cols, "c_prio": np.ascontiguousarray(prio), "c_dist": np.ascontiguousarray(dist),
        "c_aug": np.ascontiguousarray(aug), "c_rows": np.ascontiguousarray(rows),
    }


class Chain:

    def __init__(self, eng, sem):
        self.eng, self.sem, self.n = eng, sem, 0

    def __call__(self, ins):
        self.n += 1
        ins.then_inc(self.sem, 1)
        self.eng.wait_ge(self.sem, self.n)


def prime(eng, *sems):
    for s in sems:
        eng.sem_inc(s, 1)


def before(n):
    return n + 1


def after(n):
    return n + 2


def bcast(ap, n):
    return ap.unsqueeze(2).to_broadcast([ap.shape[0], ap.shape[1], n])


class Names:

    def __init__(self, nc, ctx, tag):
        self.nc, self.ctx, self.tag, self.sems = nc, ctx, tag, []
        ctx.callback(self.close)

    def sb(self, name, shape, dt=F32):
        return self.ctx.enter_context(self.nc.sbuf_tensor(f"{self.tag}_{name}", shape, dt))

    def ps(self, name, shape, dt=F32):
        return self.ctx.enter_context(self.nc.psum_tensor(f"{self.tag}_{name}", shape, dt))

    def sem(self, name):
        self.sems.append(self.nc.alloc_semaphore(f"{self.tag}_{name}"))
        return self.sems[-1]

    def close(self):
        if self.sems:
            self.nc.clear_and_free_semaphores(self.sems)
            self.nc.all_engine_barrier(sem_only=True)


def layernorm_stats(nc, tag, x, mean, rstd, neg_half):
    with ExitStack() as ctx:
        n = Names(nc, ctx, tag)
        st = n.sb("st", [P, TILES, 6])
        tmp = n.sb("tmp", [P, 2, TILES])
        s_st, s_v, s_p = n.sem("stats"), n.sem("var_ready"), n.sem("pow")
        block = ctx.enter_context(nc.Block())

        @block.vector
        def _(dve):
            chain = Chain(dve, s_v)
            with dve.Fori(0, TILES // 4) as i:
                for k in range(4):
                    dve.bn_stats(st[:, bass.ds(i * 4 + k, 1), :], x[:, bass.ds(i * 4 + k, 1), :]).then_inc(s_st, 1)
            dve.wait_ge(s_st, TILES)
            chain(dve.tensor_tensor(mean[:, :], st[:, :, 1], st[:, :, 4], ALU.add))
            chain(dve.tensor_scalar(mean[:, :], mean[:, :], 0.5, None, ALU.mult))
            chain(dve.tensor_tensor(tmp[:, 0, :], st[:, :, 1], st[:, :, 4], ALU.subtract))
            chain(dve.tensor_tensor(tmp[:, 1, :], st[:, :, 2], st[:, :, 5], ALU.add))
            chain(dve.tensor_tensor(tmp[:, 0, :], tmp[:, 0, :], tmp[:, 0, :], ALU.mult))
            chain(dve.tensor_scalar(tmp[:, 0, :], tmp[:, 0, :], 0.25, EPS, ALU.mult, ALU.add))
            chain(dve.scalar_tensor_tensor(tmp[:, 1, :], tmp[:, 1, :], 1.0 / D, tmp[:, 0, :], ALU.mult, ALU.add))

        @block.gpsimd
        def _(pool):
            pool.wait_ge(s_v, 7)
            pool.tensor_tensor(rstd[:, :], tmp[:, 1, :], neg_half[:, 0:TILES], ALU.pow).then_inc(s_p, 1)


def normalise_and_route(nc, tag, T, router_w, xn_residual):
    x, mean, rstd, ident = T["x"], T["mean"], T["rstd"], T["ident"]
    with ExitStack() as ctx:
        n = Names(nc, ctx, tag)
        xn = n.sb("xn", [P, 2, UT, D])
        xT = n.sb("xT", [P, 2, UW])
        ps_t = n.ps("ps_t", [P, 2, UW])
        ps_l = n.ps("ps_l", [P, 2, 512])
        s_xn = [n.sem(f"xn_ready{b}") for b in range(2)]
        s_res = n.sem("residual_added")
        s_tp = [n.sem(f"transposed{b}") for b in range(2)]
        s_xT = [n.sem(f"xT_ready{b}") for b in range(2)]
        s_all = [n.sem(f"xT_stored{b}") for b in range(2)]
        s_lg = [n.sem(f"logits_ready{b}") for b in range(2)]
        s_ls = [n.sem(f"logits_stored{b}") for b in range(2)]
        block = ctx.enter_context(nc.Block())

        @block.vector
        def _(dve):
            prime(dve, *s_xn)
            with dve.Fori(0, UNITS // 2) as i:
                for b in range(2):
                    dve.wait_ge(s_tp[b], before(i))
                    for k in range(UT):
                        t = (i * 2 + b) * UT + k
                        ins = dve.tensor_scalar(xn[:, b, k, :], x[:, bass.ds(t, 1), :], mean[:, bass.ds(t, 1)],
                                                rstd[:, bass.ds(t, 1)], ALU.subtract, ALU.mult)
                    ins.then_inc(s_xn[b], 1)
                    if xn_residual:
                        dve.wait_ge(s_xn[b], after(i))
                        xs = x[:, bass.ds((i * 2 + b) * UT, UT), :]
                        dve.scalar_tensor_tensor(xs, xn[:, b, :, :], 0.5, xs, ALU.mult, ALU.add).then_inc(s_res, 1)
                        dve.wait_ge(s_res, i * 2 + b + 1)

        @block.tensor
        def _(pe):
            prime(pe, *s_tp, *s_lg)
            with pe.Fori(0, UNITS // 2) as i:
                for b in range(2):
                    pe.wait_ge(s_xn[b], after(i))
                    pe.wait_ge(s_all[b], before(i))
                    for k in range(UT):
                        ins = pe.transpose(ps_t[:, b, k * P:(k + 1) * P], xn[:, b, k, :], ident[:, :])
                    ins.then_inc(s_tp[b], 1)
                for b in range(2):
                    pe.wait_ge(s_xT[b], after(i))
                    pe.wait_ge(s_ls[b], before(i))
                    for k in range(UT):
                        ins = pe.matmul(ps_l[:, b, k * E:(k + 1) * E], xT[:, b, k * P:(k + 1) * P], router_w[:, :],
                                        start=True, stop=True)
                    ins.then_inc(s_lg[b], 1)

        @block.scalar
        def _(act):
            prime(act, *s_xT, *s_all, *s_ls)
            with act.Fori(0, UNITS // 2) as i:
                for b in range(2):
                    act.wait_ge(s_tp[b], after(i))
                    act.wait_ge(s_lg[b], before(i))
                    act.activation(xT[:, b, :], ps_t[:, b, :], ACT.Copy).then_inc(s_xT[b], 1)
                    act.activation(T["xnT"][:, bass.ds((i * 2 + b) * UW, UW)], ps_t[:, b, :], ACT.Copy).then_inc(s_all[b], 1)
                for b in range(2):
                    act.wait_ge(s_lg[b], after(i))
                    act.activation(T["logits"][:, bass.ds((i * 2 + b) * UT, UT), :],
                                   ps_l[:, b, 0:UT * E].rearrange("p (t e) -> p t e", e=E), ACT.Copy).then_inc(s_ls[b], 1)


def softmax_experts(chain, act_sems, nc, T, red):
    s_in, s_out, dve = act_sems
    lg = T["logits"]
    chain(dve.tensor_reduce(red[:, 0, :], lg[:, :, :], AX.X, ALU.max))
    dve.tensor_tensor(lg[:, :, :], lg[:, :, :], bcast(red[:, 0, :], E), ALU.subtract).then_inc(s_in, 1)
    dve.wait_ge(s_out, 1)
    chain(dve.tensor_reduce(red[:, 0, :], lg[:, :, :], AX.X, ALU.add))
    chain(dve.reciprocal(red[:, 1, :], red[:, 0, :]))
    chain(dve.tensor_tensor(lg[:, :, :], lg[:, :, :], bcast(red[:, 1, :], E), ALU.mult))


def gates_top2(nc, tag, T):
    lg, gates, prio = T["logits"], T["gates"], T["prio"]
    with ExitStack() as ctx:
        n = Names(nc, ctx, tag)
        red = n.sb("red", [P, 2, TILES])
        left, key, hot = (n.sb(k, [P, TILES, E]) for k in ("left", "key", "hot"))
        s_c, s_in, s_out = n.sem("chain"), n.sem("shifted"), n.sem("exp_done")
        block = ctx.enter_context(nc.Block())

        @block.scalar
        def _(act):
            act.wait_ge(s_in, 1)
            act.activation(lg[:, :, :], lg[:, :, :], ACT.Exp).then_inc(s_out, 1)

        @block.vector
        def _(dve):
            chain = Chain(dve, s_c)
            softmax_experts(chain, (s_in, s_out, dve), nc, T, red)
            chain(dve.tensor_copy(left[:, :, :], lg[:, :, :]))
            for k in range(2):
                chain(dve.tensor_reduce(red[:, 0, :], left[:, :, :], AX.X, ALU.max))
                chain(dve.tensor_tensor(key[:, :, :], left[:, :, :], bcast(red[:, 0, :], E), ALU.is_equal))
                chain(dve.tensor_tensor(key[:, :, :], key[:, :, :],
                                        prio[:, :].unsqueeze(1).to_broadcast([P, TILES, E]), ALU.mult))
                chain(dve.tensor_reduce(red[:, 1, :], key[:, :, :], AX.X, ALU.max))
                chain(dve.tensor_tensor(hot[:, :, :], key[:, :, :], bcast(red[:, 1, :], E), ALU.is_equal))
                chain(dve.scalar_tensor_tensor(left[:, :, :], hot[:, :, :], -2.0, left[:, :, :], ALU.mult, ALU.add))
            chain(dve.tensor_scalar(key[:, :, :], left[:, :, :], 0.0, 0.5, ALU.is_lt, ALU.mult))
            chain(dve.tensor_tensor(gates[:, :, :], key[:, :, :], lg[:, :, :], ALU.mult))


def gates_expert_choice(nc, tag, T):
    lg, gates, ident = T["logits"], T["gates"], T["ident"]
    by_chunk = gates[:, :, :].rearrange("p (c b) e -> p c b e", c=CH)
    GB = P // E
    NG = BATCH // GB
    with ExitStack() as ctx:
        n = Names(nc, ctx, tag)
        red = n.sb("red", [P, 2, TILES])
        sT, wk, eq, cum, one = (n.sb(k, [P, NG, SEQ]) for k in ("sT", "wk", "eq", "cum", "one"))
        m8 = n.sb("m8", [P, NG, 8])
        cnt = n.sb("cnt", [P, NG, 2])
        ps = n.ps("ps", [P, NG, SEQ])
        s_c, s_in, s_out, s_p, s_tp = (n.sem(k) for k in ("chain", "shifted", "exp_done", "probs", "turned"))
        s_g, s_back = n.sem("gates_rows"), n.sem("turned_back")
        block = ctx.enter_context(nc.Block())

        @block.scalar
        def _(act):
            act.wait_ge(s_in, 1)
            act.activation(lg[:, :, :], lg[:, :, :], ACT.Exp).then_inc(s_out, 1)

        @block.tensor
        def _(pe):
            pe.wait_ge(s_p, 1)
            for g in range(NG):
                for c in range(CH):
                    ins = pe.transpose(ps[:, g, c * P:(c + 1) * P],
                                       by_chunk[:, c, g * GB:(g + 1) * GB, :].rearrange("p b e -> p (b e)"), ident[:, :])
            ins.then_inc(s_tp, 1)
            pe.wait_ge(s_g, 1)
            for g in range(NG):
                for c in range(CH):
                    ins = pe.transpose(ps[:, g, c * P:(c + 1) * P], wk[:, g, c * P:(c + 1) * P], ident[:, :])
            ins.then_inc(s_back, 1)

        @block.vector
        def _(dve):
            chain = Chain(dve, s_c)
            softmax_experts(chain, (s_in, s_out, dve), nc, T, red)
            chain(dve.memset(one[:, :, :], 1.0))
            dve.tensor_copy(by_chunk, lg[:, :, :].rearrange("p (b c) e -> p c b e", c=CH)).then_inc(s_p, 1)
            dve.wait_ge(s_tp, 1)
            chain(dve.tensor_copy(sT[:, :, :], ps[:, :, :]))
            chain(dve.tensor_copy(wk[:, :, :], sT[:, :, :]))
            rounds = (CAP - 1) // 8
            for r in range(rounds + 1):
                for g in range(NG):
                    ins = dve.max(m8[:, g, :], wk[:, g, :])
                chain(ins)
                if r < rounds:
                    for g in range(NG):
                        ins = dve.match_replace(wk[:, g, :], m8[:, g, :], wk[:, g, :], -1.0)
                    chain(ins)
            at = (CAP - 1) % 8
            for g in range(NG):
                thr = m8[:, g, at:at + 1]
                chain(dve.tensor_scalar(wk[:, g, :], sT[:, g, :], thr, 0.0, ALU.is_gt, ALU.add, accum_out=cnt[:, g, 0:1]))
                chain(dve.tensor_scalar(eq[:, g, :], sT[:, g, :], thr, None, ALU.is_equal))
                chain(dve.tensor_scalar(cnt[:, g, 1:2], cnt[:, g, 0:1], -1.0, float(CAP), ALU.mult, ALU.add))
                chain(dve.tensor_tensor_scan(cum[:, g, :], one[:, g, :], eq[:, g, :], 0.0, ALU.mult, ALU.add))
                chain(dve.scalar_tensor_tensor(eq[:, g, :], cum[:, g, :], cnt[:, g, 1:2], eq[:, g, :], ALU.is_le, ALU.mult))
                chain(dve.tensor_tensor(wk[:, g, :], wk[:, g, :], eq[:, g, :], ALU.add))
            dve.scalar_tensor_tensor(wk[:, :, :], wk[:, :, :], 0.5, sT[:, :, :], ALU.mult, ALU.mult).then_inc(s_g, 1)
            dve.wait_ge(s_back, 1)
            v = gates[:, :, :].rearrange("p (b c) e -> p b c e", c=CH)
            for g in range(NG):
                for c in range(CH):
                    dve.tensor_copy(v[:, g * GB:(g + 1) * GB, c, :],
                                    ps[:, g, c * P:(c + 1) * P].rearrange("p (b e) -> p b e", e=E))


def experts(nc, tag, T, up, down, shared, b1, b2row):
    x, gates, xnT = T["x"], T["gates"], T["xnT"]
    NE = E + shared
    uses = [(NE + 1) // 2, NE // 2]
    with ExitStack() as ctx:
        n = Names(nc, ctx, tag)
        hT = n.sb("hT", [P, 2, FC, UW])
        ps_h = n.ps("ps_h", [P, FC, UW])
        ps_y = n.ps("ps_y", [P, 2, UT, D])
        s_up = [n.sem(f"up_done{h}") for h in range(2)]
        s_gelu = [n.sem(f"gelu_done{h}") for h in range(2)]
        s_y = [n.sem(f"y_ready{b}") for b in range(2)]
        s_acc = [n.sem(f"y_added{b}") for b in range(2)]
        block = ctx.enter_context(nc.Block())

        @block.tensor
        def _(pe):
            prime(pe, *s_up, *s_y)
            with pe.Fori(0, UNITS) as i:
                def up_half(e, half):
                    pe.wait_ge(s_gelu[half], before(i * NE + e))
                    for c in range(2 * half, 2 * half + 2):
                        ins = pe.matmul(ps_h[:, c, :], up[:, e, c * P:(c + 1) * P], xnT[:, bass.ds(i * UW, UW)],
                                        start=True, stop=True)
                    ins.then_inc(s_up[half], 1)

                def down_all(e):
                    b = e % 2
                    for half in range(2):
                        pe.wait_ge(s_gelu[half], after(i * NE + e))
                    pe.wait_ge(s_acc[b], before(i * uses[b] + e // 2))
                    for t in range(UT):
                        if b2row is not None:
                            pe.matmul(ps_y[:, b, t, :], T["ones_row"][0:1, :], b2row[0:1, e, :], start=True, stop=False)
                        for c in range(FC):
                            ins = pe.matmul(ps_y[:, b, t, :], hT[:, b, c, t * P:(t + 1) * P], down[:, e, c, :],
                                            start=c == 0 and b2row is None, stop=c == FC - 1)
                    ins.then_inc(s_y[b], 1)

                for e in range(NE):
                    up_half(e, 0)
                    up_half(e, 1)
                    if e:
                        down_all(e - 1)
                down_all(NE - 1)

        @block.scalar
        def _(act):
            prime(act, *s_gelu)
            with act.Fori(0, UNITS) as i:
                for e in range(NE):
                    b = e % 2
                    act.wait_ge(s_y[b], before(i * uses[b] + e // 2))
                    for half in range(2):
                        act.wait_ge(s_up[half], after(i * NE + e))
                        if b1 is None:
                            cs = slice(2 * half, 2 * half + 2)
                            ins = act.activation(hT[:, b, cs, :], ps_h[:, cs, :], ACT.Gelu)
                        else:
                            for c in range(2 * half, 2 * half + 2):
                                ins = act.activation(hT[:, b, c, :], ps_h[:, c, :], ACT.Gelu, bias=b1[:, e, c:c + 1])
                        ins.then_inc(s_gelu[half], 1)

        @block.vector
        def _(dve):
            prime(dve, *s_acc)
            with dve.Fori(0, UNITS) as i:
                for e in range(NE):
                    b = e % 2
                    dve.wait_ge(s_y[b], after(i * uses[b] + e // 2))
                    if e:
                        dve.wait_ge(s_acc[1 - b], after(i * uses[1 - b] + (e - 1) // 2))
                    for t in range(UT):
                        tile = bass.ds(i * UT + t, 1)
                        gate = gates[:, tile, e] if e < E else 0.5
                        ins = dve.scalar_tensor_tensor(x[:, tile, :], ps_y[:, b, t, :].unsqueeze(1), gate, x[:, tile, :],
                                                       ALU.mult, ALU.add)
                    ins.then_inc(s_acc[b], 1)


def attention(nc, tag, T, W, dist, result, residual):
    x, mean, rstd, ident = T["x"], T["mean"], T["rstd"], T["ident"]
    cols = T["cols"]
    rows = T["rows"][0:W["aug"].shape[0]]
    PAIRS = HEADS // 2
    with ExitStack() as ctx:
        n = Names(nc, ctx, tag)
        xn = n.sb("xn", [P, CH, D])
        xT = n.sb("xT", [P, SEQ])
        rq, rk = n.sb("rq", [P, G, SEQ]), n.sb("rk", [P, G, SEQ])
        qs = n.sb("qs", [P, G, SEQ], F32R)
        qm = n.sb("qm", [P, G, SEQ], F32R)
        km = n.sb("km", [P, G, HG, SEQ], F32R)
        va = n.sb("va", [P, CH, HEADS, HW])
        mx = n.sb("mx", [P, HEADS, CH])
        ms = n.sb("ms", [P, CH, HEADS, HW])
        pT = n.sb("pT", [P, 2, 2, CH, SEQ])
        oT = n.sb("oT", [P, G, SEQ])
        rs = n.sb("rs", [P, G * CH * HG])
        on = n.sb("on", [P, CH, HEADS, HD])
        ps_q = n.ps("ps_q", [P, G, SEQ])
        ps_s = n.ps("ps_s", [P, 2, CH, SEQ])
        ps_k = ps_s
        ps_t = n.ps("ps_t", [P, 2, CH, SEQ])
        ps_o = n.ps("ps_o", [P, 2, 512])
        sem = {k: n.sem(k) for k in (
            "zeroed", "xn", "x_turned", "xT", "proj_q", "proj_k", "proj_v", "r_q", "r_k", "qs", "km", "va",
            "scores", "max", "neg", "lo", "max_turned", "qm", "scoresT", "probs", "pv", "oT", "out_turned",
            "recip", "scaled", "stored")}
        block = ctx.enter_context(nc.Block())

        @block.vector
        def _(dve):
            dve.memset(va[:, :, :, :], 0.0).then_inc(sem["zeroed"], 1)
            dve.wait_ge(sem["zeroed"], 1)
            dve.memset(va[:, :, :, HD:HD + 1], 1.0).then_inc(sem["zeroed"], 1)
            dve.memset(ms[:, :, :, :], 0.0).then_inc(sem["zeroed"], 1)
            dve.memset(km[:, :, :, :].bitcast(F32), 0.0).then_inc(sem["zeroed"], 1)
            dve.wait_ge(sem["zeroed"], 4)
            prime(dve, sem["stored"])
            with dve.Fori(0, BATCH) as i:
                for c in range(CH):
                    t = bass.ds(i * CH + c, 1)
                    ins = dve.tensor_scalar(xn[:, c, :], x[:, t, :], mean[:, t], rstd[:, t], ALU.subtract, ALU.mult)
                ins.then_inc(sem["xn"], 1)
                dve.wait_ge(sem["r_q"], i + 1)
                dve.scalar_tensor_tensor(qs[:, :, :], ps_q[:, :, :], cols[:, 0:1], rq[:, :, :], ALU.mult, ALU.add)\
                   .then_inc(sem["qs"], 1)
                dve.wait_ge(sem["r_k"], i + 1)
                for h in range(HG):
                    r = slice(h * HW, (h + 1) * HW)
                    ins = dve.scalar_tensor_tensor(km[r, :, h, :], ps_k[r, :, :, :].rearrange("p a b s -> p (a b) s"),
                                                   cols[r, 2:3], rk[r, :, :], ALU.mult, ALU.add)
                ins.then_inc(sem["km"], 1)
                dve.wait_ge(sem["proj_v"], i + 1)
                v_in = ps_o[:, 1, 0:CH * D].rearrange("p (c h d) -> p c h d", c=CH, d=HD)
                if W["bv"] is None:
                    ins = dve.tensor_copy(va[:, :, :, 0:HD], v_in)
                else:
                    for c in range(CH):
                        ins = dve.tensor_tensor(va[:, c, :, 0:HD], v_in[:, c, :, :],
                                                W["bv"][:, :].rearrange("p (h d) -> p h d", d=HD), ALU.add)
                ins.then_inc(sem["va"], 1)
                for u in range(PAIRS):
                    dve.wait_ge(sem["scores"], i * PAIRS + u + 1)
                    dve.tensor_reduce(mx[:, 2 * u:2 * u + 2, :], ps_s[:, :, :, :], AX.X, ALU.max).then_inc(sem["max"], 1)
                dve.wait_ge(sem["max"], (i + 1) * PAIRS)
                m_in = mx[:, :, :].rearrange("p h c -> p c h")
                hi = ms[:, :, :, ROW_M]
                dve.tensor_scalar(hi.bitcast(F32R), m_in, -1.0, None, ALU.mult).then_inc(sem["neg"], 1)
                dve.wait_ge(sem["neg"], i + 1)
                dve.scalar_tensor_tensor(ms[:, :, :, ROW_M + 1], m_in, -1.0, hi, ALU.mult, ALU.subtract).then_inc(sem["lo"], 1)
                dve.wait_ge(sem["max_turned"], i + 1)
                dve.tensor_tensor(qm[:, :, :], ps_q[:, :, :], qs[:, :, :].bitcast(F32), ALU.add).then_inc(sem["qm"], 1)
                dve.wait_ge(sem["out_turned"], i + 1)
                o_in = ps_q[:, :, :].rearrange("p g (c h w) -> p g c h w", c=CH, w=HW)
                dve.reciprocal(rs[:, :].rearrange("p (g c h) -> p g c h", g=G, c=CH), o_in[:, :, :, :, HD]).then_inc(sem["recip"], 1)
                dve.wait_ge(sem["recip"], i + 1)
                for g in range(G):
                    sums = bcast(rs[:, g * CH * HG:(g + 1) * CH * HG], HD).rearrange("p (c h) d -> p c h d", c=CH)
                    dst = on[:, :, g * HG:(g + 1) * HG, :]
                    if not residual:
                        dst = result[:, bass.ds(i * CH, CH), g * HG * HD:(g + 1) * HG * HD].rearrange("p c (h d) -> p c h d", d=HD)
                    ins = dve.tensor_tensor(dst, o_in[:, g, :, :, 0:HD], sums, ALU.mult)
                if residual:
                    ins.then_inc(sem["scaled"], 1)
                    dve.wait_ge(sem["scaled"], i + 1)
                    xs = result[:, bass.ds(i * CH, CH), :]
                    ins = dve.tensor_tensor(xs, xs, on[:, :, :, :].rearrange("p c h d -> p c (h d)"), ALU.add)
                ins.then_inc(sem["stored"], 1)

        @block.tensor
        def _(pe):
            with pe.Fori(0, BATCH) as i:
                pe.wait_ge(sem["xn"], i + 1)
                for c in range(CH):
                    ins = pe.transpose(ps_o[:, 0, c * P:(c + 1) * P], xn[:, c, :], ident[:, :])
                ins.then_inc(sem["x_turned"], 1)
                pe.wait_ge(sem["xT"], i + 1)
                pe.wait_ge(sem["stored"], before(i))
                for g in range(G):
                    gs = slice(g * P, (g + 1) * P)
                    pe.matmul(ps_q[:, g, :], W["q"][:, gs], xT[:, :], start=True, stop=False)
                    ins = pe.matmul(ps_q[:, g, :], W["aug"][:, 0, gs], rows[:, 0, :], start=False, stop=True)
                ins.then_inc(sem["proj_q"], 1)
                for g in range(G):
                    gs = slice(g * P, (g + 1) * P)
                    pe.matmul(ps_k[:, g // 2, g % 2, :], W["k"][:, gs], xT[:, :], start=True, stop=False)
                    ins = pe.matmul(ps_k[:, g // 2, g % 2, :], W["aug"][:, 1, gs], rows[:, 1, :], start=False, stop=True)
                ins.then_inc(sem["proj_k"], 1)
                for c in range(CH):
                    ins = pe.matmul(ps_o[:, 1, c * D:(c + 1) * D], xT[:, c * P:(c + 1) * P], W["v"][:, :], start=True, stop=True)
                ins.then_inc(sem["proj_v"], 1)
                pe.wait_ge(sem["qs"], i + 1)
                pe.wait_ge(sem["km"], i + 1)
                for u in range(PAIRS):
                    if u:
                        pe.wait_ge(sem["max"], i * PAIRS + u)
                    for j in range(2):
                        g, h = divmod(2 * u + j, HG)
                        for c in range(CH):
                            ins = pe.matmul(ps_s[:, j, c, :], qs[:, g, c * P:(c + 1) * P], km[:, g, h, :],
                                            start=True, stop=dist is None)
                            if dist is not None:
                                for part in range(2):
                                    ins = pe.matmul(ps_s[:, j, c, :], dist["eye"][:, part, :], dist["tab"][:, c, :],
                                                    start=False, stop=part == 1)
                    ins.then_inc(sem["scores"], 1)
                pe.wait_ge(sem["lo"], i + 1)
                for g in range(G):
                    for c in range(CH):
                        ins = pe.transpose(ps_q[:, g, c * P:(c + 1) * P],
                                           ms[:, c, g * HG:(g + 1) * HG, :].rearrange("p h w -> p (h w)"), ident[:, :])
                ins.then_inc(sem["max_turned"], 1)
                pe.wait_ge(sem["qm"], i + 1)
                pe.wait_ge(sem["va"], i + 1)

                def scores_turned(u):
                    if u:
                        pe.wait_ge(sem["probs"], i * PAIRS + u)
                    for j in range(2):
                        g, h = divmod(2 * u + j, HG)
                        for c in range(CH):
                            ins = pe.matmul(ps_t[:, j, c, :], km[:, g, h, c * P:(c + 1) * P], qm[:, g, :],
                                            start=True, stop=dist is None)
                            if dist is not None:
                                for part in range(2):
                                    ins = pe.matmul(ps_t[:, j, c, :], dist["eye"][:, part, :], dist["tab"][:, c, :],
                                                    start=False, stop=part == 1)
                    ins.then_inc(sem["scoresT"], 1)

                def weigh_values(u):
                    g = u // 2
                    pe.wait_ge(sem["probs"], i * PAIRS + u + 1)
                    if u % 2 == 0 and g >= 2:
                        pe.wait_ge(sem["oT"], i * G + g - 1)
                    for j in range(2):
                        head = 2 * u + j
                        h = head % HG
                        for c in range(CH):
                            ins = pe.matmul(ps_o[h * HW:(h + 1) * HW, g % 2, 0:SEQ], va[:, c, head, :], pT[:, u % 2, j, c, :],
                                            start=c == 0, stop=c == CH - 1)
                    ins.then_inc(sem["pv"], 1)

                for u in range(PAIRS):
                    scores_turned(u)
                    if u:
                        weigh_values(u - 1)
                weigh_values(PAIRS - 1)
                for g in range(G):
                    pe.wait_ge(sem["oT"], i * G + g + 1)
                    for c in range(CH):
                        ins = pe.transpose(ps_q[:, g, c * P:(c + 1) * P], oT[:, g, c * P:(c + 1) * P], ident[:, :])
                ins.then_inc(sem["out_turned"], 1)

        @block.scalar
        def _(act):
            with act.Fori(0, BATCH) as i:
                act.wait_ge(sem["x_turned"], i + 1)
                act.activation(xT[:, :], ps_o[:, 0, 0:SEQ], ACT.Copy).then_inc(sem["xT"], 1)
                act.wait_ge(sem["proj_q"], i + 1)
                act.activation(rq[:, :, :].bitcast(F32R), ps_q[:, :, :], ACT.Copy, scale=cols[:, 1:2]).then_inc(sem["r_q"], 1)
                act.wait_ge(sem["proj_k"], i + 1)
                act.activation(rk[:, :, :].bitcast(F32R), ps_k[:, :, :, :].rearrange("p a b s -> p (a b) s"), ACT.Copy,
                               scale=cols[:, 3:4]).then_inc(sem["r_k"], 1)
                for u in range(PAIRS):
                    act.wait_ge(sem["scoresT"], i * PAIRS + u + 1)
                    if u >= 2:
                        act.wait_ge(sem["pv"], i * PAIRS + u - 1)
                    act.activation(pT[:, u % 2, :, :, :], ps_t[:, :, :, :], ACT.Exp, scale=SM_SCALE).then_inc(sem["probs"], 1)
                    if u % 2 == 0 and u:
                        g = u // 2 - 1
                        act.wait_ge(sem["pv"], i * PAIRS + u)
                        act.activation(oT[:, g, :], ps_o[:, g % 2, 0:SEQ], ACT.Copy).then_inc(sem["oT"], 1)
                act.wait_ge(sem["pv"], (i + 1) * PAIRS)
                act.activation(oT[:, G - 1, :], ps_o[:, (G - 1) % 2, 0:SEQ], ACT.Copy).then_inc(sem["oT"], 1)



def attention_weights(nc, tag, parts, dist, T):
    with ExitStack() as ctx:
        n = Names(nc, ctx, tag)
        neg = n.sb("neg", [P, 3])
        s_z, s_c = n.sem("zeroed"), n.sem("chain")
        block = ctx.enter_context(nc.Block())

        @block.vector
        def _(dve):
            chain = Chain(dve, s_c)
            for dst, _, zero in parts:
                if zero:
                    chain(dve.memset(dst, 0.0))
            for dst, src, _ in parts:
                d = dst.rearrange("p (h w) -> p h w", w=HW)
                s = src.rearrange("p (h d) -> p h d", d=HD)
                for term in range(3):
                    dve.tensor_copy(d[:, :, term * HD:(term + 1) * HD], s)
            if dist is None:
                return
            chain(dve.tensor_scalar(neg[:, 0:1], dist["scale"][:, 0:1], -1.0, None, ALU.mult))
            chain(dve.tensor_copy(neg[:, 1:2].bitcast(F32R), neg[:, 0:1]))
            chain(dve.tensor_tensor(neg[:, 2:3], neg[:, 0:1], neg[:, 1:2], ALU.subtract))
            for part in range(2):
                dve.tensor_scalar(dist["eye"][:, part, :], T["ident"][:, :], neg[:, 1 + part:2 + part], None, ALU.mult)
            dve.tensor_copy(dist["tab"][:, :, :], dist["raw"][:, :, :])


def project_and_mlp(nc, tag, T, a_all, W):
    x, mean, rstd, ident = T["x"], T["mean"], T["rstd"], T["ident"]
    with ExitStack() as ctx:
        n = Names(nc, ctx, tag)
        a = n.sb("a", [P, UT, D])
        r0, r1 = n.sb("r0", [P, UT, D]), n.sb("r1", [P, UT, D])
        r2, r3 = n.sb("r2", [P, UT, D]), n.sb("r3", [P, UT, D])
        aT, x1T = n.sb("aT", [P, UW]), n.sb("x1T", [P, UW])
        hT = n.sb("hT", [P, FC, UW])
        st, mv = n.sb("st", [P, UT, 6]), n.sb("mv", [P, UT, 3])
        rs = n.sb("rs", [P, UT])
        ps_t, ps_h, ps_y = n.ps("ps_t", [P, UW]), n.ps("ps_h", [P, FC, UW]), n.ps("ps_y", [P, UT, D])
        sem = {k: n.sem(k) for k in ("a", "a_turned", "aT", "proj", "var", "pow", "x1", "x1_turned", "x1T", "up", "h", "y", "own")}
        block = ctx.enter_context(nc.Block())

        def wide(v):
            return v[:, :].unsqueeze(1).to_broadcast([P, UT, D])

        OWN = 18

        @block.gpsimd
        def _(pool):
            with pool.Fori(0, UNITS) as i:
                pool.tensor_copy(a[:, :, :], a_all[:, bass.ds(i * UT, UT), :]).then_inc(sem["a"], 1)
                for k in range(2):
                    pool.wait_ge(sem["var"], 2 * i + k + 1)
                    pool.tensor_tensor(rs[:, :], mv[:, :, 1], T["neg_half"][:, 0:UT], ALU.pow).then_inc(sem["pow"], 1)

        @block.tensor
        def _(pe):
            def turn(src, done):
                for k in range(UT):
                    ins = pe.transpose(ps_t[:, k * P:(k + 1) * P], src[:, k, :], ident[:, :])
                ins.then_inc(done, 1)

            with pe.Fori(0, UNITS) as i:
                pe.wait_ge(sem["a"], i + 1)
                turn(a, sem["a_turned"])
                pe.wait_ge(sem["aT"], i + 1)
                for k in range(UT):
                    ins = pe.matmul(ps_y[:, k, :], aT[:, k * P:(k + 1) * P], W["o"][:, :], start=True, stop=True)
                ins.then_inc(sem["proj"], 1)
                pe.wait_ge(sem["x1"], i + 1)
                turn(r1, sem["x1_turned"])
                pe.wait_ge(sem["x1T"], i + 1)
                for c in range(FC):
                    pe.matmul(ps_h[:, c, :], W["up"][:, c * P:(c + 1) * P], x1T[:, :], start=True, stop=True)\
                      .then_inc(sem["up"], 1)
                pe.wait_ge(sem["h"], (i + 1) * FC)
                for k in range(UT):
                    for c in range(FC):
                        ins = pe.matmul(ps_y[:, k, :], hT[:, c, k * P:(k + 1) * P], W["down"][:, c, :],
                                        start=c == 0, stop=c == FC - 1)
                ins.then_inc(sem["y"], 1)

        @block.scalar
        def _(act):
            with act.Fori(0, UNITS) as i:
                act.wait_ge(sem["a_turned"], i + 1)
                act.activation(aT[:, :], ps_t[:, :], ACT.Copy).then_inc(sem["aT"], 1)
                act.wait_ge(sem["x1_turned"], i + 1)
                act.activation(x1T[:, :], ps_t[:, :], ACT.Copy).then_inc(sem["x1T"], 1)
                for c in range(FC):
                    act.wait_ge(sem["up"], i * FC + c + 1)
                    act.activation(hT[:, c, :], ps_h[:, c, :], ACT.Relu, bias=W["b1"][:, c:c + 1]).then_inc(sem["h"], 1)

        @block.vector
        def _(dve):
            with dve.Fori(0, UNITS) as i:
                steps = [0]

                def step(ins):
                    steps[0] += 1
                    ins.then_inc(sem["own"], 1)
                    dve.wait_ge(sem["own"], i * OWN + steps[0])

                def norm(src, dst, k):
                    for t in range(UT):
                        ins = dve.bn_stats(st[:, t, :], src[:, t, :])
                    step(ins)
                    dve.tensor_tensor(mv[:, :, 0], st[:, :, 1], st[:, :, 4], ALU.add)
                    dve.tensor_tensor(mv[:, :, 2], st[:, :, 1], st[:, :, 4], ALU.subtract)
                    step(dve.tensor_tensor(mv[:, :, 1], st[:, :, 2], st[:, :, 5], ALU.add))
                    dve.tensor_scalar(mv[:, :, 0], mv[:, :, 0], 0.5, None, ALU.mult)
                    dve.scalar_tensor_tensor(mv[:, :, 2], mv[:, :, 2], 0.25, mv[:, :, 2], ALU.mult, ALU.mult)
                    step(dve.tensor_scalar(mv[:, :, 1], mv[:, :, 1], 1.0 / D, EPS, ALU.mult, ALU.add))
                    dve.tensor_tensor(mv[:, :, 1], mv[:, :, 1], mv[:, :, 2], ALU.add).then_inc(sem["var"], 1)
                    dve.wait_ge(sem["pow"], 2 * i + k + 1)
                    for t in range(UT):
                        ins = dve.tensor_scalar(dst[:, t, :], src[:, t, :], mv[:, t, 0:1], rs[:, t:t + 1],
                                                ALU.subtract, ALU.mult)
                    step(ins)

                for t in range(UT):
                    tile = bass.ds(i * UT + t, 1)
                    ins = dve.tensor_scalar(r0[:, t, :], x[:, tile, :], mean[:, tile], rstd[:, tile], ALU.subtract, ALU.mult)
                step(ins)
                step(dve.tensor_tensor(r0[:, :, :], r0[:, :, :], wide(W["bo"]), ALU.add))
                dve.wait_ge(sem["proj"], i + 1)
                step(dve.tensor_tensor(r2[:, :, :], ps_y[:, :, :], r0[:, :, :], ALU.add))
                norm(r2, r3, 0)
                step(dve.tensor_tensor(r3[:, :, :], r3[:, :, :], wide(W["g1"]), ALU.mult))
                step(dve.tensor_tensor(r1[:, :, :], r3[:, :, :], wide(W["be1"]), ALU.add))
                dve.sem_inc(sem["x1"], 1)
                step(dve.tensor_tensor(r2[:, :, :], r1[:, :, :], wide(W["b2"]), ALU.add))
                dve.wait_ge(sem["y"], i + 1)
                step(dve.tensor_tensor(r3[:, :, :], ps_y[:, :, :], r2[:, :, :], ALU.add))
                norm(r3, r2, 1)
                step(dve.tensor_tensor(r2[:, :, :], r2[:, :, :], wide(W["g2"]), ALU.mult))
                step(dve.tensor_tensor(r2[:, :, :], r2[:, :, :], wide(W["be2"]), ALU.add))
                xs = x[:, bass.ds(i * UT, UT), :]
                step(dve.tensor_tensor(xs, xs, r2[:, :, :], ALU.add))
                assert steps[0] == OWN, steps[0]



def ffn(nc, tag, T, W, shared):
    layernorm_stats(nc, tag + "s", T["x"], T["mean"], T["rstd"], T["neg_half"])
    with ExitStack() as ctx:
        n = Names(nc, ctx, tag)
        T = dict(T, xnT=n.sb("xnT", [P, TILES * P]), logits=n.sb("logits", [P, TILES, E]), gates=n.sb("gates", [P, TILES, E]))
        normalise_and_route(nc, tag + "r", T, W["router"], xn_residual=bool(shared))
        (gates_top2 if shared else gates_expert_choice)(nc, tag + "g", T)
        experts(nc, tag + "e", T, W["up"], W["down"], shared, W.get("b1"), W.get("b2"))


def program(nc, A, out):
    with ExitStack() as ctx:
        n = Names(nc, ctx, "k")
        T = {"x": n.sb("x", [P, TILES, D]), "mean": n.sb("mean", [P, TILES]), "rstd": n.sb("rstd", [P, TILES]),
             "neg_half": n.sb("neg_half", [P, TILES]), "ident": n.sb("ident", [P, P]), "prio": n.sb("prio", [P, E]),
             "ones_row": n.sb("ones_row", [1, P]), "cols": n.sb("cols", [P, 16]), "rows": n.sb("rows", [1 + HEADS, 2, SEQ])}
        s_in, s_c, s_out = n.sem("loaded"), n.sem("constants"), n.sem("stored")

        def load(tag, *pairs):
            with ExitStack() as c:
                s_load = Names(nc, c, tag).sem("loaded")
                block = c.enter_context(nc.Block())

                @block.sync
                def _(sp):
                    for dst, src in pairs:
                        sp.dma_start(dst, src).then_inc(s_load, 16)
                    sp.wait_ge(s_load, 16 * len(pairs))

        load("in", (T["x"][:, :, :], A["L0_attn_x"].rearrange("b (c p) d -> p (b c) d", p=P)),
             (T["ident"][:, :], A["c_ident"]), (T["prio"][:, :], A["c_prio"]), (T["cols"][:, :], A["c_cols"]),
             (T["rows"][:, :, :], A["c_rows"].rearrange("k (s t) -> k s t", s=2)))
        with nc.Block() as block:
            @block.vector
            def _(dve):
                dve.memset(T["neg_half"][:, :], -0.5).then_inc(s_c, 1)
                dve.memset(T["ones_row"][:, :], 1.0).then_inc(s_c, 1)

        def l0_ffn(tag):
            with ExitStack() as c:
                m = Names(nc, c, tag)
                W = {"up": m.sb("up0", [P, E, F]), "down": m.sb("down0", [P, E, FC, D]), "b1": m.sb("b1", [P, E, FC]),
                     "b2": m.sb("b2", [1, E, D]), "router": m.sb("router0", [P, E])}
                load(tag + "w", (W["router"][:, :], A["L0_router_T"]),
                     (W["up"][:, :, :], A["L0_ffn_w1"].rearrange("e d f -> d e f")),
                     (W["down"][:, :, :, :], A["L0_ffn_w2"].rearrange("e (c f) d -> f e c d", f=P)),
                     (W["b1"][:, :, :], A["L0_b1_T"]), (W["b2"][:, :, :], A["L0_ffn_b2"].unsqueeze(0)))
                ffn(nc, tag, T, W, 0)

        def l1_ffn(tag):
            with ExitStack() as c:
                m = Names(nc, c, tag)
                W = {"up": m.sb("up1", [P, E + 1, F]), "down": m.sb("down1", [P, E + 1, FC, D]), "router": m.sb("router1", [P, E])}
                load(tag + "w", (W["router"][:, :], A["L1_ffn_router_w"]),
                     (W["up"][:, 0:E, :], A["L1_ffn_routed_up"].rearrange("e d f -> d e f")),
                     (W["up"][:, E:E + 1, :], A["L1_ffn_shared_up"].rearrange("e d f -> d e f")),
                     (W["down"][:, 0:E, :, :], A["L1_ffn_routed_down"].rearrange("e (c f) d -> f e c d", f=P)),
                     (W["down"][:, E:E + 1, :, :], A["L1_ffn_shared_down"].rearrange("e (c f) d -> f e c d", f=P)))
                ffn(nc, tag, T, W, 1)

        def stacks(m, aug_rows):
            return {"q": m.sb("wq", [P, HEADS * HW]), "k": m.sb("wk", [P, HEADS * HW]), "v": m.sb("wv", [P, D]),
                    "aug": m.sb("aug", [aug_rows, 2, HEADS * HW]), "bv": None}

        def l0_attention(tag):
            with ExitStack() as c:
                m = Names(nc, c, tag)
                W = stacks(m, 1)
                raw = m.sb("raw", [P, 2, D])
                qkv = A["L0_qkv_T"]
                load(tag + "w", (raw[:, :, :], qkv[:, 0:2 * D].rearrange("p (k d) -> p k d", k=2)),
                     (W["v"][:, :], qkv[:, 2 * D:3 * D]), (W["aug"][:, :, :], A["c_aug"][0:1, :].rearrange("k (s t) -> k s t", s=2)))
                attention_weights(nc, tag + "p", [(W["q"][:, :], raw[:, 0, :], True), (W["k"][:, :], raw[:, 1, :], True)], None, T)
                layernorm_stats(nc, tag + "s", T["x"], T["mean"], T["rstd"], T["neg_half"])
                attention(nc, tag + "c", T, W, None, T["x"], True)

        def l1_attention(tag):
            with ExitStack() as c:
                m = Names(nc, c, tag)
                a_all = m.sb("a_all", [P, TILES, D])
                W = {"o": m.sb("wo", [P, D]), "up": m.sb("w1", [P, F]), "down": m.sb("w2", [P, FC, D]), "b1": m.sb("bf1", [P, FC])}
                for k in ("bo", "g1", "be1", "b2", "g2", "be2", "bv"):
                    W[k] = m.sb(k, [P, D])

                def wide(name):
                    return A[name].unsqueeze(0).to_broadcast([P, D])

                load(tag + "w", (W["o"][:, :], A["L1_attn_Wo"]), (W["up"][:, :], A["L1_attn_W1"]),
                     (W["down"][:, :, :], A["L1_attn_W2"].rearrange("(c f) d -> f c d", f=P)), (W["b1"][:, :], A["L1_W1b_T"]),
                     (W["bo"][:, :], wide("L1_attn_bo")), (W["g1"][:, :], wide("L1_attn_ln1_g")), (W["be1"][:, :], wide("L1_attn_ln1_b")),
                     (W["b2"][:, :], wide("L1_attn_b2")), (W["g2"][:, :], wide("L1_attn_ln2_g")), (W["be2"][:, :], wide("L1_attn_ln2_b")),
                     (W["bv"][:, :], wide("L1_attn_bv")))
                layernorm_stats(nc, tag + "s", T["x"], T["mean"], T["rstd"], T["neg_half"])
                with ExitStack() as c2:
                    m2 = Names(nc, c2, tag + "2")
                    S = stacks(m2, 1 + HEADS)
                    S["bv"] = W["bv"]
                    raw, bias = m2.sb("raw", [P, 2, D]), m2.sb("bias", [1, 2, D])
                    dist = {"scale": m2.sb("scale", [P, 1]), "eye": m2.sb("eye", [P, 2, P], F32R),
                            "tab": m2.sb("tab", [P, CH, SEQ], F32R), "raw": m2.sb("rawtab", [P, CH, SEQ])}
                    load(tag + "2w", (raw[:, 0, :], A["L1_attn_Wq"]), (raw[:, 1, :], A["L1_attn_Wk"]), (S["v"][:, :], A["L1_attn_Wv"]),
                         (bias[:, 0, :], A["L1_attn_bq"].unsqueeze(0)), (bias[:, 1, :], A["L1_attn_bk"].unsqueeze(0)),
                         (S["aug"][:, :, :], A["c_aug"].rearrange("k (s t) -> k s t", s=2)),
                         (dist["scale"][:, :], A["L1_dist_scale"].to_broadcast([P, 1])),
                         (dist["raw"][:, :, :], A["c_dist"].rearrange("p (c t) -> p c t", c=CH)))
                    attention_weights(nc, tag + "p", [
                        (S["q"][:, :], raw[:, 0, :], True), (S["k"][:, :], raw[:, 1, :], True),
                        (S["aug"][0:1, 0, :], bias[:, 0, :], False), (S["aug"][0:1, 1, :], bias[:, 1, :], False)], dist, T)
                    attention(nc, tag + "c", T, S, dist, a_all, False)
                project_and_mlp(nc, tag + "m", T, a_all, W)

        l0_ffn("a")
        l0_attention("b")
        l0_ffn("c")
        l1_ffn("d")
        l1_attention("e")
        l1_ffn("f")

        with nc.Block() as block:
            @block.sync
            def _(sp):
                sp.dma_start(out.rearrange("b (c p) d -> p (b c) d", p=P), T["x"][:, :, :]).then_inc(s_out, 16)
                sp.wait_ge(s_out, 16)


def kernel(**inputs):
    import concourse.bacc as _bacc
    from concourse.bass_utils import run_bass_kernel_spmd as _run

    a = {k: np.ascontiguousarray(v) for k, v in inputs.items()}
    a["L0_router_T"] = np.ascontiguousarray(np.transpose(a.pop("L0_ffn_router_w")))
    b1 = a.pop("L0_ffn_b1")
    a["L0_b1_T"] = np.ascontiguousarray(np.transpose(b1.reshape(E, FC, P), (2, 0, 1)))
    a["L0_qkv_T"] = np.ascontiguousarray(np.transpose(a.pop("L0_attn_W_qkv")))
    a["L1_W1b_T"] = np.ascontiguousarray(np.transpose(a.pop("L1_attn_b1").reshape(FC, P)))
    a["L1_dist_scale"] = a.pop("L1_attn_dist_scale").reshape(1, 1)
    a.update(shape_constants())

    nc = _bacc.Bacc("TRN2", target_bir_lowering=False, num_devices=1)
    arrays, aps = {}, {}
    for name, v in a.items():
        arrays[f"in_{name}"] = v
        aps[name] = nc.dram_tensor(f"in_{name}", v.shape, mybir.dt.from_np(v.dtype), kind="ExternalInput").ap()
    out = nc.dram_tensor("out_0", (BATCH, SEQ, D), F32, kind="ExternalOutput").ap()
    program(nc, aps, out)
    r = _run(nc, [arrays], core_ids=[0])
    return r.results[0]["out_0"]
```

```python
from contextlib import ExitStack

import numpy as np

import concourse.bass as bass
from concourse import mybir

F32 = mybir.dt.float32
F32R = mybir.dt.float32r
ALU = mybir.AluOpType
ACT = mybir.ActivationFunctionType
AX = mybir.AxisListType

P = 128
BATCH, SEQ, D = 32, 256, 128
CH = SEQ // P
TILES = BATCH * CH
UT = 4
UNITS = TILES // UT
UW = UT * P
E = 8
F = 512
FC = F // P
CAP = SEQ * 2 // E + 1
HEADS, HD = 16, D // 16
G, HG = 4, 4
HW = P // HG
ROW_M, ROW_MASK, ROW_DIST = 3 * HD, 3 * HD + 2, 3 * HD + 3
EPS = 1e-5
SM_SCALE = float(1.0 / np.sqrt(HD))
MASKED = -1e30
AUG_MASK = 2 * HW + 1
AUG_T, AUG_U = AUG_MASK + HEADS, AUG_MASK + HEADS + 1
AUG = AUG_U + 1


def shape_constants():
    ident = np.eye(P, dtype=np.float32)
    cols = np.zeros((P, 16), np.float32)
    r = np.arange(P) % HW
    term = r // HD
    distance = (r >= ROW_DIST) & (r < ROW_DIST + 4)
    cols[:, 0] = (term == 2) | distance
    cols[:, 1] = np.where(r >= ROW_M, 0, np.where(term == 2, -1, 1))
    cols[:, 2] = (term == 1) | (r == ROW_MASK) | distance
    cols[:, 3] = np.where(r >= ROW_M, 0, np.where(term == 1, -1, 1))
    cols[:, 4] = r == ROW_MASK
    cols[:, 5] = (r == ROW_M) | (r == ROW_M + 1)
    prio = np.broadcast_to(np.arange(E, 0, -1, dtype=np.float32), (P, E))
    t = np.arange(SEQ)
    below = np.maximum(t[:P, None] - t[None, :P], 0).astype(np.float32)
    dist = np.concatenate([below, below.T], axis=1)
    aug = np.zeros((AUG, 2, HEADS, HW), np.float32)
    rows = np.zeros((AUG, SEQ), np.float32)
    sign = np.where(t < P, 1, -1)
    rows[0] = rows[HW] = 1
    rows[2 * HW] = sign
    rows[AUG_T] = t
    rows[AUG_U] = sign * t
    aug[AUG_T, 0, :, ROW_DIST:ROW_DIST + 2] = 1
    aug[AUG_U, 1, :, ROW_DIST + 2:ROW_DIST + 4] = 1
    for h in range(HEADS):
        aug[AUG_MASK + h, 1, h, ROW_MASK] = 1
        rows[AUG_MASK + h, :h] = MASKED
    aug = aug.reshape(AUG, 2 * HEADS * HW)
    return {
        "c_ident": ident, "c_cols": cols, "c_prio": np.ascontiguousarray(prio),
        "c_iota": np.ascontiguousarray(np.broadcast_to(np.arange(CAP, dtype=np.float32), (P, CAP))), "c_dist": np.ascontiguousarray(dist),
        "c_aug": np.ascontiguousarray(aug), "c_rows": np.ascontiguousarray(rows),
    }


class Chain:

    def __init__(self, eng, sem):
        self.eng, self.sem, self.n = eng, sem, 0

    def __call__(self, ins):
        self.n += 1
        ins.then_inc(self.sem, 1)
        self.eng.wait_ge(self.sem, self.n)


def prime(eng, *sems):
    for s in sems:
        eng.sem_inc(s, 1)


def before(n):
    return n + 1


def after(n):
    return n + 2


def bcast(ap, n):
    return ap.unsqueeze(2).to_broadcast([ap.shape[0], ap.shape[1], n])


class Names:

    def __init__(self, nc, ctx, tag):
        self.nc, self.ctx, self.tag, self.sems = nc, ctx, tag, []
        ctx.callback(self.close)

    def sb(self, name, shape, dt=F32):
        return self.ctx.enter_context(self.nc.sbuf_tensor(f"{self.tag}_{name}", shape, dt))

    def ps(self, name, shape, dt=F32):
        return self.ctx.enter_context(self.nc.psum_tensor(f"{self.tag}_{name}", shape, dt))

    def sem(self, name):
        self.sems.append(self.nc.alloc_semaphore(f"{self.tag}_{name}"))
        return self.sems[-1]

    def close(self):
        if self.sems:
            self.nc.clear_and_free_semaphores(self.sems)
            self.nc.all_engine_barrier(sem_only=True)


def layernorm_stats(nc, tag, x, mean, rstd, neg_half):
    with ExitStack() as ctx:
        n = Names(nc, ctx, tag)
        st = n.sb("st", [P, TILES, 6])
        tmp = n.sb("tmp", [P, 2, TILES])
        s_st, s_v, s_p = n.sem("stats"), n.sem("var_ready"), n.sem("pow")
        block = ctx.enter_context(nc.Block())

        @block.vector
        def _(dve):
            chain = Chain(dve, s_v)
            with dve.Fori(0, TILES // 4) as i:
                for k in range(4):
                    dve.bn_stats(st[:, bass.ds(i * 4 + k, 1), :], x[:, bass.ds(i * 4 + k, 1), :]).then_inc(s_st, 1)
            dve.wait_ge(s_st, TILES)
            chain(dve.tensor_tensor(mean[:, :], st[:, :, 1], st[:, :, 4], ALU.add))
            chain(dve.tensor_scalar(mean[:, :], mean[:, :], 0.5, None, ALU.mult))
            chain(dve.tensor_tensor(tmp[:, 0, :], st[:, :, 1], st[:, :, 4], ALU.subtract))
            chain(dve.tensor_tensor(tmp[:, 1, :], st[:, :, 2], st[:, :, 5], ALU.add))
            chain(dve.tensor_tensor(tmp[:, 0, :], tmp[:, 0, :], tmp[:, 0, :], ALU.mult))
            chain(dve.tensor_scalar(tmp[:, 0, :], tmp[:, 0, :], 0.25, EPS, ALU.mult, ALU.add))
            chain(dve.scalar_tensor_tensor(tmp[:, 1, :], tmp[:, 1, :], 1.0 / D, tmp[:, 0, :], ALU.mult, ALU.add))

        @block.gpsimd
        def _(pool):
            pool.wait_ge(s_v, 7)
            pool.tensor_tensor(rstd[:, :], tmp[:, 1, :], neg_half[:, 0:TILES], ALU.pow).then_inc(s_p, 1)


def normalise_and_route(nc, tag, T, router_w, xn_residual):
    x, mean, rstd, ident = T["x"], T["mean"], T["rstd"], T["ident"]
    with ExitStack() as ctx:
        n = Names(nc, ctx, tag)
        xn = n.sb("xn", [P, 2, UT, D])
        xT = n.sb("xT", [P, 2, UW])
        ps_t = n.ps("ps_t", [P, 2, UW])
        ps_l = n.ps("ps_l", [P, 2, 512])
        s_xn = [n.sem(f"xn_ready{b}") for b in range(2)]
        s_res = n.sem("residual_added")
        s_tp = [n.sem(f"transposed{b}") for b in range(2)]
        s_xT = [n.sem(f"xT_ready{b}") for b in range(2)]
        s_all = [n.sem(f"xT_stored{b}") for b in range(2)]
        s_lo = [n.sem(f"xT_lo{b}") for b in range(2)]
        keep = "xh" in T
        s_lg = [n.sem(f"logits_ready{b}") for b in range(2)]
        s_ls = [n.sem(f"logits_stored{b}") for b in range(2)]
        block = ctx.enter_context(nc.Block())

        @block.vector
        def _(dve):
            prime(dve, *s_xn, *s_lo)
            with dve.Fori(0, UNITS // 2) as i:
                for b in range(2):
                    dve.wait_ge(s_tp[b], before(i))
                    for k in range(UT):
                        t = (i * 2 + b) * UT + k
                        ins = dve.tensor_scalar(xn[:, b, k, :], x[:, bass.ds(t, 1), :], mean[:, bass.ds(t, 1)],
                                                rstd[:, bass.ds(t, 1)], ALU.subtract, ALU.mult)
                    ins.then_inc(s_xn[b], 1)
                    if xn_residual:
                        dve.wait_ge(s_xn[b], after(i))
                        xs = x[:, bass.ds((i * 2 + b) * UT, UT), :]
                        dve.scalar_tensor_tensor(xs, xn[:, b, :, :], 0.5, xs, ALU.mult, ALU.add).then_inc(s_res, 1)
                        dve.wait_ge(s_res, i * 2 + b + 1)
                if keep:
                    for b in range(2):
                        cols = bass.ds((i * 2 + b) * UW, UW)
                        dve.wait_ge(s_xT[b], after(i))
                        dve.wait_ge(s_all[b], after(i))
                        dve.tensor_tensor(T["xl"][:, cols], xT[:, b, :], T["xh"][:, cols].bitcast(F32), ALU.subtract)\
                           .then_inc(s_lo[b], 1)

        @block.tensor
        def _(pe):
            prime(pe, *s_tp, *s_lg)
            with pe.Fori(0, UNITS // 2) as i:
                for b in range(2):
                    pe.wait_ge(s_xn[b], after(i))
                    pe.wait_ge(s_all[b] if keep else s_xT[b], before(i))
                    for k in range(UT):
                        ins = pe.transpose(ps_t[:, b, k * P:(k + 1) * P], xn[:, b, k, :], ident[:, :])
                    ins.then_inc(s_tp[b], 1)
                for b in range(2):
                    pe.wait_ge(s_xT[b], after(i))
                    pe.wait_ge(s_ls[b], before(i))
                    for k in range(UT):
                        ins = pe.matmul(ps_l[:, b, k * E:(k + 1) * E], xT[:, b, k * P:(k + 1) * P], router_w[:, :],
                                        start=True, stop=True)
                    ins.then_inc(s_lg[b], 1)

        @block.scalar
        def _(act):
            prime(act, *s_xT, *s_all, *s_ls)
            with act.Fori(0, UNITS // 2) as i:
                for b in range(2):
                    act.wait_ge(s_tp[b], after(i))
                    act.wait_ge(s_lg[b], before(i))
                    if keep:
                        act.wait_ge(s_lo[b], before(i))
                    act.activation(xT[:, b, :], ps_t[:, b, :], ACT.Copy).then_inc(s_xT[b], 1)
                    if keep:
                        act.activation(T["xh"][:, bass.ds((i * 2 + b) * UW, UW)], ps_t[:, b, :], ACT.Copy).then_inc(s_all[b], 1)
                for b in range(2):
                    act.wait_ge(s_lg[b], after(i))
                    act.activation(T["logits"][:, bass.ds((i * 2 + b) * UT, UT), :],
                                   ps_l[:, b, 0:UT * E].rearrange("p (t e) -> p t e", e=E), ACT.Copy).then_inc(s_ls[b], 1)


def softmax_experts(chain, act_sems, nc, T, red):
    s_in, s_out, dve = act_sems
    lg = T["logits"]
    chain(dve.tensor_reduce(red[:, 0, :], lg[:, :, :], AX.X, ALU.max))
    dve.tensor_tensor(lg[:, :, :], lg[:, :, :], bcast(red[:, 0, :], E), ALU.subtract).then_inc(s_in, 1)
    dve.wait_ge(s_out, 1)
    chain(dve.tensor_reduce(red[:, 0, :], lg[:, :, :], AX.X, ALU.add))
    chain(dve.reciprocal(red[:, 1, :], red[:, 0, :]))
    chain(dve.tensor_tensor(lg[:, :, :], lg[:, :, :], bcast(red[:, 1, :], E), ALU.mult))


def gates_top2(nc, tag, T):
    lg, gates, prio = T["logits"], T["gates"], T["prio"]
    with ExitStack() as ctx:
        n = Names(nc, ctx, tag)
        red = n.sb("red", [P, 2, TILES])
        left, key, hot = (n.sb(k, [P, TILES, E]) for k in ("left", "key", "hot"))
        s_c, s_in, s_out = n.sem("chain"), n.sem("shifted"), n.sem("exp_done")
        block = ctx.enter_context(nc.Block())

        @block.scalar
        def _(act):
            act.wait_ge(s_in, 1)
            act.activation(lg[:, :, :], lg[:, :, :], ACT.Exp).then_inc(s_out, 1)

        @block.vector
        def _(dve):
            chain = Chain(dve, s_c)
            softmax_experts(chain, (s_in, s_out, dve), nc, T, red)
            chain(dve.tensor_copy(left[:, :, :], lg[:, :, :]))
            for k in range(2):
                chain(dve.tensor_reduce(red[:, 0, :], left[:, :, :], AX.X, ALU.max))
                chain(dve.tensor_tensor(key[:, :, :], left[:, :, :], bcast(red[:, 0, :], E), ALU.is_equal))
                chain(dve.tensor_tensor(key[:, :, :], key[:, :, :],
                                        prio[:, :].unsqueeze(1).to_broadcast([P, TILES, E]), ALU.mult))
                chain(dve.tensor_reduce(red[:, 1, :], key[:, :, :], AX.X, ALU.max))
                chain(dve.tensor_tensor(hot[:, :, :], key[:, :, :], bcast(red[:, 1, :], E), ALU.is_equal))
                chain(dve.scalar_tensor_tensor(left[:, :, :], hot[:, :, :], -2.0, left[:, :, :], ALU.mult, ALU.add))
            chain(dve.tensor_scalar(key[:, :, :], left[:, :, :], 0.0, 0.5, ALU.is_lt, ALU.mult))
            chain(dve.tensor_tensor(gates[:, :, :], key[:, :, :], lg[:, :, :], ALU.mult))


def gates_expert_choice(nc, tag, T):
    lg, gates, ident = T["logits"], T["gates"], T["ident"]
    by_chunk = gates[:, :, :].rearrange("p (c b) e -> p c b e", c=CH)
    GB = P // E
    NG = BATCH // GB
    with ExitStack() as ctx:
        n = Names(nc, ctx, tag)
        red = n.sb("red", [P, 2, TILES])
        sT, wk, eq, cum, one = (n.sb(k, [P, NG, SEQ]) for k in ("sT", "wk", "eq", "cum", "one"))
        m8 = n.sb("m8", [P, NG, 8])
        cnt = n.sb("cnt", [P, NG, 2])
        ps, ps_c = n.ps("ps", [P, NG, SEQ]), n.ps("ps_c", [P, NG, SEQ])
        s_c, s_in, s_out, s_p, s_tp = (n.sem(k) for k in ("chain", "shifted", "exp_done", "probs", "turned"))
        s_g, s_back = n.sem("gates_rows"), n.sem("turned_back")
        block = ctx.enter_context(nc.Block())

        @block.scalar
        def _(act):
            act.wait_ge(s_in, 1)
            act.activation(lg[:, :, :], lg[:, :, :], ACT.Exp).then_inc(s_out, 1)

        @block.tensor
        def _(pe):
            pe.wait_ge(s_p, 1)
            for g in range(NG):
                for c in range(CH):
                    ins = pe.transpose(ps[:, g, c * P:(c + 1) * P],
                                       by_chunk[:, c, g * GB:(g + 1) * GB, :].rearrange("p b e -> p (b e)"), ident[:, :])
            ins.then_inc(s_tp, 1)
            pe.wait_ge(s_g, 1)
            for g in range(NG):
                for c in range(CH):
                    pe.transpose(ps[:, g, c * P:(c + 1) * P], wk[:, g, c * P:(c + 1) * P], ident[:, :])
                    ins = pe.transpose(ps_c[:, g, c * P:(c + 1) * P], cum[:, g, c * P:(c + 1) * P], ident[:, :])
            ins.then_inc(s_back, 1)

        @block.vector
        def _(dve):
            chain = Chain(dve, s_c)
            softmax_experts(chain, (s_in, s_out, dve), nc, T, red)
            chain(dve.memset(one[:, :, :], 1.0))
            dve.tensor_copy(by_chunk, lg[:, :, :].rearrange("p (b c) e -> p c b e", c=CH)).then_inc(s_p, 1)
            dve.wait_ge(s_tp, 1)
            chain(dve.tensor_copy(sT[:, :, :], ps[:, :, :]))
            chain(dve.tensor_copy(wk[:, :, :], sT[:, :, :]))
            rounds = (CAP - 1) // 8
            for r in range(rounds + 1):
                for g in range(NG):
                    ins = dve.max(m8[:, g, :], wk[:, g, :])
                chain(ins)
                if r < rounds:
                    for g in range(NG):
                        ins = dve.match_replace(wk[:, g, :], m8[:, g, :], wk[:, g, :], -1.0)
                    chain(ins)
            at = (CAP - 1) % 8
            for g in range(NG):
                thr = m8[:, g, at:at + 1]
                chain(dve.tensor_scalar(wk[:, g, :], sT[:, g, :], thr, 0.0, ALU.is_gt, ALU.add, accum_out=cnt[:, g, 0:1]))
                chain(dve.tensor_scalar(eq[:, g, :], sT[:, g, :], thr, None, ALU.is_equal))
                chain(dve.tensor_scalar(cnt[:, g, 1:2], cnt[:, g, 0:1], -1.0, float(CAP), ALU.mult, ALU.add))
                chain(dve.tensor_tensor_scan(cum[:, g, :], one[:, g, :], eq[:, g, :], 0.0, ALU.mult, ALU.add))
                chain(dve.scalar_tensor_tensor(eq[:, g, :], cum[:, g, :], cnt[:, g, 1:2], eq[:, g, :], ALU.is_le, ALU.mult))
                chain(dve.tensor_tensor(wk[:, g, :], wk[:, g, :], eq[:, g, :], ALU.add))
            for g in range(NG):
                ins = dve.tensor_tensor_scan(cum[:, g, :], one[:, g, :], wk[:, g, :], 0.0, ALU.mult, ALU.add)
            chain(ins)
            chain(dve.tensor_tensor(cum[:, :, :], cum[:, :, :], wk[:, :, :], ALU.mult))
            chain(dve.tensor_scalar(cum[:, :, :], cum[:, :, :], -1.0, None, ALU.add))
            dve.scalar_tensor_tensor(wk[:, :, :], wk[:, :, :], 0.5, sT[:, :, :], ALU.mult, ALU.mult).then_inc(s_g, 1)
            dve.wait_ge(s_back, 1)
            for rows, out in ((ps, gates), (ps_c, T["slots"])):
                v = out[:, :, :].rearrange("p (b c) e -> p b c e", c=CH)
                for g in range(NG):
                    for c in range(CH):
                        dve.tensor_copy(v[:, g * GB:(g + 1) * GB, c, :],
                                        rows[:, g, c * P:(c + 1) * P].rearrange("p (b e) -> p b e", e=E))


def experts(nc, tag, T, weights):
    x, gates, xh, xl, ident = T["x"], T["gates"], T["xh"], T["xl"], T["ident"]
    NE = len(weights)
    PEEL = 4
    with ExitStack() as ctx:
        n = Names(nc, ctx, tag)
        raw = n.sb("raw", [P, 2, F])
        wh, wl = ([n.sb(f"{k}{b}", [P, 2, F], F32R) for b in range(2)] for k in ("wh", "wl"))
        h = n.sb("h", [P, FC, UW])
        hh, hl = ([n.sb(f"{k}{b}", [P, FC, UW], F32R) for b in range(2)] for k in ("hh", "hl"))
        yT = n.sb("yT", [P, 2, UW])
        ps_h = n.ps("ps_h", [P, FC, UW])
        ps_y = n.ps("ps_y", [P, 2, UW])
        ps_z = n.ps("ps_z", [P, UT, D])
        s_raw, s_wh, s_wl = n.sem("weights_in"), n.sem("weights_hi"), n.sem("weights_lo")
        s_up = [n.sem(f"up_done{k}") for k in range(2)]
        s_gelu = [n.sem(f"gelu_done{k}") for k in range(2)]
        s_hi = [n.sem(f"h_hi{k}") for k in range(2)]
        s_lo = [n.sem(f"h_lo{k}") for k in range(2)]
        s_y, s_yT, s_z, s_add = n.sem("y_done"), n.sem("y_stored"), n.sem("y_turned"), n.sem("y_added")
        block = ctx.enter_context(nc.Block())

        def units(eng, step, split=None):
            for e in range(NE):
                for i in range(PEEL):
                    step((e, i), i % 2)
                if split and e + 1 < NE:
                    split(e + 1)
                with eng.Fori(PEEL // 2, UNITS // 2) as j:
                    for b in range(2):
                        step((e, j * 2 + b), b)
            for i in range(PEEL):
                step((NE, i), i % 2)

        def back(pos, k):
            e, i = pos
            if not isinstance(i, int):
                return e, i - k
            m = e * UNITS + i - k
            return (m // UNITS, m % UNITS) if 0 <= m < NE * UNITS else None

        def count(pos):
            return pos[0] * UNITS + pos[1]

        def wait(eng, sem, value):
            if not isinstance(value, int) or value > 0:
                eng.wait_ge(sem, value)

        @block.sync
        def _(sp):
            for e in range(NE):
                if e:
                    sp.wait_ge(s_wl, e)
                for k in range(2):
                    sp.dma_start(raw[:, k, :].rearrange("p (c d) -> p c d", c=FC) if k else raw[:, k, :], weights[e][k])\
                      .then_inc(s_raw, 16)

        @block.gpsimd
        def _(pool):
            for e in range(NE):
                pool.wait_ge(s_wh, e + 1)
                pool.tensor_tensor(wl[e % 2][:, :, :], raw[:, :, :], wh[e % 2][:, :, :].bitcast(F32), ALU.subtract).then_inc(s_wl, 1)

        @block.tensor
        def _(pe):
            def three(out, w, cols, moving, first, last):
                (wa, wb), (ma, mb) = w, moving
                pe.matmul(out, wa[cols], ma, start=first, stop=False)
                pe.matmul(out, wb[cols], ma, start=False, stop=False)
                return pe.matmul(out, wa[cols], mb, start=False, stop=last)

            def step(pos, b):
                up, down, turn = back(pos, 0), back(pos, 2), back(pos, 3)
                if up:
                    e, i = up
                    if isinstance(i, int) and i == 0:
                        pe.wait_ge(s_wl, e + 1)
                    cols = bass.ds(i * UW, UW)
                    for half in range(2):
                        wait(pe, s_gelu[half], count(up))
                        for c in range(2 * half, 2 * half + 2):
                            ins = three(ps_h[:, c, :], (wh[e % 2], wl[e % 2]), (slice(None), 0, slice(c * P, (c + 1) * P)),
                                        (xh[:, cols], xl[:, cols]), True, True)
                        ins.then_inc(s_up[half], 1)
                if down:
                    for half in range(2):
                        wait(pe, s_lo[half], count(down) + 1)
                    wait(pe, s_yT, count(down) - 1)
                    for c in range(FC):
                        w = (slice(None), 1, slice(c * D, (c + 1) * D))
                        ins = three(ps_y[:, b, :], (wh[down[0] % 2], wl[down[0] % 2]), w, (hh[b][:, c, :], hl[b][:, c, :]),
                                    c == 0, c == FC - 1)
                    ins.then_inc(s_y, 1)
                if turn:
                    wait(pe, s_yT, count(turn) + 1)
                    wait(pe, s_add, count(turn))
                    for t in range(UT):
                        ins = pe.transpose(ps_z[:, t, :], yT[:, 1 - b, t * P:(t + 1) * P], ident[:, :])
                    ins.then_inc(s_z, 1)

            units(pe, step)

        @block.scalar
        def _(act):
            def split(e):
                act.wait_ge(s_raw, 32 * (e + 1))
                if e >= 2:
                    act.wait_ge(s_y, (e - 1) * UNITS)
                act.activation(wh[e % 2][:, :, :], raw[:, :, :], ACT.Copy).then_inc(s_wh, 1)

            def step(pos, b):
                up, store = back(pos, 0), back(pos, 3)
                if store:
                    wait(act, s_y, count(store) + 1)
                    wait(act, s_z, count(store) - 1)
                    act.activation(yT[:, 1 - b, :], ps_y[:, 1 - b, :], ACT.Copy).then_inc(s_yT, 1)
                if up:
                    for half in range(2):
                        cs = slice(2 * half, 2 * half + 2)
                        wait(act, s_up[half], count(up) + 1)
                        wait(act, s_lo[half], count(up))
                        act.activation(h[:, cs, :], ps_h[:, cs, :], ACT.Gelu).then_inc(s_gelu[half], 1)
                        if half == 0:
                            wait(act, s_gelu[0], count(up) + 1)
                            wait(act, s_y, count(up) - 1)
                            act.activation(hh[b][:, cs, :], h[:, cs, :], ACT.Copy).then_inc(s_hi[0], 1)

            split(0)
            units(act, step, split)

        @block.vector
        def _(dve):
            def step(pos, b):
                up, add = back(pos, 0), back(pos, 4)
                if add:
                    wait(dve, s_z, count(add) + 1)
                    wait(dve, s_add, count(add))
                    for t in range(UT):
                        tile = bass.ds(add[1] * UT + t, 1)
                        gate = gates[:, tile, add[0]] if add[0] < E else 0.5
                        ins = dve.scalar_tensor_tensor(x[:, tile, :], ps_z[:, t, :].unsqueeze(1), gate, x[:, tile, :],
                                                       ALU.mult, ALU.add)
                    ins.then_inc(s_add, 1)
                if up:
                    for half in range(2):
                        cs = slice(2 * half, 2 * half + 2)
                        if half == 1:
                            wait(dve, s_gelu[1], count(up) + 1)
                            wait(dve, s_y, count(up) - 1)
                            dve.tensor_copy(hh[b][:, cs, :], h[:, cs, :]).then_inc(s_hi[1], 1)
                        wait(dve, s_hi[half], count(up) + 1)
                        dve.tensor_tensor(hl[b][:, cs, :], h[:, cs, :], hh[b][:, cs, :].bitcast(F32), ALU.subtract)\
                           .then_inc(s_lo[half], 1)

            units(dve, step)


def attention(nc, tag, T, W, dist, result, residual):
    x, mean, rstd, ident, cols = T["x"], T["mean"], T["rstd"], T["ident"], T["cols"]
    LEAD, LAST = 3, 14
    DVE_ROWS = 2
    with ExitStack() as ctx:
        n = Names(nc, ctx, tag)
        xn = n.sb("xn", [P, CH, D])
        xT = n.sb("xT", [P, SEQ])
        rq, rk, tk = (n.sb(k, [P, G, SEQ]) for k in ("rq", "rk", "tk"))
        qs = n.sb("qs", [P, G, SEQ], F32R)
        qm = [n.sb(f"qm{b}", [P, G, SEQ], F32R) for b in range(2)]
        km = [n.sb(f"km{b}", [P, G, HG, SEQ], F32R) for b in range(2)]
        va = [n.sb(f"va{b}", [P, CH, HEADS, HW]) for b in range(2)]
        mx = n.sb("mx", [P, HEADS, CH])
        ms = n.sb("ms", [P, CH, HEADS, HW])
        pT = n.sb("pT", [P, 2, CH, SEQ])
        oT = n.sb("oT", [P, G, SEQ])
        rs = n.sb("rs", [P, G * CH * HG])
        on = n.sb("on", [P, CH, HEADS, HD])
        ps_q = n.ps("ps_q", [P, G, SEQ])
        ps_s = n.ps("ps_s", [P, 2, CH, SEQ])
        ps_t = n.ps("ps_t", [P, 2, CH, SEQ])
        ps_o = n.ps("ps_o", [P, 2, 512])
        sem = {k: n.sem(k) for k in (
            "zeroed", "xn", "x_turned", "xT", "proj_q", "proj_k", "proj_v", "r_q", "r_k", "qs", "km", "km_a", "va",
            "scores", "max", "neg", "lo", "max_turned", "qm", "scoresT", "probs", "pv", "oT", "out_turned",
            "recip", "scaled", "stored")}
        block = ctx.enter_context(nc.Block())

        def rounds(eng, body):
            body(-1, 1, True, False)
            body(0, 0, True, True)
            body(1, 1, True, True)
            with eng.Fori(1, BATCH // 2 - 1) as i:
                for b in range(2):
                    body(i * 2 + b, b, True, True)
            body(BATCH - 2, 0, True, True)
            body(BATCH - 1, 1, False, True)

        def dve_back_end(dve, m):
            dve.wait_ge(sem["out_turned"], m + 1)
            o_in = ps_q[:, :, :].rearrange("p g (c h w) -> p g c h w", c=CH, w=HW)
            dve.reciprocal(rs[:, :].rearrange("p (g c h) -> p g c h", g=G, c=CH), o_in[:, :, :, :, HD]).then_inc(sem["recip"], 1)
            dve.wait_ge(sem["recip"], m + 1)
            tiles = bass.ds(m * CH, CH)
            for g in range(G):
                sums = bcast(rs[:, g * CH * HG:(g + 1) * CH * HG], HD).rearrange("p (c h) d -> p c h d", c=CH)
                dst = on[:, :, g * HG:(g + 1) * HG, :]
                if not residual:
                    dst = result[:, tiles, g * HG * HD:(g + 1) * HG * HD].rearrange("p c (h d) -> p c h d", d=HD)
                ins = dve.tensor_tensor(dst, o_in[:, g, :, :, 0:HD], sums, ALU.mult)
            if residual:
                ins.then_inc(sem["scaled"], 1)
                dve.wait_ge(sem["scaled"], m + 1)
                xs = result[:, tiles, :]
                ins = dve.tensor_tensor(xs, xs, on[:, :, :, :].rearrange("p c h d -> p c (h d)"), ALU.add)
            ins.then_inc(sem["stored"], 1)

        def dve_xn(dve, m):
            for c in range(CH):
                t = bass.ds(m * CH + c, 1)
                ins = dve.tensor_scalar(xn[:, c, :], x[:, t, :], mean[:, t], rstd[:, t], ALU.subtract, ALU.mult)
            ins.then_inc(sem["xn"], 1)

        @block.vector
        def _(dve):
            for b in range(2):
                dve.memset(va[b][:, :, :, :], 0.0).then_inc(sem["zeroed"], 1)
            dve.wait_ge(sem["zeroed"], 2)
            for b in range(2):
                dve.memset(va[b][:, :, :, HD:HD + 1], 1.0).then_inc(sem["zeroed"], 1)
            dve.memset(ms[:, :, :, :], 0.0).then_inc(sem["zeroed"], 1)
            for b in range(2):
                dve.memset(km[b][:, :, :, :].bitcast(F32), 0.0).then_inc(sem["zeroed"], 1)
            dve.wait_ge(sem["zeroed"], 7)
            dve_xn(dve, 0)

            def body(r, b, front, back):
                f = r + 1
                if back and not (isinstance(r, int) and r == 0):
                    dve_back_end(dve, r - 1)
                if front:
                    dve.wait_ge(sem["r_k"], f + 1)
                    for h in range(DVE_ROWS):
                        rows = slice(h * HW, (h + 1) * HW)
                        ins = dve.scalar_tensor_tensor(km[1 - b][rows, :, h, :],
                                                       ps_s[rows, :, :, :].rearrange("p a b s -> p (a b) s"),
                                                       cols[rows, 2:3], rk[rows, :, :], ALU.mult, ALU.add)
                    ins.then_inc(sem["km_a"], 1)
                    dve.wait_ge(sem["r_q"], f + 1)
                    dve.scalar_tensor_tensor(qs[:, :, :], ps_q[:, :, :], cols[:, 0:1], rq[:, :, :], ALU.mult, ALU.add)\
                       .then_inc(sem["qs"], 1)
                    dve.wait_ge(sem["proj_v"], f + 1)
                    v_in = ps_o[:, 1, 0:CH * D].rearrange("p (c h d) -> p c h d", c=CH, d=HD)
                    if W["bv"] is None:
                        ins = dve.tensor_copy(va[1 - b][:, :, :, 0:HD], v_in)
                    else:
                        for c in range(CH):
                            ins = dve.tensor_tensor(va[1 - b][:, c, :, 0:HD], v_in[:, c, :, :],
                                                    W["bv"][:, :].rearrange("p (h d) -> p h d", d=HD), ALU.add)
                    ins.then_inc(sem["va"], 1)
                    for u in range(HEADS):
                        head = (u % G) * HG + u // G
                        dve.wait_ge(sem["scores"], f * HEADS + u + 1)
                        ins = dve.tensor_reduce(mx[:, head, :], ps_s[:, u % 2, :, :], AX.X, ALU.max)
                        ins.then_inc(sem["max"], 1)
                    dve.wait_ge(sem["max"], (f + 1) * HEADS)
                    m_in = mx[:, :, :].rearrange("p h c -> p c h")
                    hi = ms[:, :, :, ROW_M]
                    dve.tensor_scalar(hi.bitcast(F32R), m_in, -1.0, None, ALU.mult).then_inc(sem["neg"], 1)
                    dve.wait_ge(sem["neg"], f + 1)
                    dve.scalar_tensor_tensor(ms[:, :, :, ROW_M + 1], m_in, -1.0, hi, ALU.mult, ALU.subtract).then_inc(sem["lo"], 1)
                    if back and not isinstance(r, int) or isinstance(r, int) and f + 1 < BATCH:
                        dve.wait_ge(sem["x_turned"], f + 1)
                        dve_xn(dve, f + 1)
                    dve.wait_ge(sem["max_turned"], f + 1)
                    dve.tensor_tensor(qm[1 - b][:, :, :], ps_q[:, :, :], qs[:, :, :].bitcast(F32), ALU.add).then_inc(sem["qm"], 1)

            rounds(dve, body)
            dve_back_end(dve, BATCH - 1)

        @block.gpsimd
        def _(pool):
            pool.wait_ge(sem["zeroed"], 7)

            def body(r, b, front, back):
                if front:
                    f = r + 1
                    pool.wait_ge(sem["r_k"], f + 1)
                    if back:
                        pool.wait_ge(sem["scoresT"], r * HEADS + 1)
                    for h in range(DVE_ROWS, HG):
                        rows = slice(h * HW, (h + 1) * HW)
                        ins = pool.tensor_tensor(km[1 - b][rows, :, h, :], tk[rows, :, :], rk[rows, :, :], ALU.add)
                    ins.then_inc(sem["km"], 1)

            rounds(pool, body)

        @block.tensor
        def _(pe):
            def turn_output(m):
                pe.wait_ge(sem["oT"], (m + 1) * G)
                for g in range(G):
                    for c in range(CH):
                        ins = pe.transpose(ps_q[:, g, c * P:(c + 1) * P], oT[:, g, c * P:(c + 1) * P], ident[:, :])
                ins.then_inc(sem["out_turned"], 1)

            def own_chunk_distance(ps, u, c, side):
                for part in range(2):
                    ins = pe.matmul(ps[:, u % 2, c, c * P:(c + 1) * P], dist["eye"][:, part, :], dist["tab"][:, side, :],
                                    start=False, stop=part == 1)
                return ins

            def body(r, b, front, back):
                f = r + 1

                def scores(u):
                    h, g = divmod(u, G)
                    if u == 0:
                        pe.wait_ge(sem["qs"], f + 1)
                        pe.wait_ge(sem["km_a"], f + 1)
                        pe.wait_ge(sem["va"], f + 1)
                    if h == DVE_ROWS and g == 0:
                        pe.wait_ge(sem["km"], f + 1)
                    if u >= 2:
                        pe.wait_ge(sem["max"], f * HEADS + u - 1)
                    for c in range(CH):
                        ins = pe.matmul(ps_s[:, u % 2, c, :], qs[:, g, c * P:(c + 1) * P], km[1 - b][:, g, h, :],
                                        start=True, stop=dist is None)
                        if dist is not None:
                            ins = own_chunk_distance(ps_s, u, c, 1 - c)
                    ins.then_inc(sem["scores"], 1)

                def scores_turned(u):
                    g, h = divmod(u, HG)
                    if u >= 2:
                        pe.wait_ge(sem["probs"], r * HEADS + u - 1)
                    for c in range(CH):
                        ins = pe.matmul(ps_t[:, u % 2, c, :], km[b][:, g, h, c * P:(c + 1) * P], qm[b][:, g, :],
                                        start=True, stop=dist is None)
                        if dist is not None:
                            ins = own_chunk_distance(ps_t, u, c, c)
                    ins.then_inc(sem["scoresT"], 1)

                def weigh_values(u):
                    g, h = divmod(u, HG)
                    pe.wait_ge(sem["probs"], r * HEADS + u + 1)
                    if h == 0 and g >= 2:
                        pe.wait_ge(sem["oT"], r * G + g - 1)
                    for c in range(CH):
                        ins = pe.matmul(ps_o[h * HW:(h + 1) * HW, g % 2, 0:SEQ], va[b][:, c, u, :], pT[:, u % 2, c, :],
                                        start=c == 0, stop=c == CH - 1)
                    ins.then_inc(sem["pv"], 1)

                if front:
                    pe.wait_ge(sem["xn"], f + 1)
                    for c in range(CH):
                        ins = pe.transpose(ps_o[:, 0, c * P:(c + 1) * P], xn[:, c, :], ident[:, :])
                    ins.then_inc(sem["x_turned"], 1)
                if back:
                    pe.wait_ge(sem["qm"], r + 1)
                    pe.wait_ge(sem["va"], r + 1)
                    scores_turned(0)
                    if not (isinstance(r, int) and r == 0):
                        turn_output(r - 1)
                if front:
                    pe.wait_ge(sem["xT"], f + 1)
                    augmented = W["aug"] is not None

                    def project(dst, k, g):
                        gs = slice(g * P, (g + 1) * P)
                        ins = pe.matmul(dst, W["qk"[k]][:, gs], xT[:, :], start=True, stop=not augmented)
                        if augmented:
                            ins = pe.matmul(dst, W["aug"][:, k, gs], W["rows"][:, :], start=False, stop=True)
                        return ins

                    for g in range(G):
                        ins = project(ps_s[:, g // 2, g % 2, :], 1, g)
                    ins.then_inc(sem["proj_k"], 1)
                    if back:
                        scores_turned(1)
                        pe.wait_ge(sem["stored"], before(r))
                    for g in range(G):
                        ins = project(ps_q[:, g, :], 0, g)
                    ins.then_inc(sem["proj_q"], 1)
                    for c in range(CH):
                        ins = pe.matmul(ps_o[:, 1, c * D:(c + 1) * D], xT[:, c * P:(c + 1) * P], W["v"][:, :], start=True, stop=True)
                    ins.then_inc(sem["proj_v"], 1)
                elif back:
                    scores_turned(1)
                done = 0
                for u in range(2, HEADS + 1):
                    if back:
                        weigh_values(u - 2)
                        if u < HEADS:
                            scores_turned(u)
                        else:
                            weigh_values(u - 1)
                    if front:
                        while back and u >= LEAD and done * (LAST - LEAD + 1) < (u - LEAD + 1) * HEADS and done < HEADS:
                            scores(done)
                            done += 1
                if front:
                    while done < HEADS:
                        scores(done)
                        done += 1
                    pe.wait_ge(sem["lo"], f + 1)
                    for g in range(G):
                        for c in range(CH):
                            ins = pe.transpose(ps_q[:, g, c * P:(c + 1) * P],
                                               ms[:, c, g * HG:(g + 1) * HG, :].rearrange("p h w -> p (h w)"), ident[:, :])
                    ins.then_inc(sem["max_turned"], 1)

            rounds(pe, body)
            pe.wait_ge(sem["stored"], before(BATCH - 1))
            turn_output(BATCH - 1)

        @block.scalar
        def _(act):
            act.sem_inc(sem["stored"], 1)

            def body(r, b, front, back):
                f = r + 1

                def exps(u):
                    act.wait_ge(sem["scoresT"], r * HEADS + u + 1)
                    if u >= 2:
                        act.wait_ge(sem["pv"], r * HEADS + u - 1)
                    act.activation(pT[:, u % 2, :, :], ps_t[:, u % 2, :, :], ACT.Exp, scale=SM_SCALE).then_inc(sem["probs"], 1)
                    g, h = divmod(u, HG)
                    if h == 2 and g:
                        output(g - 1)

                def output(g):
                    act.wait_ge(sem["pv"], r * HEADS + (g + 1) * HG)
                    act.activation(oT[:, g, :], ps_o[:, g % 2, 0:SEQ], ACT.Copy).then_inc(sem["oT"], 1)

                if front:
                    act.wait_ge(sem["x_turned"], f + 1)
                    act.activation(xT[:, :], ps_o[:, 0, 0:SEQ], ACT.Copy).then_inc(sem["xT"], 1)
                if back:
                    exps(0)
                if front:
                    act.wait_ge(sem["proj_k"], f + 1)
                    if back:
                        act.wait_ge(sem["km"], f)
                    k_in = ps_s[:, :, :, :].rearrange("p a b s -> p (a b) s")
                    act.activation(rk[:, :, :].bitcast(F32R), k_in, ACT.Identity, bias=cols[:, 5:6], scale=cols[:, 3:4])
                    act.activation(tk[:, :, :], k_in, ACT.Copy, scale=cols[:, 2:3]).then_inc(sem["r_k"], 1)
                if back:
                    exps(1)
                if front:
                    act.wait_ge(sem["proj_q"], f + 1)
                    if back:
                        act.wait_ge(sem["qs"], f)
                    act.activation(rq[:, :, :].bitcast(F32R), ps_q[:, :, :], ACT.Identity, bias=cols[:, 4:5], scale=cols[:, 1:2])\
                       .then_inc(sem["r_q"], 1)
                if back:
                    for u in range(2, HEADS):
                        exps(u)
                    output(G - 1)

            rounds(act, body)


def attention_weights(nc, tag, parts, bias, dist, T):
    with ExitStack() as ctx:
        n = Names(nc, ctx, tag)
        neg = n.sb("neg", [P, 3])
        s_c = n.sem("chain")
        block = ctx.enter_context(nc.Block())

        def spread(dve, dst, src):
            d = dst.rearrange("p (h w) -> p h w", w=HW)
            s = src.rearrange("p (h d) -> p h d", d=HD)
            for term in range(3):
                ins = dve.tensor_copy(d[:, :, term * HD:(term + 1) * HD], s)
            return ins

        @block.vector
        def _(dve):
            chain = Chain(dve, s_c)
            for dst, _ in parts:
                chain(dve.memset(dst, 0.0))
            for dst, src in parts:
                spread(dve, dst, src)
            if bias is None:
                return
            raw, S = bias
            chain(dve.memset(raw["one"][:, :], 1.0))
            chain(dve.tensor_copy(raw["hi"][:, :, :].bitcast(F32R), raw["b"][:, :, :]))
            chain(dve.tensor_tensor(raw["b"][:, :, :], raw["b"][:, :, :], raw["hi"][:, :, :], ALU.subtract))
            for k in range(2):
                spread(dve, raw["aug"][0:1, k, :], raw["hi"][0:1, k, :])
                chain(spread(dve, raw["aug"][HW:HW + 1, k, :], raw["b"][HW:HW + 1, k, :]))
            chain(dve.tensor_scalar(neg[:, 0:1], dist["scale"][:, 0:1], -1.0, None, ALU.mult))
            chain(dve.tensor_copy(neg[:, 1:2].bitcast(F32R), neg[:, 0:1]))
            chain(dve.tensor_tensor(neg[:, 2:3], neg[:, 0:1], neg[:, 1:2], ALU.subtract))
            for part in range(2):
                q_row, k_row = slice(part * HW, part * HW + 1), slice(2 * HW, 2 * HW + 1)
                heads = raw["aug"][:, :, :].rearrange("p s (h w) -> p s h w", w=HW)
                q_dst = heads[q_row, 0, :, ROW_DIST + 2 + part]
                chain(dve.tensor_scalar(q_dst, raw["one"][q_row, :], neg[q_row, 1 + part:2 + part], -1.0, ALU.mult, ALU.mult))
                k_dst = heads[k_row, 1, :, ROW_DIST + part]
                chain(dve.tensor_scalar(k_dst, raw["one"][k_row, :], neg[k_row, 1 + part:2 + part], None, ALU.mult))
                dve.tensor_scalar(dist["eye"][:, part, :], T["ident"][:, :], neg[:, 1 + part:2 + part], 2.0, ALU.mult, ALU.mult)
            dve.tensor_copy(S["aug"][:, :, :], raw["aug"][:, :, :])
            dve.tensor_copy(S["rows"][:, :], raw["rows"][:, :])
            dve.tensor_copy(dist["tab"][:, :, :], dist["raw"][:, :, :])


def project_and_mlp(nc, tag, T, a_all, W):
    x, mean, rstd, ident = T["x"], T["mean"], T["rstd"], T["ident"]
    with ExitStack() as ctx:
        n = Names(nc, ctx, tag)
        a = n.sb("a", [P, UT, D])
        r0, r1 = n.sb("r0", [P, UT, D]), n.sb("r1", [P, UT, D])
        r2, r3 = n.sb("r2", [P, UT, D]), n.sb("r3", [P, UT, D])
        aT, x1T = n.sb("aT", [P, UW]), n.sb("x1T", [P, UW])
        hT = n.sb("hT", [P, FC, UW])
        st, mv = n.sb("st", [P, UT, 6]), n.sb("mv", [P, UT, 3])
        rs = n.sb("rs", [P, UT])
        ps_t, ps_h, ps_y = n.ps("ps_t", [P, UW]), n.ps("ps_h", [P, FC, UW]), n.ps("ps_y", [P, UT, D])
        sem = {k: n.sem(k) for k in ("a", "a_turned", "aT", "proj", "var", "pow", "x1", "x1_turned", "x1T", "up", "h", "y", "own")}
        block = ctx.enter_context(nc.Block())

        def wide(v):
            return v[:, :].unsqueeze(1).to_broadcast([P, UT, D])

        OWN = 18

        @block.gpsimd
        def _(pool):
            with pool.Fori(0, UNITS) as i:
                pool.tensor_copy(a[:, :, :], a_all[:, bass.ds(i * UT, UT), :]).then_inc(sem["a"], 1)
                for k in range(2):
                    pool.wait_ge(sem["var"], 2 * i + k + 1)
                    pool.tensor_tensor(rs[:, :], mv[:, :, 1], T["neg_half"][:, 0:UT], ALU.pow).then_inc(sem["pow"], 1)

        @block.tensor
        def _(pe):
            def turn(src, done):
                for k in range(UT):
                    ins = pe.transpose(ps_t[:, k * P:(k + 1) * P], src[:, k, :], ident[:, :])
                ins.then_inc(done, 1)

            with pe.Fori(0, UNITS) as i:
                pe.wait_ge(sem["a"], i + 1)
                turn(a, sem["a_turned"])
                pe.wait_ge(sem["aT"], i + 1)
                for k in range(UT):
                    ins = pe.matmul(ps_y[:, k, :], aT[:, k * P:(k + 1) * P], W["o"][:, :], start=True, stop=True)
                ins.then_inc(sem["proj"], 1)
                pe.wait_ge(sem["x1"], i + 1)
                turn(r1, sem["x1_turned"])
                pe.wait_ge(sem["x1T"], i + 1)
                for c in range(FC):
                    pe.matmul(ps_h[:, c, :], W["up"][:, c * P:(c + 1) * P], x1T[:, :], start=True, stop=True)\
                      .then_inc(sem["up"], 1)
                pe.wait_ge(sem["h"], (i + 1) * FC)
                for k in range(UT):
                    for c in range(FC):
                        ins = pe.matmul(ps_y[:, k, :], hT[:, c, k * P:(k + 1) * P], W["down"][:, c, :],
                                        start=c == 0, stop=c == FC - 1)
                ins.then_inc(sem["y"], 1)

        @block.scalar
        def _(act):
            with act.Fori(0, UNITS) as i:
                act.wait_ge(sem["a_turned"], i + 1)
                act.activation(aT[:, :], ps_t[:, :], ACT.Copy).then_inc(sem["aT"], 1)
                act.wait_ge(sem["x1_turned"], i + 1)
                act.activation(x1T[:, :], ps_t[:, :], ACT.Copy).then_inc(sem["x1T"], 1)
                for c in range(FC):
                    act.wait_ge(sem["up"], i * FC + c + 1)
                    act.activation(hT[:, c, :], ps_h[:, c, :], ACT.Relu, bias=W["b1"][:, c:c + 1]).then_inc(sem["h"], 1)

        @block.vector
        def _(dve):
            with dve.Fori(0, UNITS) as i:
                steps = [0]

                def step(ins):
                    steps[0] += 1
                    ins.then_inc(sem["own"], 1)
                    dve.wait_ge(sem["own"], i * OWN + steps[0])

                def norm(src, dst, k):
                    for t in range(UT):
                        ins = dve.bn_stats(st[:, t, :], src[:, t, :])
                    step(ins)
                    dve.tensor_tensor(mv[:, :, 0], st[:, :, 1], st[:, :, 4], ALU.add)
                    dve.tensor_tensor(mv[:, :, 2], st[:, :, 1], st[:, :, 4], ALU.subtract)
                    step(dve.tensor_tensor(mv[:, :, 1], st[:, :, 2], st[:, :, 5], ALU.add))
                    dve.tensor_scalar(mv[:, :, 0], mv[:, :, 0], 0.5, None, ALU.mult)
                    dve.scalar_tensor_tensor(mv[:, :, 2], mv[:, :, 2], 0.25, mv[:, :, 2], ALU.mult, ALU.mult)
                    step(dve.tensor_scalar(mv[:, :, 1], mv[:, :, 1], 1.0 / D, EPS, ALU.mult, ALU.add))
                    dve.tensor_tensor(mv[:, :, 1], mv[:, :, 1], mv[:, :, 2], ALU.add).then_inc(sem["var"], 1)
                    dve.wait_ge(sem["pow"], 2 * i + k + 1)
                    for t in range(UT):
                        ins = dve.tensor_scalar(dst[:, t, :], src[:, t, :], mv[:, t, 0:1], rs[:, t:t + 1],
                                                ALU.subtract, ALU.mult)
                    step(ins)

                for t in range(UT):
                    tile = bass.ds(i * UT + t, 1)
                    ins = dve.tensor_scalar(r0[:, t, :], x[:, tile, :], mean[:, tile], rstd[:, tile], ALU.subtract, ALU.mult)
                step(ins)
                step(dve.tensor_tensor(r0[:, :, :], r0[:, :, :], wide(W["bo"]), ALU.add))
                dve.wait_ge(sem["proj"], i + 1)
                step(dve.tensor_tensor(r2[:, :, :], ps_y[:, :, :], r0[:, :, :], ALU.add))
                norm(r2, r3, 0)
                step(dve.tensor_tensor(r3[:, :, :], r3[:, :, :], wide(W["g1"]), ALU.mult))
                step(dve.tensor_tensor(r1[:, :, :], r3[:, :, :], wide(W["be1"]), ALU.add))
                dve.sem_inc(sem["x1"], 1)
                step(dve.tensor_tensor(r2[:, :, :], r1[:, :, :], wide(W["b2"]), ALU.add))
                dve.wait_ge(sem["y"], i + 1)
                step(dve.tensor_tensor(r3[:, :, :], ps_y[:, :, :], r2[:, :, :], ALU.add))
                norm(r3, r2, 1)
                step(dve.tensor_tensor(r2[:, :, :], r2[:, :, :], wide(W["g2"]), ALU.mult))
                step(dve.tensor_tensor(r2[:, :, :], r2[:, :, :], wide(W["be2"]), ALU.add))
                xs = x[:, bass.ds(i * UT, UT), :]
                step(dve.tensor_tensor(xs, xs, r2[:, :, :], ALU.add))
                assert steps[0] == OWN, steps[0]



def gather_chosen(nc, tag, T, slots, chosen, iota):
    x, mean, rstd = T["x"], T["mean"], T["rstd"]
    EB = E // 2
    with ExitStack() as ctx:
        n = Names(nc, ctx, tag)
        xn = n.sb("xn", [P, 2, CH, D])
        hi, lo = n.sb("hi", [P, 2, CH, D], F32R), n.sb("lo", [P, 2, CH, D], F32R)
        at = n.sb("at", [P, 2, CH, E, CAP], F32R)
        ps = n.ps("ps", [P, 2, 2, 512])
        s_xn = [n.sem(f"xn_ready{b}") for b in range(2)]
        s_hi = [n.sem(f"hi_ready{b}") for b in range(2)]
        s_op = [n.sem(f"operands_ready{b}") for b in range(2)]
        s_mm = [n.sem(f"gathered{b}") for b in range(2)]
        s_st = [n.sem(f"stored{b}") for b in range(2)]
        block = ctx.enter_context(nc.Block())

        @block.vector
        def _(dve):
            prime(dve, *s_xn, *s_op)
            with dve.Fori(0, BATCH // 2) as i:
                for b in range(2):
                    m = i * 2 + b
                    dve.wait_ge(s_mm[b], before(i))
                    for c in range(CH):
                        t = bass.ds(m * CH + c, 1)
                        ins = dve.tensor_scalar(xn[:, b, c, :], x[:, t, :], mean[:, t], rstd[:, t], ALU.subtract, ALU.mult)
                    ins.then_inc(s_xn[b], 1)
                    for c in range(CH):
                        place = slots[:, bass.ds(m * CH + c, 1), :].rearrange("p o e -> p (o e)")
                        dve.tensor_tensor(at[:, b, c, :, :], iota[:, :].unsqueeze(1).to_broadcast([P, E, CAP]),
                                          bcast(place, CAP), ALU.is_equal)
                    dve.wait_ge(s_hi[b], after(i))
                    dve.tensor_tensor(lo[:, b, :, :], xn[:, b, :, :], hi[:, b, :, :].bitcast(F32), ALU.subtract)\
                       .then_inc(s_op[b], 1)

        @block.scalar
        def _(act):
            prime(act, *s_hi, *s_st)
            with act.Fori(0, BATCH // 2) as i:
                for b in range(2):
                    act.wait_ge(s_xn[b], after(i))
                    act.activation(hi[:, b, :, :], xn[:, b, :, :], ACT.Copy).then_inc(s_hi[b], 1)
                for b in range(2):
                    act.wait_ge(s_mm[b], after(i))
                    dst = chosen[:, :, bass.ds(i * 2 + b, 1), :].rearrange("p (k e) o s -> p k e (o s)", k=2)
                    for k in range(2):
                        src = ps[:, b, k, 0:EB * CAP].rearrange("p (e s) -> p e s", e=EB)
                        ins = act.activation(dst[:, k, :, :], src, ACT.Copy)
                    ins.then_inc(s_st[b], 1)

        @block.tensor
        def _(pe):
            prime(pe, *s_mm)
            with pe.Fori(0, BATCH // 2) as i:
                for b in range(2):
                    pe.wait_ge(s_op[b], after(i))
                    pe.wait_ge(s_st[b], before(i))
                    for k in range(2):
                        for j, part in enumerate((hi, lo)):
                            for c in range(CH):
                                ins = pe.matmul(ps[:, b, k, 0:EB * CAP], part[:, b, c, :],
                                                at[:, b, c, k * EB:(k + 1) * EB, :].rearrange("p e s -> p (e s)"),
                                                start=j == 0 and c == 0, stop=j == 1 and c == CH - 1)
                    ins.then_inc(s_mm[b], 1)


def chosen_experts(nc, tag, chosen, W):
    N = BATCH * CAP
    STEPS = 5
    NW = N // STEPS
    assert NW * STEPS == N and NW <= 512
    with ExitStack() as ctx:
        n = Names(nc, ctx, tag)
        hT = n.sb("hT", [P, 2, FC, NW])
        ps_h = n.ps("ps_h", [P, FC, 512])
        ps_y = n.ps("ps_y", [P, 2, 512])
        s_up = [n.sem(f"up_done{h}") for h in range(2)]
        s_gelu = [n.sem(f"gelu_done{h}") for h in range(2)]
        s_y = [n.sem(f"y_ready{b}") for b in range(2)]
        s_st = [n.sem(f"y_stored{b}") for b in range(2)]
        flat = chosen[:, :, :, :].rearrange("p e b s -> p e (b s)")
        block = ctx.enter_context(nc.Block())
        EP = E // 2

        @block.tensor
        def _(pe):
            prime(pe, *s_up, *s_y)
            with pe.Fori(0, STEPS) as i:
                cols = bass.ds(i * NW, NW)

                def up_half(e, half):
                    pe.wait_ge(s_gelu[half], before(i * E + e))
                    for c in range(2 * half, 2 * half + 2):
                        ins = pe.matmul(ps_h[:, c, 0:NW], W["up"][:, e, c * P:(c + 1) * P], flat[:, e, cols], start=True, stop=True)
                    ins.then_inc(s_up[half], 1)

                def down_all(e):
                    b = e % 2
                    for half in range(2):
                        pe.wait_ge(s_gelu[half], after(i * E + e))
                    pe.wait_ge(s_st[b], before(i * EP + e // 2))
                    for c in range(FC):
                        ins = pe.matmul(ps_y[:, b, 0:NW], W["down"][:, e, c, :], hT[:, b, c, :], start=c == 0, stop=c == FC - 1)
                    ins.then_inc(s_y[b], 1)

                for e in range(E):
                    up_half(e, 0)
                    up_half(e, 1)
                    if e:
                        down_all(e - 1)
                down_all(E - 1)

        @block.scalar
        def _(act):
            prime(act, *s_gelu)
            with act.Fori(0, STEPS) as i:
                for e in range(E):
                    b = e % 2
                    act.wait_ge(s_y[b], before(i * EP + e // 2))
                    for half in range(2):
                        act.wait_ge(s_up[half], after(i * E + e))
                        for c in range(2 * half, 2 * half + 2):
                            ins = act.activation(hT[:, b, c, :], ps_h[:, c, 0:NW], ACT.Gelu, bias=W["b1"][:, e, c:c + 1])
                        ins.then_inc(s_gelu[half], 1)

        @block.vector
        def _(dve):
            prime(dve, *s_st)
            with dve.Fori(0, STEPS) as i:
                for e in range(E):
                    b = e % 2
                    dve.wait_ge(s_y[b], after(i * EP + e // 2))
                    dve.tensor_scalar(flat[:, e, bass.ds(i * NW, NW)], ps_y[:, b, 0:NW], W["b2"][:, e:e + 1], None, ALU.add)\
                       .then_inc(s_st[b], 1)


def scatter_chosen(nc, tag, T, slots, chosen, iota):
    x, gates, ident = T["x"], T["gates"], T["ident"]
    N = E * CAP
    KC = 5
    KW = N // KC
    assert KW * KC == N and KW <= P
    with ExitStack() as ctx:
        n = Names(nc, ctx, tag)
        at = n.sb("at", [P, 2, CH, E, CAP])
        og = n.sb("og", [P, 2, CH, E, CAP])
        yT = n.sb("yT", [P, 2, E, CAP])
        ogT = n.sb("ogT", [KW, 2, KC, SEQ])
        y = n.sb("y", [KW, 2, KC, D])
        ps_g = n.ps("ps_g", [P, 3, 512])
        ps_y = n.ps("ps_y", [P, 2, 512])
        ps_o = n.ps("ps_o", [P, 2, 512])
        s_yT = [n.sem(f"yT_ready{b}") for b in range(2)]
        s_at = n.sem("places_ready")
        s_og = [n.sem(f"gates_ready{b}") for b in range(2)]
        s_tg = [n.sem(f"gates_turned{b}") for b in range(2)]
        s_ty = [n.sem(f"y_turned{b}") for b in range(2)]
        s_gs, s_ys = ([n.sem(f"{k}{b}") for b in range(2)] for k in ("gates_stored", "y_stored"))
        s_o = [n.sem(f"out_ready{b}") for b in range(2)]
        s_add = [n.sem(f"added{b}") for b in range(2)]
        block = ctx.enter_context(nc.Block())

        @block.gpsimd
        def _(pool):
            prime(pool, *s_yT)
            with pool.Fori(0, BATCH // 2) as i:
                for b in range(2):
                    pool.wait_ge(s_ty[b], before(i))
                    pool.tensor_copy(yT[:, b, :, :], chosen[:, :, bass.ds(i * 2 + b, 1), :].rearrange("p e o s -> p e (o s)"))\
                        .then_inc(s_yT[b], 1)

        @block.vector
        def _(dve):
            prime(dve, *s_og, *s_add)

            def add(i, b):
                dve.wait_ge(s_o[b], after(i))
                xs = x[:, bass.ds((i * 2 + b) * CH, CH), :]
                dve.tensor_tensor(xs, ps_o[:, b, 0:CH * D].rearrange("p (c d) -> p c d", c=CH), xs, ALU.add).then_inc(s_add[b], 1)

            with dve.Fori(0, BATCH // 2) as i:
                for b in range(2):
                    m = i * 2 + b
                    dve.wait_ge(s_tg[b], before(i))
                    for c in range(CH):
                        place = slots[:, bass.ds(m * CH + c, 1), :].rearrange("p o e -> p (o e)")
                        ins = dve.tensor_tensor(at[:, b, c, :, :], iota[:, :].unsqueeze(1).to_broadcast([P, E, CAP]),
                                                bcast(place, CAP), ALU.is_equal)
                    ins.then_inc(s_at, 1)
                    dve.wait_ge(s_at, m + 1)
                    for c in range(CH):
                        gate = gates[:, bass.ds(m * CH + c, 1), :].rearrange("p o e -> p (o e)")
                        ins = dve.tensor_tensor(og[:, b, c, :, :], at[:, b, c, :, :], bcast(gate, CAP), ALU.mult)
                    ins.then_inc(s_og[b], 1)
                for b in range(2):
                    add(i, b)

        @block.tensor
        def _(pe):
            prime(pe, *s_tg, *s_ty, *s_o)
            with pe.Fori(0, BATCH // 2) as i:
                for b in range(2):
                    pe.wait_ge(s_og[b], after(i))
                    pe.wait_ge(s_gs[1 - b], after(i) if b else before(i))
                    for c in range(CH):
                        flat = og[:, b, c, :, :].rearrange("p e s -> p (e s)")
                        for k in range(KC):
                            q = k * CH + c
                            ins = pe.transpose(ps_g[0:KW, q // 4, (q % 4) * P:(q % 4 + 1) * P], flat[:, k * KW:(k + 1) * KW], ident[:, :])
                    ins.then_inc(s_tg[b], 1)
                    pe.wait_ge(s_yT[b], after(i))
                    pe.wait_ge(s_ys[1 - b], after(i) if b else before(i))
                    flat = yT[:, b, :, :].rearrange("p e s -> p (e s)")
                    for k in range(KC):
                        ins = pe.transpose(ps_y[0:KW, k // 4, (k % 4) * P:(k % 4 + 1) * P], flat[:, k * KW:(k + 1) * KW], ident[:, :])
                    ins.then_inc(s_ty[b], 1)
                for b in range(2):
                    pe.wait_ge(s_gs[b], after(i))
                    pe.wait_ge(s_ys[b], after(i))
                    pe.wait_ge(s_add[b], before(i))
                    for c in range(CH):
                        for k in range(KC):
                            ins = pe.matmul(ps_o[:, b, c * D:(c + 1) * D], ogT[:, b, k, c * P:(c + 1) * P], y[:, b, k, :],
                                            start=k == 0, stop=k == KC - 1)
                    ins.then_inc(s_o[b], 1)

        @block.scalar
        def _(act):
            prime(act, *s_gs, *s_ys)
            with act.Fori(0, BATCH // 2) as i:
                for b in range(2):
                    act.wait_ge(s_o[b], before(i))
                    act.wait_ge(s_tg[b], after(i))
                    flat = ogT[:, b, :, :].rearrange("p k t -> p (k t)")
                    act.activation(flat, ps_g[0:KW, :, :].rearrange("p a s -> p (a s)")[:, 0:KC * SEQ], ACT.Copy).then_inc(s_gs[b], 1)
                    act.wait_ge(s_ty[b], after(i))
                    flat = y[:, b, :, :].rearrange("p k d -> p (k d)")
                    act.activation(flat, ps_y[0:KW, :, :].rearrange("p a s -> p (a s)")[:, 0:KC * D], ACT.Copy).then_inc(s_ys[b], 1)



def expert_choice_ffn(nc, tag, T, W):
    layernorm_stats(nc, tag + "s", T["x"], T["mean"], T["rstd"], T["neg_half"])
    with ExitStack() as ctx:
        n = Names(nc, ctx, tag)
        T = dict(T, logits=n.sb("logits", [P, TILES, E]), gates=n.sb("gates", [P, TILES, E]), slots=n.sb("slots", [P, TILES, E]))
        normalise_and_route(nc, tag + "r", T, W["router"], xn_residual=False)
        gates_expert_choice(nc, tag + "g", T)
        chosen = n.sb("chosen", [P, E, BATCH, CAP])
        gather_chosen(nc, tag + "i", T, T["slots"], chosen, T["iota"])
        chosen_experts(nc, tag + "e", chosen, W)
        scatter_chosen(nc, tag + "o", T, T["slots"], chosen, T["iota"])


def token_choice_ffn(nc, tag, T, W):
    layernorm_stats(nc, tag + "s", T["x"], T["mean"], T["rstd"], T["neg_half"])
    with ExitStack() as ctx:
        n = Names(nc, ctx, tag)
        T = dict(T, xh=n.sb("xh", [P, TILES * P], F32R), xl=n.sb("xl", [P, TILES * P], F32R), logits=n.sb("logits", [P, TILES, E]), gates=n.sb("gates", [P, TILES, E]))
        normalise_and_route(nc, tag + "r", T, W["router"], xn_residual=True)
        gates_top2(nc, tag + "g", T)
        experts(nc, tag + "e", T, W["experts"])


def program(nc, A, out):
    with ExitStack() as ctx:
        n = Names(nc, ctx, "k")
        T = {"x": n.sb("x", [P, TILES, D]), "mean": n.sb("mean", [P, TILES]), "rstd": n.sb("rstd", [P, TILES]),
             "neg_half": n.sb("neg_half", [P, TILES]), "ident": n.sb("ident", [P, P]), "prio": n.sb("prio", [P, E]),
             "iota": n.sb("iota", [P, CAP]), "cols": n.sb("cols", [P, 16])}
        s_in, s_c, s_out = n.sem("loaded"), n.sem("constants"), n.sem("stored")

        def load(tag, *pairs):
            with ExitStack() as c:
                s_load = Names(nc, c, tag).sem("loaded")
                block = c.enter_context(nc.Block())

                @block.sync
                def _(sp):
                    for dst, src in pairs:
                        sp.dma_start(dst, src).then_inc(s_load, 16)
                    sp.wait_ge(s_load, 16 * len(pairs))

        load("in", (T["x"][:, :, :], A["L0_attn_x"].rearrange("b (c p) d -> p (b c) d", p=P)),
             (T["ident"][:, :], A["c_ident"]), (T["prio"][:, :], A["c_prio"]), (T["cols"][:, :], A["c_cols"]),
             (T["iota"][:, :], A["c_iota"]))
        with nc.Block() as block:
            @block.vector
            def _(dve):
                dve.memset(T["neg_half"][:, :], -0.5).then_inc(s_c, 1)

        def l0_ffn(tag):
            with ExitStack() as c:
                m = Names(nc, c, tag)
                W = {"up": m.sb("up0", [P, E, F]), "down": m.sb("down0", [P, E, FC, D]), "b1": m.sb("b1", [P, E, FC]),
                     "b2": m.sb("b2", [P, E]), "router": m.sb("router0", [P, E])}
                load(tag + "w", (W["router"][:, :], A["L0_router_T"]),
                     (W["up"][:, :, :], A["L0_ffn_w1"].rearrange("e d f -> d e f")),
                     (W["down"][:, :, :, :], A["L0_ffn_w2"].rearrange("e (c f) d -> f e c d", f=P)),
                     (W["b1"][:, :, :], A["L0_b1_T"]), (W["b2"][:, :], A["L0_b2_T"]))
                expert_choice_ffn(nc, tag, T, W)

        def l1_ffn(tag):
            with ExitStack() as c:
                m = Names(nc, c, tag)
                down = "(c f) d -> f c d"
                W = {"router": m.sb("router1", [P, E]), "experts": [
                    (A["L1_ffn_routed_up"][e], A["L1_ffn_routed_down"][e].rearrange(down, f=P)) for e in range(E)] + [
                    (A["L1_ffn_shared_up"][0], A["L1_ffn_shared_down"][0].rearrange(down, f=P))]}
                load(tag + "w", (W["router"][:, :], A["L1_ffn_router_w"]))
                token_choice_ffn(nc, tag, T, W)

        def stacks(m):
            return {"q": m.sb("wq", [P, HEADS * HW]), "k": m.sb("wk", [P, HEADS * HW]), "v": m.sb("wv", [P, D]),
                    "aug": None, "bv": None}

        def l0_attention(tag):
            with ExitStack() as c:
                m = Names(nc, c, tag)
                W = stacks(m)
                raw = m.sb("raw", [P, 2, D])
                qkv = A["L0_qkv_T"]
                load(tag + "w", (raw[:, :, :], qkv[:, 0:2 * D].rearrange("p (k d) -> p k d", k=2)),
                     (W["v"][:, :], qkv[:, 2 * D:3 * D]))
                attention_weights(nc, tag + "p", [(W["q"][:, :], raw[:, 0, :]), (W["k"][:, :], raw[:, 1, :])], None, None, T)
                layernorm_stats(nc, tag + "s", T["x"], T["mean"], T["rstd"], T["neg_half"])
                attention(nc, tag + "c", T, W, None, T["x"], True)

        def l1_attention(tag):
            with ExitStack() as c:
                m = Names(nc, c, tag)
                a_all = m.sb("a_all", [P, TILES, D])
                W = {"o": m.sb("wo", [P, D]), "up": m.sb("w1", [P, F]), "down": m.sb("w2", [P, FC, D]), "b1": m.sb("bf1", [P, FC])}
                for k in ("bo", "g1", "be1", "b2", "g2", "be2", "bv"):
                    W[k] = m.sb(k, [P, D])

                def wide(name):
                    return A[name].unsqueeze(0).to_broadcast([P, D])

                load(tag + "w", (W["o"][:, :], A["L1_attn_Wo"]), (W["up"][:, :], A["L1_attn_W1"]),
                     (W["down"][:, :, :], A["L1_attn_W2"].rearrange("(c f) d -> f c d", f=P)), (W["b1"][:, :], A["L1_W1b_T"]),
                     (W["bo"][:, :], wide("L1_attn_bo")), (W["g1"][:, :], wide("L1_attn_ln1_g")), (W["be1"][:, :], wide("L1_attn_ln1_b")),
                     (W["b2"][:, :], wide("L1_attn_b2")), (W["g2"][:, :], wide("L1_attn_ln2_g")), (W["be2"][:, :], wide("L1_attn_ln2_b")),
                     (W["bv"][:, :], wide("L1_attn_bv")))
                layernorm_stats(nc, tag + "s", T["x"], T["mean"], T["rstd"], T["neg_half"])
                with ExitStack() as c2:
                    m2 = Names(nc, c2, tag + "2")
                    S = stacks(m2)
                    S["bv"] = W["bv"]
                    S["aug"], S["rows"] = m2.sb("aug", [AUG, 2, HEADS * HW], F32R), m2.sb("rows", [AUG, SEQ], F32R)
                    raw = m2.sb("raw", [P, 2, D])
                    bias = {"aug": m2.sb("rawaug", [AUG, 2, HEADS * HW]), "rows": m2.sb("rawrows", [AUG, SEQ]),
                            "b": m2.sb("bqk", [AUG, 2, D]), "hi": m2.sb("bqk_hi", [AUG, 2, D]),
                            "one": m2.sb("one", [AUG, HEADS])}
                    dist = {"scale": m2.sb("scale", [P, 1]), "eye": m2.sb("eye", [P, 2, P], F32R),
                            "tab": m2.sb("tab", [P, 2, P], F32R), "raw": m2.sb("rawtab", [P, 2, P])}
                    load(tag + "2w", (raw[:, 0, :], A["L1_attn_Wq"]), (raw[:, 1, :], A["L1_attn_Wk"]), (S["v"][:, :], A["L1_attn_Wv"]),
                         (bias["aug"][:, :, :], A["c_aug"].rearrange("k (s t) -> k s t", s=2)), (bias["rows"][:, :], A["c_rows"]),
                         (bias["b"][:, 0, :], A["L1_attn_bq"].unsqueeze(0).to_broadcast([AUG, D])),
                         (bias["b"][:, 1, :], A["L1_attn_bk"].unsqueeze(0).to_broadcast([AUG, D])),
                         (dist["scale"][:, :], A["L1_dist_scale"].to_broadcast([P, 1])),
                         (dist["raw"][:, :, :], A["c_dist"].rearrange("p (c t) -> p c t", c=2)))
                    attention_weights(nc, tag + "p", [(S["q"][:, :], raw[:, 0, :]), (S["k"][:, :], raw[:, 1, :])], (bias, S), dist, T)
                    attention(nc, tag + "c", T, S, dist, a_all, False)
                project_and_mlp(nc, tag + "m", T, a_all, W)

        l0_ffn("a")
        l0_attention("b")
        l0_ffn("c")
        l1_ffn("d")
        l1_attention("e")
        l1_ffn("f")

        with nc.Block() as block:
            @block.sync
            def _(sp):
                sp.dma_start(out.rearrange("b (c p) d -> p (b c) d", p=P), T["x"][:, :, :]).then_inc(s_out, 16)
                sp.wait_ge(s_out, 16)


def kernel(**inputs):
    import concourse.bacc as _bacc
    from concourse.bass_utils import run_bass_kernel_spmd as _run

    a = {k: np.ascontiguousarray(v) for k, v in inputs.items()}
    a["L0_router_T"] = np.ascontiguousarray(np.transpose(a.pop("L0_ffn_router_w")))
    b1 = a.pop("L0_ffn_b1")
    a["L0_b1_T"] = np.ascontiguousarray(np.transpose(b1.reshape(E, FC, P), (2, 0, 1)))
    a["L0_b2_T"] = np.ascontiguousarray(np.transpose(a.pop("L0_ffn_b2")))
    a["L0_qkv_T"] = np.ascontiguousarray(np.transpose(a.pop("L0_attn_W_qkv")))
    a["L1_W1b_T"] = np.ascontiguousarray(np.transpose(a.pop("L1_attn_b1").reshape(FC, P)))
    a["L1_dist_scale"] = a.pop("L1_attn_dist_scale").reshape(1, 1)
    a.update(shape_constants())

    nc = _bacc.Bacc("TRN2", target_bir_lowering=False, num_devices=1)
    arrays, aps = {}, {}
    for name, v in a.items():
        arrays[f"in_{name}"] = v
        aps[name] = nc.dram_tensor(f"in_{name}", v.shape, mybir.dt.from_np(v.dtype), kind="ExternalInput").ap()
    out = nc.dram_tensor("out_0", (BATCH, SEQ, D), F32, kind="ExternalOutput").ap()
    program(nc, aps, out)
    r = _run(nc, [arrays], core_ids=[0])
    return r.results[0]["out_0"]
```

```python
from contextlib import ExitStack

import numpy as np

import concourse.bass as bass
from concourse import mybir

F32 = mybir.dt.float32
F32R = mybir.dt.float32r
ALU = mybir.AluOpType
ACT = mybir.ActivationFunctionType
AX = mybir.AxisListType

P = 128
BATCH, SEQ, D = 32, 256, 128
CH = SEQ // P
TILES = BATCH * CH
UT = 4
UNITS = TILES // UT
UW = UT * P
E = 8
F = 512
FC = F // P
CAP = SEQ * 2 // E + 1
HEADS, HD = 16, D // 16
G, HG = 4, 4
HW = P // HG
ROW_M, ROW_MASK, ROW_DIST = 3 * HD, 3 * HD + 2, 3 * HD + 3
EPS = 1e-5
SM_SCALE = float(1.0 / np.sqrt(HD))
MASKED = -1e30
AUG_MASK = 2 * HW + 1
AUG_T, AUG_U = AUG_MASK + HEADS, AUG_MASK + HEADS + 1
AUG = AUG_U + 1


def shape_constants():
    ident = np.eye(P, dtype=np.float32)
    cols = np.zeros((P, 16), np.float32)
    r = np.arange(P) % HW
    term = r // HD
    distance = (r >= ROW_DIST) & (r < ROW_DIST + 4)
    cols[:, 0] = (term == 2) | distance
    cols[:, 1] = np.where(r >= ROW_M, 0, np.where(term == 2, -1, 1))
    cols[:, 2] = (term == 1) | (r == ROW_MASK) | distance
    cols[:, 3] = np.where(r >= ROW_M, 0, np.where(term == 1, -1, 1))
    cols[:, 4] = r == ROW_MASK
    cols[:, 5] = (r == ROW_M) | (r == ROW_M + 1)
    prio = np.broadcast_to(np.arange(E, 0, -1, dtype=np.float32), (P, E))
    t = np.arange(SEQ)
    below = np.maximum(t[:P, None] - t[None, :P], 0).astype(np.float32)
    dist = np.concatenate([below, below.T], axis=1)
    aug = np.zeros((AUG, 2, HEADS, HW), np.float32)
    rows = np.zeros((AUG, SEQ), np.float32)
    sign = np.where(t < P, 1, -1)
    rows[0] = rows[HW] = 1
    rows[2 * HW] = sign
    rows[AUG_T] = t
    rows[AUG_U] = sign * t
    aug[AUG_T, 0, :, ROW_DIST:ROW_DIST + 2] = 1
    aug[AUG_U, 1, :, ROW_DIST + 2:ROW_DIST + 4] = 1
    for h in range(HEADS):
        aug[AUG_MASK + h, 1, h, ROW_MASK] = 1
        rows[AUG_MASK + h, :h] = MASKED
    aug = aug.reshape(AUG, 2 * HEADS * HW)
    return {
        "c_ident": ident, "c_cols": cols, "c_prio": np.ascontiguousarray(prio),
        "c_iota": np.ascontiguousarray(np.broadcast_to(np.arange(CAP, dtype=np.float32), (P, CAP))), "c_dist": np.ascontiguousarray(dist),
        "c_aug": np.ascontiguousarray(aug), "c_rows": np.ascontiguousarray(rows),
    }


class Chain:

    def __init__(self, eng, sem):
        self.eng, self.sem, self.n = eng, sem, 0

    def __call__(self, ins):
        self.n += 1
        ins.then_inc(self.sem, 1)
        self.eng.wait_ge(self.sem, self.n)


def prime(eng, *sems):
    for s in sems:
        eng.sem_inc(s, 1)


def before(n):
    return n + 1


def after(n):
    return n + 2


def bcast(ap, n):
    return ap.unsqueeze(2).to_broadcast([ap.shape[0], ap.shape[1], n])


class Names:

    def __init__(self, nc, ctx, tag):
        self.nc, self.ctx, self.tag, self.sems = nc, ctx, tag, []
        ctx.callback(self.close)

    def sb(self, name, shape, dt=F32):
        return self.ctx.enter_context(self.nc.sbuf_tensor(f"{self.tag}_{name}", shape, dt))

    def ps(self, name, shape, dt=F32):
        return self.ctx.enter_context(self.nc.psum_tensor(f"{self.tag}_{name}", shape, dt))

    def sem(self, name):
        self.sems.append(self.nc.alloc_semaphore(f"{self.tag}_{name}"))
        return self.sems[-1]

    def close(self):
        if self.sems:
            self.nc.clear_and_free_semaphores(self.sems)
            self.nc.all_engine_barrier(sem_only=True)


def layernorm_stats(nc, tag, x, mean, rstd, neg_half):
    with ExitStack() as ctx:
        n = Names(nc, ctx, tag)
        st = n.sb("st", [P, TILES, 6])
        tmp = n.sb("tmp", [P, 2, TILES])
        s_st, s_v, s_p = n.sem("stats"), n.sem("var_ready"), n.sem("pow")
        block = ctx.enter_context(nc.Block())

        @block.vector
        def _(dve):
            chain = Chain(dve, s_v)
            with dve.Fori(0, TILES // 4) as i:
                for k in range(4):
                    dve.bn_stats(st[:, bass.ds(i * 4 + k, 1), :], x[:, bass.ds(i * 4 + k, 1), :]).then_inc(s_st, 1)
            dve.wait_ge(s_st, TILES)
            chain(dve.tensor_tensor(mean[:, :], st[:, :, 1], st[:, :, 4], ALU.add))
            chain(dve.tensor_scalar(mean[:, :], mean[:, :], 0.5, None, ALU.mult))
            chain(dve.tensor_tensor(tmp[:, 0, :], st[:, :, 1], st[:, :, 4], ALU.subtract))
            chain(dve.tensor_tensor(tmp[:, 1, :], st[:, :, 2], st[:, :, 5], ALU.add))
            chain(dve.tensor_tensor(tmp[:, 0, :], tmp[:, 0, :], tmp[:, 0, :], ALU.mult))
            chain(dve.tensor_scalar(tmp[:, 0, :], tmp[:, 0, :], 0.25, EPS, ALU.mult, ALU.add))
            chain(dve.scalar_tensor_tensor(tmp[:, 1, :], tmp[:, 1, :], 1.0 / D, tmp[:, 0, :], ALU.mult, ALU.add))

        @block.gpsimd
        def _(pool):
            pool.wait_ge(s_v, 7)
            pool.tensor_tensor(rstd[:, :], tmp[:, 1, :], neg_half[:, 0:TILES], ALU.pow).then_inc(s_p, 1)


def normalise_and_route(nc, tag, T, router_w, xn_residual):
    x, mean, rstd, ident = T["x"], T["mean"], T["rstd"], T["ident"]
    with ExitStack() as ctx:
        n = Names(nc, ctx, tag)
        xn = n.sb("xn", [P, 2, UT, D])
        xT = n.sb("xT", [P, 2, UW])
        ps_t = n.ps("ps_t", [P, 2, UW])
        ps_l = n.ps("ps_l", [P, 2, 512])
        s_xn = [n.sem(f"xn_ready{b}") for b in range(2)]
        s_res = n.sem("residual_added")
        s_tp = [n.sem(f"transposed{b}") for b in range(2)]
        s_xT = [n.sem(f"xT_ready{b}") for b in range(2)]
        s_all = [n.sem(f"xT_stored{b}") for b in range(2)]
        s_lo = [n.sem(f"xT_lo{b}") for b in range(2)]
        keep = "xh" in T
        s_lg = [n.sem(f"logits_ready{b}") for b in range(2)]
        s_ls = [n.sem(f"logits_stored{b}") for b in range(2)]
        block = ctx.enter_context(nc.Block())

        @block.vector
        def _(dve):
            prime(dve, *s_xn, *s_lo)
            with dve.Fori(0, UNITS // 2) as i:
                for b in range(2):
                    dve.wait_ge(s_tp[b], before(i))
                    for k in range(UT):
                        t = (i * 2 + b) * UT + k
                        ins = dve.tensor_scalar(xn[:, b, k, :], x[:, bass.ds(t, 1), :], mean[:, bass.ds(t, 1)],
                                                rstd[:, bass.ds(t, 1)], ALU.subtract, ALU.mult)
                    ins.then_inc(s_xn[b], 1)
                    if xn_residual:
                        dve.wait_ge(s_xn[b], after(i))
                        xs = x[:, bass.ds((i * 2 + b) * UT, UT), :]
                        dve.scalar_tensor_tensor(xs, xn[:, b, :, :], 0.5, xs, ALU.mult, ALU.add).then_inc(s_res, 1)
                        dve.wait_ge(s_res, i * 2 + b + 1)
                if keep:
                    for b in range(2):
                        cols = bass.ds((i * 2 + b) * UW, UW)
                        dve.wait_ge(s_xT[b], after(i))
                        dve.wait_ge(s_all[b], after(i))
                        dve.tensor_tensor(T["xl"][:, cols], xT[:, b, :], T["xh"][:, cols].bitcast(F32), ALU.subtract)\
                           .then_inc(s_lo[b], 1)

        @block.tensor
        def _(pe):
            prime(pe, *s_tp, *s_lg)
            with pe.Fori(0, UNITS // 2) as i:
                for b in range(2):
                    pe.wait_ge(s_xn[b], after(i))
                    pe.wait_ge(s_all[b] if keep else s_xT[b], before(i))
                    for k in range(UT):
                        ins = pe.transpose(ps_t[:, b, k * P:(k + 1) * P], xn[:, b, k, :], ident[:, :])
                    ins.then_inc(s_tp[b], 1)
                for b in range(2):
                    pe.wait_ge(s_xT[b], after(i))
                    pe.wait_ge(s_ls[b], before(i))
                    for k in range(UT):
                        ins = pe.matmul(ps_l[:, b, k * E:(k + 1) * E], xT[:, b, k * P:(k + 1) * P], router_w[:, :],
                                        start=True, stop=True)
                    ins.then_inc(s_lg[b], 1)

        @block.scalar
        def _(act):
            prime(act, *s_xT, *s_all, *s_ls)
            with act.Fori(0, UNITS // 2) as i:
                for b in range(2):
                    act.wait_ge(s_tp[b], after(i))
                    act.wait_ge(s_lg[b], before(i))
                    if keep:
                        act.wait_ge(s_lo[b], before(i))
                    act.activation(xT[:, b, :], ps_t[:, b, :], ACT.Copy).then_inc(s_xT[b], 1)
                    if keep:
                        act.activation(T["xh"][:, bass.ds((i * 2 + b) * UW, UW)], ps_t[:, b, :], ACT.Copy).then_inc(s_all[b], 1)
                for b in range(2):
                    act.wait_ge(s_lg[b], after(i))
                    act.activation(T["logits"][:, bass.ds((i * 2 + b) * UT, UT), :],
                                   ps_l[:, b, 0:UT * E].rearrange("p (t e) -> p t e", e=E), ACT.Copy).then_inc(s_ls[b], 1)


def softmax_experts(chain, act_sems, nc, T, red):
    s_in, s_out, dve = act_sems
    lg = T["logits"]
    chain(dve.tensor_reduce(red[:, 0, :], lg[:, :, :], AX.X, ALU.max))
    dve.tensor_tensor(lg[:, :, :], lg[:, :, :], bcast(red[:, 0, :], E), ALU.subtract).then_inc(s_in, 1)
    dve.wait_ge(s_out, 1)
    chain(dve.tensor_reduce(red[:, 0, :], lg[:, :, :], AX.X, ALU.add))
    chain(dve.reciprocal(red[:, 1, :], red[:, 0, :]))
    chain(dve.tensor_tensor(lg[:, :, :], lg[:, :, :], bcast(red[:, 1, :], E), ALU.mult))


def gates_top2(nc, tag, T):
    lg, gates, prio = T["logits"], T["gates"], T["prio"]
    with ExitStack() as ctx:
        n = Names(nc, ctx, tag)
        red = n.sb("red", [P, 2, TILES])
        left, key, hot = (n.sb(k, [P, TILES, E]) for k in ("left", "key", "hot"))
        s_c, s_in, s_out = n.sem("chain"), n.sem("shifted"), n.sem("exp_done")
        block = ctx.enter_context(nc.Block())

        @block.scalar
        def _(act):
            act.wait_ge(s_in, 1)
            act.activation(lg[:, :, :], lg[:, :, :], ACT.Exp).then_inc(s_out, 1)

        @block.vector
        def _(dve):
            chain = Chain(dve, s_c)
            softmax_experts(chain, (s_in, s_out, dve), nc, T, red)
            chain(dve.tensor_copy(left[:, :, :], lg[:, :, :]))
            for k in range(2):
                chain(dve.tensor_reduce(red[:, 0, :], left[:, :, :], AX.X, ALU.max))
                chain(dve.tensor_tensor(key[:, :, :], left[:, :, :], bcast(red[:, 0, :], E), ALU.is_equal))
                chain(dve.tensor_tensor(key[:, :, :], key[:, :, :],
                                        prio[:, :].unsqueeze(1).to_broadcast([P, TILES, E]), ALU.mult))
                chain(dve.tensor_reduce(red[:, 1, :], key[:, :, :], AX.X, ALU.max))
                chain(dve.tensor_tensor(hot[:, :, :], key[:, :, :], bcast(red[:, 1, :], E), ALU.is_equal))
                chain(dve.scalar_tensor_tensor(left[:, :, :], hot[:, :, :], -2.0, left[:, :, :], ALU.mult, ALU.add))
            chain(dve.tensor_scalar(key[:, :, :], left[:, :, :], 0.0, 0.5, ALU.is_lt, ALU.mult))
            chain(dve.tensor_tensor(gates[:, :, :], key[:, :, :], lg[:, :, :], ALU.mult))


def gates_expert_choice(nc, tag, T):
    lg, gates, ident = T["logits"], T["gates"], T["ident"]
    by_chunk = gates[:, :, :].rearrange("p (c b) e -> p c b e", c=CH)
    GB = P // E
    NG = BATCH // GB
    with ExitStack() as ctx:
        n = Names(nc, ctx, tag)
        red = n.sb("red", [P, 2, TILES])
        sT, wk, eq, cum, one = (n.sb(k, [P, NG, SEQ]) for k in ("sT", "wk", "eq", "cum", "one"))
        m8 = n.sb("m8", [P, NG, 8])
        cnt = n.sb("cnt", [P, NG, 2])
        ps, ps_c = n.ps("ps", [P, NG, SEQ]), n.ps("ps_c", [P, NG, SEQ])
        s_c, s_in, s_out, s_p, s_tp = (n.sem(k) for k in ("chain", "shifted", "exp_done", "probs", "turned"))
        s_g, s_back = n.sem("gates_rows"), n.sem("turned_back")
        block = ctx.enter_context(nc.Block())

        @block.scalar
        def _(act):
            act.wait_ge(s_in, 1)
            act.activation(lg[:, :, :], lg[:, :, :], ACT.Exp).then_inc(s_out, 1)

        @block.tensor
        def _(pe):
            pe.wait_ge(s_p, 1)
            for g in range(NG):
                for c in range(CH):
                    ins = pe.transpose(ps[:, g, c * P:(c + 1) * P],
                                       by_chunk[:, c, g * GB:(g + 1) * GB, :].rearrange("p b e -> p (b e)"), ident[:, :])
            ins.then_inc(s_tp, 1)
            pe.wait_ge(s_g, 1)
            for g in range(NG):
                for c in range(CH):
                    pe.transpose(ps[:, g, c * P:(c + 1) * P], wk[:, g, c * P:(c + 1) * P], ident[:, :])
                    ins = pe.transpose(ps_c[:, g, c * P:(c + 1) * P], cum[:, g, c * P:(c + 1) * P], ident[:, :])
            ins.then_inc(s_back, 1)

        @block.vector
        def _(dve):
            chain = Chain(dve, s_c)
            softmax_experts(chain, (s_in, s_out, dve), nc, T, red)
            chain(dve.memset(one[:, :, :], 1.0))
            dve.tensor_copy(by_chunk, lg[:, :, :].rearrange("p (b c) e -> p c b e", c=CH)).then_inc(s_p, 1)
            dve.wait_ge(s_tp, 1)
            chain(dve.tensor_copy(sT[:, :, :], ps[:, :, :]))
            chain(dve.tensor_copy(wk[:, :, :], sT[:, :, :]))
            rounds = (CAP - 1) // 8
            for r in range(rounds + 1):
                for g in range(NG):
                    ins = dve.max(m8[:, g, :], wk[:, g, :])
                chain(ins)
                if r < rounds:
                    for g in range(NG):
                        ins = dve.match_replace(wk[:, g, :], m8[:, g, :], wk[:, g, :], -1.0)
                    chain(ins)
            at = (CAP - 1) % 8
            for g in range(NG):
                thr = m8[:, g, at:at + 1]
                chain(dve.tensor_scalar(wk[:, g, :], sT[:, g, :], thr, 0.0, ALU.is_gt, ALU.add, accum_out=cnt[:, g, 0:1]))
                chain(dve.tensor_scalar(eq[:, g, :], sT[:, g, :], thr, None, ALU.is_equal))
                chain(dve.tensor_scalar(cnt[:, g, 1:2], cnt[:, g, 0:1], -1.0, float(CAP), ALU.mult, ALU.add))
                chain(dve.tensor_tensor_scan(cum[:, g, :], one[:, g, :], eq[:, g, :], 0.0, ALU.mult, ALU.add))
                chain(dve.scalar_tensor_tensor(eq[:, g, :], cum[:, g, :], cnt[:, g, 1:2], eq[:, g, :], ALU.is_le, ALU.mult))
                chain(dve.tensor_tensor(wk[:, g, :], wk[:, g, :], eq[:, g, :], ALU.add))
            for g in range(NG):
                ins = dve.tensor_tensor_scan(cum[:, g, :], one[:, g, :], wk[:, g, :], 0.0, ALU.mult, ALU.add)
            chain(ins)
            chain(dve.tensor_tensor(cum[:, :, :], cum[:, :, :], wk[:, :, :], ALU.mult))
            chain(dve.tensor_scalar(cum[:, :, :], cum[:, :, :], -1.0, None, ALU.add))
            dve.scalar_tensor_tensor(wk[:, :, :], wk[:, :, :], 0.5, sT[:, :, :], ALU.mult, ALU.mult).then_inc(s_g, 1)
            dve.wait_ge(s_back, 1)
            for rows, out in ((ps, gates), (ps_c, T["slots"])):
                v = out[:, :, :].rearrange("p (b c) e -> p b c e", c=CH)
                for g in range(NG):
                    for c in range(CH):
                        dve.tensor_copy(v[:, g * GB:(g + 1) * GB, c, :],
                                        rows[:, g, c * P:(c + 1) * P].rearrange("p (b e) -> p b e", e=E))


def experts(nc, tag, T, weights):
    x, gates, xh, xl, ident = T["x"], T["gates"], T["xh"], T["xl"], T["ident"]
    NE = len(weights)
    PEEL = 4
    with ExitStack() as ctx:
        n = Names(nc, ctx, tag)
        raw = n.sb("raw", [P, 2, F])
        wh, wl = ([n.sb(f"{k}{b}", [P, 2, F], F32R) for b in range(2)] for k in ("wh", "wl"))
        h = n.sb("h", [P, FC, UW])
        hh, hl = ([n.sb(f"{k}{b}", [P, FC, UW], F32R) for b in range(2)] for k in ("hh", "hl"))
        yT = n.sb("yT", [P, 2, UW])
        ps_h = n.ps("ps_h", [P, FC, UW])
        ps_y = n.ps("ps_y", [P, 2, UW])
        ps_z = n.ps("ps_z", [P, UT, D])
        s_raw, s_wh, s_wl = n.sem("weights_in"), n.sem("weights_hi"), n.sem("weights_lo")
        s_up = [n.sem(f"up_done{k}") for k in range(2)]
        s_gelu = [n.sem(f"gelu_done{k}") for k in range(2)]
        s_hi = [n.sem(f"h_hi{k}") for k in range(2)]
        s_lo = [n.sem(f"h_lo{k}") for k in range(2)]
        s_y, s_yT, s_z, s_add = n.sem("y_done"), n.sem("y_stored"), n.sem("y_turned"), n.sem("y_added")
        block = ctx.enter_context(nc.Block())

        def units(eng, step, split=None):
            for e in range(NE):
                for i in range(PEEL):
                    step((e, i), i % 2)
                if split and e + 1 < NE:
                    split(e + 1)
                with eng.Fori(PEEL // 2, UNITS // 2) as j:
                    for b in range(2):
                        step((e, j * 2 + b), b)
            for i in range(PEEL):
                step((NE, i), i % 2)

        def back(pos, k):
            e, i = pos
            if not isinstance(i, int):
                return e, i - k
            m = e * UNITS + i - k
            return (m // UNITS, m % UNITS) if 0 <= m < NE * UNITS else None

        def count(pos):
            return pos[0] * UNITS + pos[1]

        def wait(eng, sem, value):
            if not isinstance(value, int) or value > 0:
                eng.wait_ge(sem, value)

        @block.sync
        def _(sp):
            for e in range(NE):
                if e:
                    sp.wait_ge(s_wl, e)
                for k in range(2):
                    sp.dma_start(raw[:, k, :].rearrange("p (c d) -> p c d", c=FC) if k else raw[:, k, :], weights[e][k])\
                      .then_inc(s_raw, 16)

        @block.gpsimd
        def _(pool):
            for e in range(NE):
                pool.wait_ge(s_wh, e + 1)
                pool.tensor_tensor(wl[e % 2][:, :, :], raw[:, :, :], wh[e % 2][:, :, :].bitcast(F32), ALU.subtract).then_inc(s_wl, 1)

        @block.tensor
        def _(pe):
            def three(out, w, cols, moving, first, last):
                (wa, wb), (ma, mb) = w, moving
                pe.matmul(out, wa[cols], ma, start=first, stop=False)
                pe.matmul(out, wb[cols], ma, start=False, stop=False)
                return pe.matmul(out, wa[cols], mb, start=False, stop=last)

            def step(pos, b):
                up, down, turn = back(pos, 0), back(pos, 2), back(pos, 3)
                if up:
                    e, i = up
                    if isinstance(i, int) and i == 0:
                        pe.wait_ge(s_wl, e + 1)
                    cols = bass.ds(i * UW, UW)
                    for half in range(2):
                        wait(pe, s_gelu[half], count(up))
                        for c in range(2 * half, 2 * half + 2):
                            ins = three(ps_h[:, c, :], (wh[e % 2], wl[e % 2]), (slice(None), 0, slice(c * P, (c + 1) * P)),
                                        (xh[:, cols], xl[:, cols]), True, True)
                        ins.then_inc(s_up[half], 1)
                if down:
                    for half in range(2):
                        wait(pe, s_lo[half], count(down) + 1)
                    wait(pe, s_yT, count(down) - 1)
                    for c in range(FC):
                        w = (slice(None), 1, slice(c * D, (c + 1) * D))
                        ins = three(ps_y[:, b, :], (wh[down[0] % 2], wl[down[0] % 2]), w, (hh[b][:, c, :], hl[b][:, c, :]),
                                    c == 0, c == FC - 1)
                    ins.then_inc(s_y, 1)
                if turn:
                    wait(pe, s_yT, count(turn) + 1)
                    wait(pe, s_add, count(turn))
                    for t in range(UT):
                        ins = pe.transpose(ps_z[:, t, :], yT[:, 1 - b, t * P:(t + 1) * P], ident[:, :])
                    ins.then_inc(s_z, 1)

            units(pe, step)

        @block.scalar
        def _(act):
            def split(e):
                act.wait_ge(s_raw, 32 * (e + 1))
                if e >= 2:
                    act.wait_ge(s_y, (e - 1) * UNITS)
                act.activation(wh[e % 2][:, :, :], raw[:, :, :], ACT.Copy).then_inc(s_wh, 1)

            def step(pos, b):
                up, store = back(pos, 0), back(pos, 3)
                if store:
                    wait(act, s_y, count(store) + 1)
                    wait(act, s_z, count(store) - 1)
                    act.activation(yT[:, 1 - b, :], ps_y[:, 1 - b, :], ACT.Copy).then_inc(s_yT, 1)
                if up:
                    for half in range(2):
                        cs = slice(2 * half, 2 * half + 2)
                        wait(act, s_up[half], count(up) + 1)
                        wait(act, s_lo[half], count(up))
                        act.activation(h[:, cs, :], ps_h[:, cs, :], ACT.Gelu).then_inc(s_gelu[half], 1)
                        if half == 0:
                            wait(act, s_gelu[0], count(up) + 1)
                            wait(act, s_y, count(up) - 1)
                            act.activation(hh[b][:, cs, :], h[:, cs, :], ACT.Copy).then_inc(s_hi[0], 1)

            split(0)
            units(act, step, split)

        @block.vector
        def _(dve):
            def step(pos, b):
                up, add = back(pos, 0), back(pos, 4)
                if add:
                    wait(dve, s_z, count(add) + 1)
                    wait(dve, s_add, count(add))
                    for t in range(UT):
                        tile = bass.ds(add[1] * UT + t, 1)
                        gate = gates[:, tile, add[0]] if add[0] < E else 0.5
                        ins = dve.scalar_tensor_tensor(x[:, tile, :], ps_z[:, t, :].unsqueeze(1), gate, x[:, tile, :],
                                                       ALU.mult, ALU.add)
                    ins.then_inc(s_add, 1)
                if up:
                    for half in range(2):
                        cs = slice(2 * half, 2 * half + 2)
                        if half == 1:
                            wait(dve, s_gelu[1], count(up) + 1)
                            wait(dve, s_y, count(up) - 1)
                            dve.tensor_copy(hh[b][:, cs, :], h[:, cs, :]).then_inc(s_hi[1], 1)
                        wait(dve, s_hi[half], count(up) + 1)
                        dve.tensor_tensor(hl[b][:, cs, :], h[:, cs, :], hh[b][:, cs, :].bitcast(F32), ALU.subtract)\
                           .then_inc(s_lo[half], 1)

            units(dve, step)


def attention(nc, tag, T, W, dist, result, residual):
    x, mean, rstd, ident, cols = T["x"], T["mean"], T["rstd"], T["ident"], T["cols"]
    DVE_ROWS = 1
    SKEW, LAG = 2, 2
    V_AT, MAX_AT, OUT_AT, K_AT, Q_AT = 4, (0, 1), (2, 5), (4, 7), (8, 11)
    GH = G // 2
    assert V_AT >= SKEW + LAG and OUT_AT[1] >= SKEW + LAG
    with ExitStack() as ctx:
        n = Names(nc, ctx, tag)
        xn = n.sb("xn", [P, CH, D])
        xT = n.sb("xT", [P, SEQ])
        rq, rk, tk = (n.sb(k, [P, G, SEQ]) for k in ("rq", "rk", "tk"))
        qs = [n.sb(f"qs{b}", [P, G, SEQ], F32R) for b in range(3)]
        qm = [n.sb(f"qm{b}", [P, G, SEQ], F32R) for b in range(3)]
        km = [n.sb(f"km{b}", [P, G, HG, SEQ], F32R) for b in range(3)]
        va = [n.sb(f"va{b}", [P, CH, HEADS, HW]) for b in range(3)]
        mx = n.sb("mx", [P, HEADS, CH])
        ms = n.sb("ms", [P, CH, HEADS, HW])
        pT = n.sb("pT", [P, 2, CH, SEQ])
        oT = n.sb("oT", [P, G, SEQ])
        rs = n.sb("rs", [P, G * CH * HG])
        on = n.sb("on", [P, CH, HEADS, HD])
        ps_s = n.ps("ps_s", [P, 2, CH, SEQ])
        ps_t = n.ps("ps_t", [P, 2, CH, SEQ])
        ps_o = n.ps("ps_o", [P, 2, 512])
        ps_q = n.ps("ps_q", [P, G, SEQ])
        sem = {k: n.sem(k) for k in (
            "zeroed", "xn", "x_turned", "xT", "proj_q", "proj_k", "proj_v", "r_q", "r_k", "t_k", "qs", "km", "km_a", "va",
            "scores", "max", "neg", "lo", "max_turned", "qm", "scoresT", "probs", "pv", "oT", "out_turned",
            "recip", "scaled", "stored")}
        block = ctx.enter_context(nc.Block())

        def rounds(eng, body):
            for r in (-2, -1, 0, 1, 2):
                body(r, r % 3)
            full = (BATCH - 3) // 3
            with eng.Fori(1, full) as i:
                for k in range(3):
                    body(i * 3 + k, k)
            for r in range(3 * full, BATCH + 1):
                body(r, r % 3)

        def stage3(r, u, lag=0):
            v = u - SKEW - lag
            return (r, v) if v >= 0 else (r - 1, v + HEADS)

        def has(m):
            return not isinstance(m, int) or 0 <= m < BATCH

        def half(hf):
            return slice(hf * GH, (hf + 1) * GH)

        def divide(dve, m, hf):
            n_done = m * 2 + hf + 1
            dve.wait_ge(sem["out_turned"], n_done)
            o_in = ps_q[:, :, :].rearrange("p g (c h w) -> p g c h w", c=CH, w=HW)
            dve.reciprocal(rs[:, :].rearrange("p (g c h) -> p g c h", g=G, c=CH)[:, half(hf)], o_in[:, half(hf), :, :, HD])\
               .then_inc(sem["recip"], 1)
            dve.wait_ge(sem["recip"], n_done)
            tiles = bass.ds(m * CH, CH)
            for g in range(hf * GH, (hf + 1) * GH):
                sums = bcast(rs[:, g * CH * HG:(g + 1) * CH * HG], HD).rearrange("p (c h) d -> p c h d", c=CH)
                dst = on[:, :, g * HG:(g + 1) * HG, :]
                if not residual:
                    dst = result[:, tiles, g * HG * HD:(g + 1) * HG * HD].rearrange("p c (h d) -> p c h d", d=HD)
                ins = dve.tensor_tensor(dst, o_in[:, g, :, :, 0:HD], sums, ALU.mult)
            ins.then_inc(sem["stored"], 1)
            if residual:
                dve.wait_ge(sem["stored"], n_done)
                part = slice(hf * GH * HG * HD, (hf + 1) * GH * HG * HD)
                xs = result[:, tiles, part]
                dve.tensor_tensor(xs, xs, on[:, :, :, :].rearrange("p c h d -> p c (h d)")[:, :, part], ALU.add)\
                   .then_inc(sem["scaled"], 1)

        def normalise(dve, m):
            for c in range(CH):
                t = bass.ds(m * CH + c, 1)
                ins = dve.tensor_scalar(xn[:, c, :], x[:, t, :], mean[:, t], rstd[:, t], ALU.subtract, ALU.mult)
            ins.then_inc(sem["xn"], 1)

        @block.vector
        def _(dve):
            for b in range(3):
                dve.memset(va[b][:, :, :, :], 0.0).then_inc(sem["zeroed"], 1)
            dve.wait_ge(sem["zeroed"], 3)
            for b in range(3):
                dve.memset(va[b][:, :, :, HD:HD + 1], 1.0).then_inc(sem["zeroed"], 1)
            dve.memset(ms[:, :, :, :], 0.0).then_inc(sem["zeroed"], 1)
            for b in range(3):
                dve.memset(km[b][:, :, :, :].bitcast(F32), 0.0).then_inc(sem["zeroed"], 1)
            dve.wait_ge(sem["zeroed"], 10)
            normalise(dve, 0)

            def body(r, k):
                m1, m2, b1 = r + 2, r + 1, (k + 2) % 3

                def fill_values():
                    dve.wait_ge(sem["proj_v"], m1 + 1)
                    v_in = ps_o[:, 1, 0:CH * D].rearrange("p (c h d) -> p c h d", c=CH, d=HD)
                    if W["bv"] is None:
                        ins = dve.tensor_copy(va[b1][:, :, :, 0:HD], v_in)
                    else:
                        for c in range(CH):
                            ins = dve.tensor_tensor(va[b1][:, c, :, 0:HD], v_in[:, c, :, :],
                                                    W["bv"][:, :].rearrange("p (h d) -> p h d", d=HD), ALU.add)
                    ins.then_inc(sem["va"], 1)

                def fill_keys(hf):
                    dve.wait_ge(sem["r_k"], m1 * 2 + hf + 1)
                    dve.wait_ge(sem["t_k"], m1 * 2 + hf + 1)
                    for h in range(DVE_ROWS):
                        rows = slice(h * HW, (h + 1) * HW)
                        ins = dve.scalar_tensor_tensor(km[b1][rows, half(hf), h, :], ps_q[rows, half(hf), :], cols[rows, 2:3],
                                                       rk[rows, half(hf), :], ALU.mult, ALU.add)
                    ins.then_inc(sem["km_a"], 1)

                def fill_queries(hf):
                    dve.wait_ge(sem["r_q"], m1 * 2 + hf + 1)
                    dve.scalar_tensor_tensor(qs[b1][:, half(hf), :], ps_q[:, half(hf), :], cols[:, 0:1], rq[:, half(hf), :],
                                             ALU.mult, ALU.add)\
                       .then_inc(sem["qs"], 1)

                def split_maxima():
                    dve.wait_ge(sem["max"], (r + 1) * HEADS)
                    m_in = mx[:, :, :].rearrange("p h c -> p c h")
                    hi = ms[:, :, :, ROW_M]
                    dve.tensor_scalar(hi.bitcast(F32R), m_in, -1.0, None, ALU.mult).then_inc(sem["neg"], 1)
                    dve.wait_ge(sem["neg"], r + 1)
                    dve.scalar_tensor_tensor(ms[:, :, :, ROW_M + 1], m_in, -1.0, hi, ALU.mult, ALU.subtract).then_inc(sem["lo"], 1)

                if has(r):
                    split_maxima()
                for u in range(HEADS):
                    if has(m2):
                        head = (u % G) * HG + u // G
                        dve.wait_ge(sem["scores"], m2 * HEADS + u + 1)
                        if u == 0 and has(r):
                            dve.wait_ge(sem["lo"], r + 1)
                        dve.tensor_reduce(mx[:, head, :], ps_s[:, u % 2, :, :], AX.X, ALU.max).then_inc(sem["max"], 1)
                    if u in MAX_AT and has(r):
                        hf = MAX_AT.index(u)
                        dve.wait_ge(sem["max_turned"], r * 2 + hf + 1)
                        dve.tensor_tensor(qm[k][:, half(hf), :], ps_q[:, half(hf), :], qs[k][:, half(hf), :].bitcast(F32), ALU.add)\
                           .then_inc(sem["qm"], 1)
                    if u == 2 and has(m1) and (not isinstance(r, int) or has(m1 + 1)):
                        dve.wait_ge(sem["x_turned"], m1 + 1)
                        normalise(dve, m1 + 1)
                    if u in OUT_AT and has(r - 1):
                        divide(dve, r - 1, OUT_AT.index(u))
                    if has(m1) and u == V_AT:
                        fill_values()
                    if has(m1) and u - 2 in K_AT:
                        fill_keys(K_AT.index(u - 2))
                    if has(m1) and u - 2 in Q_AT:
                        fill_queries(Q_AT.index(u - 2))

            rounds(dve, body)

        @block.gpsimd
        def _(pool):
            pool.wait_ge(sem["zeroed"], 10)

            def body(r, k):
                m1, b1 = r + 2, (k + 2) % 3
                for hf in range(2):
                    if has(m1):
                        pool.wait_ge(sem["t_k"], m1 * 2 + hf + 1)
                        for h in range(DVE_ROWS, HG):
                            rows = slice(h * HW, (h + 1) * HW)
                            ins = pool.tensor_tensor(km[b1][rows, half(hf), h, :], tk[rows, half(hf), :], rk[rows, half(hf), :],
                                                     ALU.add)
                        ins.then_inc(sem["km"], 1)

            rounds(pool, body)

        @block.tensor
        def _(pe):
            augmented = W["aug"] is not None

            def turn_output(m, hf):
                pe.wait_ge(sem["oT"], m * G + (hf + 1) * GH)
                for g in range(hf * GH, (hf + 1) * GH):
                    for c in range(CH):
                        ins = pe.transpose(ps_q[:, g, c * P:(c + 1) * P], oT[:, g, c * P:(c + 1) * P], ident[:, :])
                ins.then_inc(sem["out_turned"], 1)

            def own_chunk_distance(ps, u, c, side):
                for part in range(2):
                    ins = pe.matmul(ps[:, u % 2, c, c * P:(c + 1) * P], dist["eye"][:, part, :], dist["tab"][:, side, :],
                                    start=False, stop=part == 1)
                return ins

            def project(which, hf, done):
                for g in range(hf * GH, (hf + 1) * GH):
                    gs = slice(g * P, (g + 1) * P)
                    ins = pe.matmul(ps_q[:, g, :], W["qk"][which][:, gs], xT[:, :], start=True, stop=not augmented)
                    if augmented:
                        ins = pe.matmul(ps_q[:, g, :], W["aug"][:, which, gs], W["rows"][:, :], start=False, stop=True)
                ins.then_inc(done, 1)

            def body(r, k):
                m1, m2, b2 = r + 2, r + 1, (k + 1) % 3

                def scores(u):
                    h, g = divmod(u, G)
                    if u == 0:
                        pe.wait_ge(sem["qs"], (m2 + 1) * 2)
                        pe.wait_ge(sem["km_a"], (m2 + 1) * 2)
                        pe.wait_ge(sem["km"], (m2 + 1) * 2)
                    if u >= 2 or has(m2 - 1):
                        pe.wait_ge(sem["max"], m2 * HEADS + u - 1)
                    for c in range(CH):
                        ins = pe.matmul(ps_s[:, u % 2, c, :], qs[b2][:, g, c * P:(c + 1) * P], km[b2][:, g, h, :],
                                        start=True, stop=dist is None)
                        if dist is not None:
                            ins = own_chunk_distance(ps_s, u, c, 1 - c)
                    ins.then_inc(sem["scores"], 1)

                def scores_turned(m, v, b):
                    g, h = divmod(v, HG)
                    if v % (GH * HG) == 0:
                        pe.wait_ge(sem["qm"], m * 2 + g // GH + 1)
                    if v >= 2 or has(m - 1):
                        pe.wait_ge(sem["probs"], m * HEADS + v - 1)
                    for c in range(CH):
                        ins = pe.matmul(ps_t[:, v % 2, c, :], km[b][:, g, h, c * P:(c + 1) * P], qm[b][:, g, :],
                                        start=True, stop=dist is None)
                        if dist is not None:
                            ins = own_chunk_distance(ps_t, v, c, c)
                    ins.then_inc(sem["scoresT"], 1)

                def weigh_values(m, v, b):
                    g, h = divmod(v, HG)
                    pe.wait_ge(sem["probs"], m * HEADS + v + 1)
                    if h == 0 and g < 2 and has(m + 2):
                        pe.wait_ge(sem[("xT", "va")[g]], m + 3)
                    elif h == 0 and (g >= 2 or has(m - 1)):
                        pe.wait_ge(sem["oT"], m * G + g - 1)
                    for c in range(CH):
                        ins = pe.matmul(ps_o[h * HW:(h + 1) * HW, g % 2, 0:SEQ], va[b][:, c, v, :], pT[:, v % 2, c, :],
                                        start=c == 0, stop=c == CH - 1)
                    ins.then_inc(sem["pv"], 1)

                def turn_x():
                    pe.wait_ge(sem["xn"], m1 + 1)
                    if has(r - 1):
                        pe.wait_ge(sem["oT"], r * G - 1)
                    for c in range(CH):
                        ins = pe.transpose(ps_o[:, 0, c * P:(c + 1) * P], xn[:, c, :], ident[:, :])
                    ins.then_inc(sem["x_turned"], 1)

                def project_values():
                    pe.wait_ge(sem["xT"], m1 + 1)
                    if has(r - 1):
                        pe.wait_ge(sem["oT"], r * G)
                    elif has(m1 - 1):
                        pe.wait_ge(sem["va"], m1)
                    for c in range(CH):
                        ins = pe.matmul(ps_o[:, 1, c * D:(c + 1) * D], xT[:, c * P:(c + 1) * P], W["v"][:, :], start=True, stop=True)
                    ins.then_inc(sem["proj_v"], 1)

                def turn_maxima(hf):
                    if hf == 0:
                        pe.wait_ge(sem["lo"], r + 1)
                    if has(m2):
                        pe.wait_ge(sem["qs"], (m2 + 1) * 2)
                    else:
                        pe.wait_ge(sem["stored"], (r - 1) * 2)
                    for g in range(hf * GH, (hf + 1) * GH):
                        for c in range(CH):
                            ins = pe.transpose(ps_q[:, g, c * P:(c + 1) * P],
                                               ms[:, c, g * HG:(g + 1) * HG, :].rearrange("p h w -> p (h w)"), ident[:, :])
                    ins.then_inc(sem["max_turned"], 1)

                for u in range(HEADS):
                    m, v = stage3(r, u, LAG)
                    if has(m):
                        weigh_values(m, v, k if u >= SKEW + LAG else (k + 2) % 3)
                    m, v = stage3(r, u)
                    if has(m):
                        scores_turned(m, v, k if u >= SKEW else (k + 2) % 3)
                    if has(m1) and u == 0:
                        turn_x()
                    if has(m1) and u == V_AT:
                        project_values()
                    if has(r - 1) and u in OUT_AT:
                        hf = OUT_AT.index(u)
                        if has(r):
                            pe.wait_ge(sem["qm"], r * 2 + hf + 1)
                        else:
                            pe.wait_ge(sem["stored"], (r - 1) * 2)
                        turn_output(r - 1, hf)
                    if has(m2):
                        scores(u)
                    if has(r) and u in MAX_AT:
                        turn_maxima(MAX_AT.index(u))
                    if has(m1) and u in K_AT:
                        hf = K_AT.index(u)
                        if has(r - 1):
                            pe.wait_ge(sem["stored"], (r - 1) * 2 + hf + 1)
                        elif has(r):
                            pe.wait_ge(sem["qm"], r * 2 + hf + 1)
                        elif has(m2):
                            pe.wait_ge(sem["qs"], (m2 + 1) * 2)
                        project(1, hf, sem["proj_k"])
                    if has(m1) and u in Q_AT:
                        hf = Q_AT.index(u)
                        pe.wait_ge(sem["km_a"], m1 * 2 + hf + 1)
                        project(0, hf, sem["proj_q"])

            rounds(pe, body)

        @block.scalar
        def _(act):
            def body(r, k):
                m1 = r + 2

                def output(m, g):
                    act.wait_ge(sem["pv"], m * HEADS + (g + 1) * HG)
                    if g % GH == 0 and has(m - 1):
                        act.wait_ge(sem["out_turned"], (m - 1) * 2 + g // GH + 1)
                    act.activation(oT[:, g, :], ps_o[:, g % 2, 0:SEQ], ACT.Copy).then_inc(sem["oT"], 1)

                for u in range(HEADS):
                    m, v = stage3(r, u, LAG)
                    if has(m) and v % HG == HG - 1:
                        output(m, v // HG)
                    if has(m1) and u - 1 in K_AT:
                        hf = K_AT.index(u - 1)
                        act.wait_ge(sem["proj_k"], m1 * 2 + hf + 1)
                        if has(r + 1):
                            act.wait_ge(sem["km"], (m1 - 1) * 2 + hf + 1)
                        act.activation(rk[:, half(hf), :].bitcast(F32R), ps_q[:, half(hf), :], ACT.Identity, bias=cols[:, 5:6],
                                       scale=cols[:, 3:4]).then_inc(sem["r_k"], 1)
                    if has(m1) and u - 1 in Q_AT:
                        hf = Q_AT.index(u - 1)
                        act.wait_ge(sem["proj_q"], m1 * 2 + hf + 1)
                        act.activation(rq[:, half(hf), :].bitcast(F32R), ps_q[:, half(hf), :], ACT.Identity, bias=cols[:, 4:5],
                                       scale=cols[:, 1:2]).then_inc(sem["r_q"], 1)
                    m, v = stage3(r, u)
                    if has(m):
                        act.wait_ge(sem["scoresT"], m * HEADS + v + 1)
                        if v >= 2 or has(m - 1):
                            act.wait_ge(sem["pv"], m * HEADS + v - 1)
                        act.activation(pT[:, v % 2, :, :], ps_t[:, v % 2, :, :], ACT.Exp, scale=SM_SCALE).then_inc(sem["probs"], 1)
                    if has(m1) and u == 0:
                        act.wait_ge(sem["x_turned"], m1 + 1)
                        act.activation(xT[:, :], ps_o[:, 0, 0:SEQ], ACT.Copy).then_inc(sem["xT"], 1)
                    if has(m1) and u - 1 in K_AT:
                        hf = K_AT.index(u - 1)
                        act.activation(tk[:, half(hf), :], ps_q[:, half(hf), :], ACT.Copy, scale=cols[:, 2:3]).then_inc(sem["t_k"], 1)

            rounds(act, body)


def attention_weights(nc, tag, parts, bias, dist, T):
    with ExitStack() as ctx:
        n = Names(nc, ctx, tag)
        neg = n.sb("neg", [P, 3])
        s_c = n.sem("chain")
        block = ctx.enter_context(nc.Block())

        def spread(dve, dst, src):
            d = dst.rearrange("p (h w) -> p h w", w=HW)
            s = src.rearrange("p (h d) -> p h d", d=HD)
            for term in range(3):
                ins = dve.tensor_copy(d[:, :, term * HD:(term + 1) * HD], s)
            return ins

        @block.vector
        def _(dve):
            chain = Chain(dve, s_c)
            for dst, _ in parts:
                chain(dve.memset(dst, 0.0))
            for dst, src in parts:
                spread(dve, dst, src)
            if bias is None:
                return
            raw, S = bias
            chain(dve.memset(raw["one"][:, :], 1.0))
            chain(dve.tensor_copy(raw["hi"][:, :, :].bitcast(F32R), raw["b"][:, :, :]))
            chain(dve.tensor_tensor(raw["b"][:, :, :], raw["b"][:, :, :], raw["hi"][:, :, :], ALU.subtract))
            for k in range(2):
                spread(dve, raw["aug"][0:1, k, :], raw["hi"][0:1, k, :])
                chain(spread(dve, raw["aug"][HW:HW + 1, k, :], raw["b"][HW:HW + 1, k, :]))
            chain(dve.tensor_scalar(neg[:, 0:1], dist["scale"][:, 0:1], -1.0, None, ALU.mult))
            chain(dve.tensor_copy(neg[:, 1:2].bitcast(F32R), neg[:, 0:1]))
            chain(dve.tensor_tensor(neg[:, 2:3], neg[:, 0:1], neg[:, 1:2], ALU.subtract))
            for part in range(2):
                q_row, k_row = slice(part * HW, part * HW + 1), slice(2 * HW, 2 * HW + 1)
                heads = raw["aug"][:, :, :].rearrange("p s (h w) -> p s h w", w=HW)
                q_dst = heads[q_row, 0, :, ROW_DIST + 2 + part]
                chain(dve.tensor_scalar(q_dst, raw["one"][q_row, :], neg[q_row, 1 + part:2 + part], -1.0, ALU.mult, ALU.mult))
                k_dst = heads[k_row, 1, :, ROW_DIST + part]
                chain(dve.tensor_scalar(k_dst, raw["one"][k_row, :], neg[k_row, 1 + part:2 + part], None, ALU.mult))
                dve.tensor_scalar(dist["eye"][:, part, :], T["ident"][:, :], neg[:, 1 + part:2 + part], 2.0, ALU.mult, ALU.mult)
            dve.tensor_copy(S["aug"][:, :, :], raw["aug"][:, :, :])
            dve.tensor_copy(S["rows"][:, :], raw["rows"][:, :])
            dve.tensor_copy(dist["tab"][:, :, :], dist["raw"][:, :, :])


def project_and_mlp(nc, tag, T, a_all, W):
    x, mean, rstd, ident = T["x"], T["mean"], T["rstd"], T["ident"]
    with ExitStack() as ctx:
        n = Names(nc, ctx, tag)
        a = n.sb("a", [P, UT, D])
        r0, r1, r2, r3 = (n.sb(k, [P, UT, D]) for k in ("r0", "x1", "r2", "r3"))
        r4, r5, r6 = (n.sb(k, [P, UT, D]) for k in ("r4", "r5", "r6"))
        aT, x1T = n.sb("aT", [P, UW]), n.sb("x1T", [P, UW])
        hT = n.sb("hT", [P, FC, UW])
        st, mv = n.sb("st", [P, UT, 6]), n.sb("mv", [P, UT, 3])
        rs = n.sb("rs", [P, UT])
        ps_ta, ps_tx = n.ps("ps_ta", [P, UW]), n.ps("ps_tx", [P, UW])
        ps_h = n.ps("ps_h", [P, FC, UW])
        ps_p, ps_y = n.ps("ps_p", [P, UT, D]), n.ps("ps_y", [P, UT, D])
        sem = {k: n.sem(k) for k in ("a", "a_turned", "aT", "proj", "summed", "var_0", "pow_0", "var_1", "pow_1",
                                     "x1", "x1_turned", "x1T", "up", "h", "y", "own")}
        block = ctx.enter_context(nc.Block())

        def wide(v):
            return v[:, :].unsqueeze(1).to_broadcast([P, UT, D])

        def rounds(eng, body):
            body(0, True, False)
            with eng.Fori(1, UNITS) as i:
                body(i, True, True)
            body(UNITS, False, True)

        @block.gpsimd
        def _(pool):
            def fetch(u):
                pool.tensor_copy(a[:, :, :], a_all[:, bass.ds(u * UT, UT), :]).then_inc(sem["a"], 1)

            def power(u, k):
                pool.wait_ge(sem[f"var_{k}"], u + 1)
                pool.tensor_tensor(rs[:, :], mv[:, :, 1], T["neg_half"][:, 0:UT], ALU.pow).then_inc(sem[f"pow_{k}"], 1)

            fetch(0)

            def body(u, front, back):
                if front:
                    power(u, 0)
                if back:
                    power(u - 1, 1)

            def fetch_next(u):
                pool.wait_ge(sem["a_turned"], u + 1)
                fetch(u + 1)

            fetch_next(0)
            body(0, True, False)
            with pool.Fori(1, UNITS - 1) as i:
                fetch_next(i)
                body(i, True, True)
            body(UNITS - 1, True, True)
            body(UNITS, False, True)

        @block.tensor
        def _(pe):
            def turn(dst, src, done):
                for k in range(UT):
                    ins = pe.transpose(dst[:, k * P:(k + 1) * P], src[:, k, :], ident[:, :])
                ins.then_inc(done, 1)

            def body(u, front, back):
                if front:
                    pe.wait_ge(sem["a"], u + 1)
                    turn(ps_ta, a, sem["a_turned"])
                    pe.wait_ge(sem["aT"], u + 1)
                    if back:
                        pe.wait_ge(sem["summed"], u)
                    for k in range(UT):
                        ins = pe.matmul(ps_p[:, k, :], aT[:, k * P:(k + 1) * P], W["o"][:, :], start=True, stop=True)
                    ins.then_inc(sem["proj"], 1)
                if back:
                    pe.wait_ge(sem["x1"], u)
                    turn(ps_tx, r1, sem["x1_turned"])
                    pe.wait_ge(sem["x1T"], u)
                    for c in range(FC):
                        pe.matmul(ps_h[:, c, :], W["up"][:, c * P:(c + 1) * P], x1T[:, :], start=True, stop=True)\
                          .then_inc(sem["up"], 1)
                    pe.wait_ge(sem["h"], u * FC)
                    for k in range(UT):
                        for c in range(FC):
                            ins = pe.matmul(ps_y[:, k, :], hT[:, c, k * P:(k + 1) * P], W["down"][:, c, :],
                                            start=c == 0, stop=c == FC - 1)
                    ins.then_inc(sem["y"], 1)

            rounds(pe, body)

        @block.scalar
        def _(act):
            def body(u, front, back):
                if front:
                    act.wait_ge(sem["a_turned"], u + 1)
                    act.activation(aT[:, :], ps_ta[:, :], ACT.Copy).then_inc(sem["aT"], 1)
                if back:
                    act.wait_ge(sem["x1_turned"], u)
                    act.activation(x1T[:, :], ps_tx[:, :], ACT.Copy).then_inc(sem["x1T"], 1)
                    for c in range(FC):
                        act.wait_ge(sem["up"], (u - 1) * FC + c + 1)
                        act.activation(hT[:, c, :], ps_h[:, c, :], ACT.Relu, bias=W["b1"][:, c:c + 1]).then_inc(sem["h"], 1)

            rounds(act, body)

        FRONT, BACK = 8, 8

        @block.vector
        def _(dve):
            def body(u, front, back):
                done = (FRONT + (u - 1) * (FRONT + BACK)) if back else 0
                steps = [0]

                def step(ins):
                    steps[0] += 1
                    ins.then_inc(sem["own"], 1)
                    dve.wait_ge(sem["own"], done + steps[0])

                def norm(src, dst, unit, k):
                    for t in range(UT):
                        ins = dve.bn_stats(st[:, t, :], src[:, t, :])
                    step(ins)
                    dve.tensor_tensor(mv[:, :, 0], st[:, :, 1], st[:, :, 4], ALU.add)
                    dve.tensor_tensor(mv[:, :, 2], st[:, :, 1], st[:, :, 4], ALU.subtract)
                    step(dve.tensor_tensor(mv[:, :, 1], st[:, :, 2], st[:, :, 5], ALU.add))
                    dve.tensor_scalar(mv[:, :, 0], mv[:, :, 0], 0.5, None, ALU.mult)
                    dve.scalar_tensor_tensor(mv[:, :, 2], mv[:, :, 2], 0.25, mv[:, :, 2], ALU.mult, ALU.mult)
                    step(dve.tensor_scalar(mv[:, :, 1], mv[:, :, 1], 1.0 / D, EPS, ALU.mult, ALU.add))
                    dve.tensor_tensor(mv[:, :, 1], mv[:, :, 1], mv[:, :, 2], ALU.add).then_inc(sem[f"var_{k}"], 1)
                    dve.wait_ge(sem[f"pow_{k}"], unit + 1)
                    for t in range(UT):
                        ins = dve.tensor_scalar(dst[:, t, :], src[:, t, :], mv[:, t, 0:1], rs[:, t:t + 1],
                                                ALU.subtract, ALU.mult)
                    step(ins)

                if front:
                    for t in range(UT):
                        tile = bass.ds(u * UT + t, 1)
                        ins = dve.tensor_scalar(r0[:, t, :], x[:, tile, :], mean[:, tile], rstd[:, tile],
                                                ALU.subtract, ALU.mult)
                    step(ins)
                    step(dve.tensor_tensor(r0[:, :, :], r0[:, :, :], wide(W["bo"]), ALU.add))
                    dve.wait_ge(sem["proj"], u + 1)
                    dve.tensor_tensor(r2[:, :, :], ps_p[:, :, :], r0[:, :, :], ALU.add).then_inc(sem["summed"], 1)
                    dve.wait_ge(sem["summed"], u + 1)
                    norm(r2, r3, u, 0)
                if back:
                    dve.wait_ge(sem["y"], u)
                    step(dve.tensor_tensor(r5[:, :, :], ps_y[:, :, :], r4[:, :, :], ALU.add))
                if front:
                    step(dve.tensor_tensor(r3[:, :, :], r3[:, :, :], wide(W["g1"]), ALU.mult))
                    dve.tensor_tensor(r1[:, :, :], r3[:, :, :], wide(W["be1"]), ALU.add).then_inc(sem["x1"], 1)
                    dve.wait_ge(sem["x1"], u + 1)
                    step(dve.tensor_tensor(r4[:, :, :], r1[:, :, :], wide(W["b2"]), ALU.add))
                if back:
                    norm(r5, r6, u - 1, 1)
                    step(dve.tensor_tensor(r6[:, :, :], r6[:, :, :], wide(W["g2"]), ALU.mult))
                    step(dve.tensor_tensor(r6[:, :, :], r6[:, :, :], wide(W["be2"]), ALU.add))
                    xs = x[:, bass.ds((u - 1) * UT, UT), :]
                    step(dve.tensor_tensor(xs, xs, r6[:, :, :], ALU.add))
                assert steps[0] == front * FRONT + back * BACK, steps[0]

            rounds(dve, body)


def gather_chosen(nc, tag, T, slots, chosen, iota):
    x, mean, rstd = T["x"], T["mean"], T["rstd"]
    EB = E // 2
    with ExitStack() as ctx:
        n = Names(nc, ctx, tag)
        xn = n.sb("xn", [P, 2, CH, D])
        hi, lo = n.sb("hi", [P, 2, CH, D], F32R), n.sb("lo", [P, 2, CH, D], F32R)
        at = n.sb("at", [P, 2, CH, E, CAP], F32R)
        ps = n.ps("ps", [P, 2, 2, 512])
        s_xn = [n.sem(f"xn_ready{b}") for b in range(2)]
        s_hi = [n.sem(f"hi_ready{b}") for b in range(2)]
        s_op = [n.sem(f"operands_ready{b}") for b in range(2)]
        s_mm = [n.sem(f"gathered{b}") for b in range(2)]
        s_st = [n.sem(f"stored{b}") for b in range(2)]
        block = ctx.enter_context(nc.Block())

        @block.vector
        def _(dve):
            prime(dve, *s_xn, *s_op)
            with dve.Fori(0, BATCH // 2) as i:
                for b in range(2):
                    m = i * 2 + b
                    dve.wait_ge(s_mm[b], before(i))
                    for c in range(CH):
                        t = bass.ds(m * CH + c, 1)
                        ins = dve.tensor_scalar(xn[:, b, c, :], x[:, t, :], mean[:, t], rstd[:, t], ALU.subtract, ALU.mult)
                    ins.then_inc(s_xn[b], 1)
                    for c in range(CH):
                        place = slots[:, bass.ds(m * CH + c, 1), :].rearrange("p o e -> p (o e)")
                        dve.tensor_tensor(at[:, b, c, :, :], iota[:, :].unsqueeze(1).to_broadcast([P, E, CAP]),
                                          bcast(place, CAP), ALU.is_equal)
                    dve.wait_ge(s_hi[b], after(i))
                    dve.tensor_tensor(lo[:, b, :, :], xn[:, b, :, :], hi[:, b, :, :].bitcast(F32), ALU.subtract)\
                       .then_inc(s_op[b], 1)

        @block.scalar
        def _(act):
            prime(act, *s_hi, *s_st)
            with act.Fori(0, BATCH // 2) as i:
                for b in range(2):
                    act.wait_ge(s_xn[b], after(i))
                    act.activation(hi[:, b, :, :], xn[:, b, :, :], ACT.Copy).then_inc(s_hi[b], 1)
                for b in range(2):
                    act.wait_ge(s_mm[b], after(i))
                    dst = chosen[:, :, bass.ds(i * 2 + b, 1), :].rearrange("p (k e) o s -> p k e (o s)", k=2)
                    for k in range(2):
                        src = ps[:, b, k, 0:EB * CAP].rearrange("p (e s) -> p e s", e=EB)
                        ins = act.activation(dst[:, k, :, :], src, ACT.Copy)
                    ins.then_inc(s_st[b], 1)

        @block.tensor
        def _(pe):
            prime(pe, *s_mm)
            with pe.Fori(0, BATCH // 2) as i:
                for b in range(2):
                    pe.wait_ge(s_op[b], after(i))
                    pe.wait_ge(s_st[b], before(i))
                    for k in range(2):
                        for j, part in enumerate((hi, lo)):
                            for c in range(CH):
                                ins = pe.matmul(ps[:, b, k, 0:EB * CAP], part[:, b, c, :],
                                                at[:, b, c, k * EB:(k + 1) * EB, :].rearrange("p e s -> p (e s)"),
                                                start=j == 0 and c == 0, stop=j == 1 and c == CH - 1)
                    ins.then_inc(s_mm[b], 1)


def chosen_experts(nc, tag, chosen, W):
    N = BATCH * CAP
    STEPS = 5
    NW = N // STEPS
    assert NW * STEPS == N and NW <= 512
    with ExitStack() as ctx:
        n = Names(nc, ctx, tag)
        hT = n.sb("hT", [P, 2, FC, NW])
        ps_h = n.ps("ps_h", [P, FC, 512])
        ps_y = n.ps("ps_y", [P, 2, 512])
        s_up = [n.sem(f"up_done{h}") for h in range(2)]
        s_gelu = [n.sem(f"gelu_done{h}") for h in range(2)]
        s_y = [n.sem(f"y_ready{b}") for b in range(2)]
        s_st = [n.sem(f"y_stored{b}") for b in range(2)]
        flat = chosen[:, :, :, :].rearrange("p e b s -> p e (b s)")
        block = ctx.enter_context(nc.Block())
        EP = E // 2

        @block.tensor
        def _(pe):
            prime(pe, *s_up, *s_y)
            with pe.Fori(0, STEPS) as i:
                cols = bass.ds(i * NW, NW)

                def up_half(e, half):
                    pe.wait_ge(s_gelu[half], before(i * E + e))
                    for c in range(2 * half, 2 * half + 2):
                        ins = pe.matmul(ps_h[:, c, 0:NW], W["up"][:, e, c * P:(c + 1) * P], flat[:, e, cols], start=True, stop=True)
                    ins.then_inc(s_up[half], 1)

                def down_all(e):
                    b = e % 2
                    for half in range(2):
                        pe.wait_ge(s_gelu[half], after(i * E + e))
                    pe.wait_ge(s_st[b], before(i * EP + e // 2))
                    for c in range(FC):
                        ins = pe.matmul(ps_y[:, b, 0:NW], W["down"][:, e, c, :], hT[:, b, c, :], start=c == 0, stop=c == FC - 1)
                    ins.then_inc(s_y[b], 1)

                for e in range(E):
                    up_half(e, 0)
                    up_half(e, 1)
                    if e:
                        down_all(e - 1)
                down_all(E - 1)

        @block.scalar
        def _(act):
            prime(act, *s_gelu)
            with act.Fori(0, STEPS) as i:
                for e in range(E):
                    b = e % 2
                    act.wait_ge(s_y[b], before(i * EP + e // 2))
                    for half in range(2):
                        act.wait_ge(s_up[half], after(i * E + e))
                        for c in range(2 * half, 2 * half + 2):
                            ins = act.activation(hT[:, b, c, :], ps_h[:, c, 0:NW], ACT.Gelu, bias=W["b1"][:, e, c:c + 1])
                        ins.then_inc(s_gelu[half], 1)

        @block.vector
        def _(dve):
            prime(dve, *s_st)
            with dve.Fori(0, STEPS) as i:
                for e in range(E):
                    b = e % 2
                    dve.wait_ge(s_y[b], after(i * EP + e // 2))
                    dve.tensor_scalar(flat[:, e, bass.ds(i * NW, NW)], ps_y[:, b, 0:NW], W["b2"][:, e:e + 1], None, ALU.add)\
                       .then_inc(s_st[b], 1)


def scatter_chosen(nc, tag, T, slots, chosen, iota):
    x, gates, ident = T["x"], T["gates"], T["ident"]
    N = E * CAP
    KC = 5
    KW = N // KC
    assert KW * KC == N and KW <= P
    with ExitStack() as ctx:
        n = Names(nc, ctx, tag)
        at = n.sb("at", [P, 2, CH, E, CAP])
        og = n.sb("og", [P, 2, CH, E, CAP])
        yT = n.sb("yT", [P, 2, E, CAP])
        ogT = n.sb("ogT", [KW, 2, KC, SEQ])
        y = n.sb("y", [KW, 2, KC, D])
        ps_g = n.ps("ps_g", [P, 3, 512])
        ps_y = n.ps("ps_y", [P, 2, 512])
        ps_o = n.ps("ps_o", [P, 2, 512])
        s_yT = [n.sem(f"yT_ready{b}") for b in range(2)]
        s_at = n.sem("places_ready")
        s_og = [n.sem(f"gates_ready{b}") for b in range(2)]
        s_tg = [n.sem(f"gates_turned{b}") for b in range(2)]
        s_ty = [n.sem(f"y_turned{b}") for b in range(2)]
        s_gs, s_ys = ([n.sem(f"{k}{b}") for b in range(2)] for k in ("gates_stored", "y_stored"))
        s_o = [n.sem(f"out_ready{b}") for b in range(2)]
        s_add = [n.sem(f"added{b}") for b in range(2)]
        block = ctx.enter_context(nc.Block())

        @block.gpsimd
        def _(pool):
            prime(pool, *s_yT)
            with pool.Fori(0, BATCH // 2) as i:
                for b in range(2):
                    pool.wait_ge(s_ty[b], before(i))
                    pool.tensor_copy(yT[:, b, :, :], chosen[:, :, bass.ds(i * 2 + b, 1), :].rearrange("p e o s -> p e (o s)"))\
                        .then_inc(s_yT[b], 1)

        @block.vector
        def _(dve):
            prime(dve, *s_og, *s_add)

            def add(i, b):
                dve.wait_ge(s_o[b], after(i))
                xs = x[:, bass.ds((i * 2 + b) * CH, CH), :]
                dve.tensor_tensor(xs, ps_o[:, b, 0:CH * D].rearrange("p (c d) -> p c d", c=CH), xs, ALU.add).then_inc(s_add[b], 1)

            with dve.Fori(0, BATCH // 2) as i:
                for b in range(2):
                    m = i * 2 + b
                    dve.wait_ge(s_tg[b], before(i))
                    for c in range(CH):
                        place = slots[:, bass.ds(m * CH + c, 1), :].rearrange("p o e -> p (o e)")
                        ins = dve.tensor_tensor(at[:, b, c, :, :], iota[:, :].unsqueeze(1).to_broadcast([P, E, CAP]),
                                                bcast(place, CAP), ALU.is_equal)
                    ins.then_inc(s_at, 1)
                    dve.wait_ge(s_at, m + 1)
                    for c in range(CH):
                        gate = gates[:, bass.ds(m * CH + c, 1), :].rearrange("p o e -> p (o e)")
                        ins = dve.tensor_tensor(og[:, b, c, :, :], at[:, b, c, :, :], bcast(gate, CAP), ALU.mult)
                    ins.then_inc(s_og[b], 1)
                for b in range(2):
                    add(i, b)

        @block.tensor
        def _(pe):
            prime(pe, *s_tg, *s_ty, *s_o)
            with pe.Fori(0, BATCH // 2) as i:
                for b in range(2):
                    pe.wait_ge(s_og[b], after(i))
                    pe.wait_ge(s_gs[1 - b], after(i) if b else before(i))
                    for c in range(CH):
                        flat = og[:, b, c, :, :].rearrange("p e s -> p (e s)")
                        for k in range(KC):
                            q = k * CH + c
                            ins = pe.transpose(ps_g[0:KW, q // 4, (q % 4) * P:(q % 4 + 1) * P], flat[:, k * KW:(k + 1) * KW], ident[:, :])
                    ins.then_inc(s_tg[b], 1)
                    pe.wait_ge(s_yT[b], after(i))
                    pe.wait_ge(s_ys[1 - b], after(i) if b else before(i))
                    flat = yT[:, b, :, :].rearrange("p e s -> p (e s)")
                    for k in range(KC):
                        ins = pe.transpose(ps_y[0:KW, k // 4, (k % 4) * P:(k % 4 + 1) * P], flat[:, k * KW:(k + 1) * KW], ident[:, :])
                    ins.then_inc(s_ty[b], 1)
                for b in range(2):
                    pe.wait_ge(s_gs[b], after(i))
                    pe.wait_ge(s_ys[b], after(i))
                    pe.wait_ge(s_add[b], before(i))
                    for c in range(CH):
                        for k in range(KC):
                            ins = pe.matmul(ps_o[:, b, c * D:(c + 1) * D], ogT[:, b, k, c * P:(c + 1) * P], y[:, b, k, :],
                                            start=k == 0, stop=k == KC - 1)
                    ins.then_inc(s_o[b], 1)

        @block.scalar
        def _(act):
            prime(act, *s_gs, *s_ys)
            with act.Fori(0, BATCH // 2) as i:
                for b in range(2):
                    act.wait_ge(s_o[b], before(i))
                    act.wait_ge(s_tg[b], after(i))
                    flat = ogT[:, b, :, :].rearrange("p k t -> p (k t)")
                    act.activation(flat, ps_g[0:KW, :, :].rearrange("p a s -> p (a s)")[:, 0:KC * SEQ], ACT.Copy).then_inc(s_gs[b], 1)
                    act.wait_ge(s_ty[b], after(i))
                    flat = y[:, b, :, :].rearrange("p k d -> p (k d)")
                    act.activation(flat, ps_y[0:KW, :, :].rearrange("p a s -> p (a s)")[:, 0:KC * D], ACT.Copy).then_inc(s_ys[b], 1)



def expert_choice_ffn(nc, tag, T, W):
    layernorm_stats(nc, tag + "s", T["x"], T["mean"], T["rstd"], T["neg_half"])
    with ExitStack() as ctx:
        n = Names(nc, ctx, tag)
        T = dict(T, logits=n.sb("logits", [P, TILES, E]), gates=n.sb("gates", [P, TILES, E]), slots=n.sb("slots", [P, TILES, E]))
        normalise_and_route(nc, tag + "r", T, W["router"], xn_residual=False)
        gates_expert_choice(nc, tag + "g", T)
        chosen = n.sb("chosen", [P, E, BATCH, CAP])
        gather_chosen(nc, tag + "i", T, T["slots"], chosen, T["iota"])
        chosen_experts(nc, tag + "e", chosen, W)
        scatter_chosen(nc, tag + "o", T, T["slots"], chosen, T["iota"])


def token_choice_ffn(nc, tag, T, W):
    layernorm_stats(nc, tag + "s", T["x"], T["mean"], T["rstd"], T["neg_half"])
    with ExitStack() as ctx:
        n = Names(nc, ctx, tag)
        T = dict(T, xh=n.sb("xh", [P, TILES * P], F32R), xl=n.sb("xl", [P, TILES * P], F32R), logits=n.sb("logits", [P, TILES, E]), gates=n.sb("gates", [P, TILES, E]))
        normalise_and_route(nc, tag + "r", T, W["router"], xn_residual=True)
        gates_top2(nc, tag + "g", T)
        experts(nc, tag + "e", T, W["experts"])


def program(nc, A, out):
    with ExitStack() as ctx:
        n = Names(nc, ctx, "k")
        T = {"x": n.sb("x", [P, TILES, D]), "mean": n.sb("mean", [P, TILES]), "rstd": n.sb("rstd", [P, TILES]),
             "neg_half": n.sb("neg_half", [P, TILES]), "ident": n.sb("ident", [P, P]), "prio": n.sb("prio", [P, E]),
             "iota": n.sb("iota", [P, CAP]), "cols": n.sb("cols", [P, 16])}
        s_in, s_c, s_out = n.sem("loaded"), n.sem("constants"), n.sem("stored")

        def load(tag, *pairs):
            with ExitStack() as c:
                s_load = Names(nc, c, tag).sem("loaded")
                block = c.enter_context(nc.Block())

                @block.sync
                def _(sp):
                    for dst, src in pairs:
                        sp.dma_start(dst, src).then_inc(s_load, 16)
                    sp.wait_ge(s_load, 16 * len(pairs))

        load("in", (T["x"][:, :, :], A["L0_attn_x"].rearrange("b (c p) d -> p (b c) d", p=P)),
             (T["ident"][:, :], A["c_ident"]), (T["prio"][:, :], A["c_prio"]), (T["cols"][:, :], A["c_cols"]),
             (T["iota"][:, :], A["c_iota"]))
        with nc.Block() as block:
            @block.vector
            def _(dve):
                dve.memset(T["neg_half"][:, :], -0.5).then_inc(s_c, 1)

        def l0_ffn(tag):
            with ExitStack() as c:
                m = Names(nc, c, tag)
                W = {"up": m.sb("up0", [P, E, F]), "down": m.sb("down0", [P, E, FC, D]), "b1": m.sb("b1", [P, E, FC]),
                     "b2": m.sb("b2", [P, E]), "router": m.sb("router0", [P, E])}
                load(tag + "w", (W["router"][:, :], A["L0_router_T"]),
                     (W["up"][:, :, :], A["L0_ffn_w1"].rearrange("e d f -> d e f")),
                     (W["down"][:, :, :, :], A["L0_ffn_w2"].rearrange("e (c f) d -> f e c d", f=P)),
                     (W["b1"][:, :, :], A["L0_b1_T"]), (W["b2"][:, :], A["L0_b2_T"]))
                expert_choice_ffn(nc, tag, T, W)

        def l1_ffn(tag):
            with ExitStack() as c:
                m = Names(nc, c, tag)
                down = "(c f) d -> f c d"
                W = {"router": m.sb("router1", [P, E]), "experts": [
                    (A["L1_ffn_routed_up"][e], A["L1_ffn_routed_down"][e].rearrange(down, f=P)) for e in range(E)] + [
                    (A["L1_ffn_shared_up"][0], A["L1_ffn_shared_down"][0].rearrange(down, f=P))]}
                load(tag + "w", (W["router"][:, :], A["L1_ffn_router_w"]))
                token_choice_ffn(nc, tag, T, W)

        def stacks(m):
            return {"qk": [m.sb("wq", [P, HEADS * HW]), m.sb("wk", [P, HEADS * HW])], "v": m.sb("wv", [P, D]),
                    "aug": None, "bv": None}

        def l0_attention(tag):
            with ExitStack() as c:
                m = Names(nc, c, tag)
                W = stacks(m)
                raw = m.sb("raw", [P, 2, D])
                qkv = A["L0_qkv_T"]
                load(tag + "w", (raw[:, :, :], qkv[:, 0:2 * D].rearrange("p (k d) -> p k d", k=2)),
                     (W["v"][:, :], qkv[:, 2 * D:3 * D]))
                attention_weights(nc, tag + "p", [(W["qk"][0][:, :], raw[:, 0, :]), (W["qk"][1][:, :], raw[:, 1, :])], None, None, T)
                layernorm_stats(nc, tag + "s", T["x"], T["mean"], T["rstd"], T["neg_half"])
                attention(nc, tag + "c", T, W, None, T["x"], True)

        def l1_attention(tag):
            with ExitStack() as c:
                m = Names(nc, c, tag)
                a_all = m.sb("a_all", [P, TILES, D])
                W = {"o": m.sb("wo", [P, D]), "up": m.sb("w1", [P, F]), "down": m.sb("w2", [P, FC, D]), "b1": m.sb("bf1", [P, FC])}
                for k in ("bo", "g1", "be1", "b2", "g2", "be2", "bv"):
                    W[k] = m.sb(k, [P, D])

                def wide(name):
                    return A[name].unsqueeze(0).to_broadcast([P, D])

                load(tag + "w", (W["o"][:, :], A["L1_attn_Wo"]), (W["up"][:, :], A["L1_attn_W1"]),
                     (W["down"][:, :, :], A["L1_attn_W2"].rearrange("(c f) d -> f c d", f=P)), (W["b1"][:, :], A["L1_W1b_T"]),
                     (W["bo"][:, :], wide("L1_attn_bo")), (W["g1"][:, :], wide("L1_attn_ln1_g")), (W["be1"][:, :], wide("L1_attn_ln1_b")),
                     (W["b2"][:, :], wide("L1_attn_b2")), (W["g2"][:, :], wide("L1_attn_ln2_g")), (W["be2"][:, :], wide("L1_attn_ln2_b")),
                     (W["bv"][:, :], wide("L1_attn_bv")))
                layernorm_stats(nc, tag + "s", T["x"], T["mean"], T["rstd"], T["neg_half"])
                with ExitStack() as c2:
                    m2 = Names(nc, c2, tag + "2")
                    S = stacks(m2)
                    S["bv"] = W["bv"]
                    S["aug"], S["rows"] = m2.sb("aug", [AUG, 2, HEADS * HW], F32R), m2.sb("rows", [AUG, SEQ], F32R)
                    raw = m2.sb("raw", [P, 2, D])
                    bias = {"aug": m2.sb("rawaug", [AUG, 2, HEADS * HW]), "rows": m2.sb("rawrows", [AUG, SEQ]),
                            "b": m2.sb("bqk", [AUG, 2, D]), "hi": m2.sb("bqk_hi", [AUG, 2, D]),
                            "one": m2.sb("one", [AUG, HEADS])}
                    dist = {"scale": m2.sb("scale", [P, 1]), "eye": m2.sb("eye", [P, 2, P], F32R),
                            "tab": m2.sb("tab", [P, 2, P], F32R), "raw": m2.sb("rawtab", [P, 2, P])}
                    load(tag + "2w", (raw[:, 0, :], A["L1_attn_Wq"]), (raw[:, 1, :], A["L1_attn_Wk"]), (S["v"][:, :], A["L1_attn_Wv"]),
                         (bias["aug"][:, :, :], A["c_aug"].rearrange("k (s t) -> k s t", s=2)), (bias["rows"][:, :], A["c_rows"]),
                         (bias["b"][:, 0, :], A["L1_attn_bq"].unsqueeze(0).to_broadcast([AUG, D])),
                         (bias["b"][:, 1, :], A["L1_attn_bk"].unsqueeze(0).to_broadcast([AUG, D])),
                         (dist["scale"][:, :], A["L1_dist_scale"].to_broadcast([P, 1])),
                         (dist["raw"][:, :, :], A["c_dist"].rearrange("p (c t) -> p c t", c=2)))
                    attention_weights(nc, tag + "p", [(S["qk"][0][:, :], raw[:, 0, :]), (S["qk"][1][:, :], raw[:, 1, :])], (bias, S), dist, T)
                    attention(nc, tag + "c", T, S, dist, a_all, False)
                project_and_mlp(nc, tag + "m", T, a_all, W)

        l0_ffn("a")
        l0_attention("b")
        l0_ffn("c")
        l1_ffn("d")
        l1_attention("e")
        l1_ffn("f")

        with nc.Block() as block:
            @block.sync
            def _(sp):
                sp.dma_start(out.rearrange("b (c p) d -> p (b c) d", p=P), T["x"][:, :, :]).then_inc(s_out, 16)
                sp.wait_ge(s_out, 16)


def kernel(**inputs):
    import concourse.bacc as _bacc
    from concourse.bass_utils import run_bass_kernel_spmd as _run

    a = {k: np.ascontiguousarray(v) for k, v in inputs.items()}
    a["L0_router_T"] = np.ascontiguousarray(np.transpose(a.pop("L0_ffn_router_w")))
    b1 = a.pop("L0_ffn_b1")
    a["L0_b1_T"] = np.ascontiguousarray(np.transpose(b1.reshape(E, FC, P), (2, 0, 1)))
    a["L0_b2_T"] = np.ascontiguousarray(np.transpose(a.pop("L0_ffn_b2")))
    a["L0_qkv_T"] = np.ascontiguousarray(np.transpose(a.pop("L0_attn_W_qkv")))
    a["L1_W1b_T"] = np.ascontiguousarray(np.transpose(a.pop("L1_attn_b1").reshape(FC, P)))
    a["L1_dist_scale"] = a.pop("L1_attn_dist_scale").reshape(1, 1)
    a.update(shape_constants())

    nc = _bacc.Bacc("TRN2", target_bir_lowering=False, num_devices=1)
    arrays, aps = {}, {}
    for name, v in a.items():
        arrays[f"in_{name}"] = v
        aps[name] = nc.dram_tensor(f"in_{name}", v.shape, mybir.dt.from_np(v.dtype), kind="ExternalInput").ap()
    out = nc.dram_tensor("out_0", (BATCH, SEQ, D), F32, kind="ExternalOutput").ap()
    program(nc, aps, out)
    r = _run(nc, [arrays], core_ids=[0])
    return r.results[0]["out_0"]
```
